# Optimizing a Trainium2 kernel written in Bass

```python
import numpy as np
import jax
import jax.numpy as jnp

def _softmax(x, axis=-1):
    return jax.nn.softmax(x, axis=axis)

def _gelu(x):
    return jax.nn.gelu(x, approximate=True)

def _silu(x):
    return jax.nn.silu(x)

def _sigmoid(x):
    return jax.nn.sigmoid(x)

def _layernorm(x, axis=-1, eps=1e-05):
    m = jnp.mean(x, axis=axis, keepdims=True)
    v = jnp.var(x, axis=axis, keepdims=True)
    return (x - m) / jnp.sqrt(v + eps)

def _scatter_add(tgt, idx, src, axis=0):
    return tgt.at[idx].add(src)

def _segment_sum(src, seg, n):
    return jax.ops.segment_sum(src, seg, n)
kernel_name = 'mk_gnn_resnorm_d4_gnn_r32_adf5f6'

def setup_inputs(seed: int=0):
    np.random.seed(seed)
    _w = jnp.asarray

    def _rec_inputs():
        import jax
        import jax.numpy as jnp
        _gk = jax.random.key(seed)
        x = -0.0003713 + 1 * jax.random.normal(jax.random.fold_in(_gk, 1), (50000, 256), jnp.float32)
        src = jax.random.randint(jax.random.fold_in(_gk, 2), (50000,), 0, 50000, jnp.int32)
        dst = jnp.minimum((50000 * jax.random.uniform(jax.random.fold_in(_gk, 3), (50000,)) ** 2.0).astype(jnp.int32), 49999)
        _o = jnp.argsort(dst, stable=True)
        src = src[_o]
        dst = dst[_o]
        edge_weight = jax.random.uniform(jax.random.fold_in(_gk, 13), (50000,), jnp.float32, 0.0, 1)
        return (x, src, dst, edge_weight)
    x, src, dst, edge_weight = _rec_inputs()

    def _L0_gnn_setup():
        import jax, jax.numpy as jnp
        import numpy as np
        N_NODES = 50000
        N_EDGES = 50000
        IN_FEATS = 256
        HIDDEN = 512
        OUT_FEATS = 256
        EPS = 0.0
        key = jax.random.key(seed)
        ks = jax.random.split(key, 6)
        x = jax.random.normal(ks[0], (N_NODES, IN_FEATS), dtype=jnp.float32)
        edge_row = jax.random.randint(ks[1], (N_EDGES,), 0, N_NODES, dtype=jnp.int32)
        edge_col = jax.random.randint(ks[2], (N_EDGES,), 0, N_NODES, dtype=jnp.int32)
        W1 = jax.random.uniform(ks[3], (IN_FEATS, HIDDEN), dtype=jnp.float32, minval=-1.0 / np.sqrt(IN_FEATS), maxval=1.0 / np.sqrt(IN_FEATS))
        b1 = jnp.zeros((HIDDEN,), dtype=jnp.float32)
        W2 = jax.random.uniform(ks[4], (HIDDEN, OUT_FEATS), dtype=jnp.float32, minval=-1.0 / np.sqrt(HIDDEN), maxval=1.0 / np.sqrt(HIDDEN))
        b2 = jnp.zeros((OUT_FEATS,), dtype=jnp.float32)
        return {'x': x, 'edge_row': edge_row, 'edge_col': edge_col, 'W1': W1, 'b1': b1, 'W2': W2, 'b2': b2}
    _L0_gnn_all = _L0_gnn_setup()
    _L0_gnn_in = {k: v for k, v in _L0_gnn_all.items() if k in ('W1', 'b1', 'W2', 'b2')}
    del _L0_gnn_all

    def _L1_gnn_setup():
        import jax, jax.numpy as jnp
        import numpy as np
        N = 50000
        E = 25000
        D = 256

        def gcn_conv(x, W, src, dst, n):
            h = x @ W
            ones = jnp.ones(src.shape[0], dtype=h.dtype)
            deg = jax.ops.segment_sum(ones, dst, num_segments=n)
            dinv = jnp.where(deg > 0, jax.lax.rsqrt(deg), 0.0)
            norm = dinv[src] * dinv[dst]
            msgs = h[src] * norm[:, None]
            return jax.ops.segment_sum(msgs, dst, num_segments=n)
        key = jax.random.key(seed)
        k1, k2, k3, k4 = jax.random.split(key, 4)
        x = jax.random.normal(k1, (N, D), dtype=jnp.float32)
        edge_index = jax.random.randint(k2, (2, E), 0, N, dtype=jnp.int64)
        scale = 1.0 / np.sqrt(D)
        W1 = jax.random.normal(k3, (D, D), dtype=jnp.float32) * scale
        W2 = jax.random.normal(k4, (D, D), dtype=jnp.float32) * scale
        return {'x': x, 'edge_index': edge_index, 'W1': W1, 'W2': W2}
    _L1_gnn_all = _L1_gnn_setup()
    _L1_gnn_in = {k: v for k, v in _L1_gnn_all.items() if k in ('W1', 'W2')}
    del _L1_gnn_all

    def _L2_gnn_setup():
        import jax, jax.numpy as jnp
        import numpy as np
        N = 50000
        E = 50000
        D = 256
        K = 2

        def spmm(edge_row, edge_col, edge_val, feats):
            msgs = edge_val[:, None] * feats[edge_col]
            return jax.ops.segment_sum(msgs, edge_row, num_segments=N)
        key = jax.random.key(seed)
        k1, k2, k3, k4, k5 = jax.random.split(key, 5)
        x = jax.random.normal(k1, (N, D), dtype=jnp.float32)
        edge_row = jax.random.randint(k2, (E,), 0, N, dtype=jnp.int64)
        edge_col = jax.random.randint(k3, (E,), 0, N, dtype=jnp.int64)
        edge_val = jax.random.uniform(k4, (E,), dtype=jnp.float32)
        fan_in, fan_out = (D * (K + 1), D)
        std = np.sqrt(2.0) * np.sqrt(2.0 / (fan_in + fan_out))
        W = jax.random.normal(k5, (fan_in, fan_out), dtype=jnp.float32) * std
        b = jnp.zeros((fan_out,), dtype=jnp.float32)
        return {'x': x, 'edge_row': edge_row, 'edge_col': edge_col, 'edge_val': edge_val, 'W': W, 'b': b}
    _L2_gnn_all = _L2_gnn_setup()
    _L2_gnn_in = {k: v for k, v in _L2_gnn_all.items() if k in ('W', 'b')}
    del _L2_gnn_all

    def _L3_gnn_setup():
        import jax, jax.numpy as jnp
        import numpy as np
        N, IN_CH, HEADS, OUT_CH, E = (50000, 256, 4, 64, 25000)
        key = jax.random.key(seed)
        k1, k2, k3, k4, k5 = jax.random.split(key, 5)
        x = jax.random.normal(k1, (N, IN_CH), dtype=jnp.float32)
        edge_index = jax.random.randint(k2, (2, E), 0, N, dtype=jnp.int64)
        bw = float(np.sqrt(6.0 / (IN_CH + HEADS * OUT_CH)))
        ba = float(np.sqrt(6.0 / (HEADS + OUT_CH)))
        weight = jax.random.uniform(k3, (IN_CH, HEADS * OUT_CH), jnp.float32, -bw, bw)
        attn_l = jax.random.uniform(k4, (HEADS, OUT_CH), jnp.float32, -ba, ba)
        attn_r = jax.random.uniform(k5, (HEADS, OUT_CH), jnp.float32, -ba, ba)
        return {'x': x, 'edge_index': edge_index, 'weight': weight, 'attn_l': attn_l, 'attn_r': attn_r}
    _L3_gnn_all = _L3_gnn_setup()
    _L3_gnn_in = {k: v for k, v in _L3_gnn_all.items() if k in ('weight', 'attn_l', 'attn_r')}
    del _L3_gnn_all
    return {'x': x, 'src': src, 'dst': dst, 'edge_weight': edge_weight, 'L0_gnn_W1': _L0_gnn_in['W1'], 'L0_gnn_b1': _L0_gnn_in['b1'], 'L0_gnn_W2': _L0_gnn_in['W2'], 'L0_gnn_b2': _L0_gnn_in['b2'], 'L1_gnn_W1': _L1_gnn_in['W1'], 'L1_gnn_W2': _L1_gnn_in['W2'], 'L2_gnn_W': _L2_gnn_in['W'], 'L2_gnn_b': _L2_gnn_in['b'], 'L3_gnn_weight': _L3_gnn_in['weight'], 'L3_gnn_attn_l': _L3_gnn_in['attn_l'], 'L3_gnn_attn_r': _L3_gnn_in['attn_r']}

def reference(x, src, dst, edge_weight, L0_gnn_W1, L0_gnn_b1, L0_gnn_W2, L0_gnn_b2, L1_gnn_W1, L1_gnn_W2, L2_gnn_W, L2_gnn_b, L3_gnn_weight, L3_gnn_attn_l, L3_gnn_attn_r):
    import jax
    import jax.numpy as jnp

    def _L0_gnn_ref(x, edge_row, edge_col, W1, b1, W2, b2):
        import jax, jax.numpy as jnp
        import numpy as np
        N_NODES = 50000
        N_EDGES = 50000
        IN_FEATS = 256
        HIDDEN = 512
        OUT_FEATS = 256
        EPS = 0.0
        agg = jax.ops.segment_sum(x[edge_col], edge_row, num_segments=N_NODES)
        h = agg + (1.0 + EPS) * x
        h = h @ W1 + b1
        out = h @ W2 + b2
        return out

    def _L1_gnn_ref(x, edge_index, W1, W2):
        import jax, jax.numpy as jnp
        import numpy as np
        N = 50000
        E = 25000
        D = 256

        def gcn_conv(x, W, src, dst, n):
            h = x @ W
            ones = jnp.ones(src.shape[0], dtype=h.dtype)
            deg = jax.ops.segment_sum(ones, dst, num_segments=n)
            dinv = jnp.where(deg > 0, jax.lax.rsqrt(deg), 0.0)
            norm = dinv[src] * dinv[dst]
            msgs = h[src] * norm[:, None]
            return jax.ops.segment_sum(msgs, dst, num_segments=n)
        n = x.shape[0]
        loops = jnp.arange(n, dtype=edge_index.dtype)
        src = jnp.concatenate([edge_index[0], loops])
        dst = jnp.concatenate([edge_index[1], loops])
        h = gcn_conv(x, W1, src, dst, n)
        h = jax.nn.relu(h)
        return gcn_conv(h, W2, src, dst, n)

    def _L2_gnn_ref(x, edge_row, edge_col, edge_val, W, b):
        import jax, jax.numpy as jnp
        import numpy as np
        N = 50000
        E = 50000
        D = 256
        K = 2

        def spmm(edge_row, edge_col, edge_val, feats):
            msgs = edge_val[:, None] * feats[edge_col]
            return jax.ops.segment_sum(msgs, edge_row, num_segments=N)
        fstack = [x]
        for _ in range(K):
            fstack.append(spmm(edge_row, edge_col, edge_val, fstack[-1]))
        h = jnp.concatenate(fstack, axis=-1)
        out = h @ W + b
        return out

    def _L3_gnn_ref(x, edge_index, weight, attn_l, attn_r):
        import jax, jax.numpy as jnp
        import numpy as np
        N, IN_CH, HEADS, OUT_CH, E = (50000, 256, 4, 64, 25000)
        heads, out_ch = attn_l.shape
        n = x.shape[0]
        xt = jnp.matmul(x, weight).reshape(-1, heads, out_ch)
        row, col = (edge_index[0], edge_index[1])
        alpha_l = jnp.einsum('ehd,hd->eh', xt[row], attn_l)
        alpha_r = jnp.einsum('ehd,hd->eh', xt[col], attn_r)
        alpha = jax.nn.softmax(jax.nn.leaky_relu(alpha_l + alpha_r, 0.01), axis=1)
        tmp = jnp.einsum('nh,nhd->nd', alpha[:n], xt[col[:n]])
        out = jnp.broadcast_to(tmp[:, None, :], (n, heads, out_ch))
        return out.reshape(n, heads * out_ch)
    edge_index = jnp.stack([src, dst])
    x = _layernorm(x + _L0_gnn_ref(x, src, dst, L0_gnn_W1, L0_gnn_b1, L0_gnn_W2, L0_gnn_b2), axis=-1)
    x = _layernorm(x + _L1_gnn_ref(x, edge_index, L1_gnn_W1, L1_gnn_W2), axis=-1)
    x = _layernorm(x + _L2_gnn_ref(x, src, dst, edge_weight, L2_gnn_W, L2_gnn_b), axis=-1)
    x = _layernorm(x + _L3_gnn_ref(x, edge_index, L3_gnn_weight, L3_gnn_attn_l, L3_gnn_attn_r), axis=-1)
    return x

_drawn_inputs = setup_inputs


def setup_inputs(seed=0):
    import zlib

    import numpy as np

    out = dict(_drawn_inputs(seed))
    spreads = {'L0_gnn_b1': (0.0, 0.1), 'L0_gnn_b2': (0.0, 0.1), 'L2_gnn_b': (0.0, 0.1)}
    factors = {}
    for name, (base, spread) in spreads.items():
        noise = np.random.default_rng([zlib.crc32(name.encode()), seed]).standard_normal(out[name].shape)
        drawn = base * np.exp(spread * noise) if base else spread * noise
        out[name] = jnp.asarray(drawn.astype(out[name].dtype))
    for name, factor in factors.items():
        out[name] = (out[name] * factor).astype(out[name].dtype)
    return out
```

```python
from contextlib import ExitStack

import numpy as np
import concourse.bass as bass
from concourse import mybir

F32 = mybir.dt.float32
F16 = mybir.dt.float16
BF16 = mybir.dt.bfloat16
I32 = mybir.dt.int32
ALU = mybir.AluOpType
ACT = mybir.ActivationFunctionType
AX = mybir.AxisListType
P = 128
D = 256
KC = D // P
G = 8
R = 4
EPS = 1e-5
ROUND = float(3 << 22)


class Shape:

    def __init__(self, n):
        self.N = n
        self.T = -(-n // (P * G)) * G
        self.NP = P * self.T
        self.NG = self.T // G
        self.last = n - (P - 1) * self.T
        self.full = self.last // G
        assert self.last == self.full * G and self.full % R == R - 1 and self.full >= 2 * R
        assert self.NG % R == 1 and self.NG > self.full + 2 * R


def run_groups(e, s, body, ragged=0):
    args = (lambda g: (g, g % R, g < s.full)) if ragged else (lambda g: (g, g % R))
    for g in range(R):
        body(*args(g))
    if ragged:
        turn = (s.full + 1) // R
        with e.Fori(1, turn - 1) as i:
            for b in range(R):
                body(i * R + b, b, True)
        for g in range((turn - 1) * R, (turn + ragged - 1) * R):
            body(*args(g))
        with e.Fori(turn + ragged - 1, s.NG // R) as i:
            for b in range(R):
                body(i * R + b, b, False)
    else:
        with e.Fori(1, s.NG // R) as i:
            for b in range(R):
                body(i * R + b, b)
    body(*args(s.NG - 1))


def first(g):
    return isinstance(g, int) and g < R


def uses(s, b):
    return (s.NG - 1 - b) // R + 1


def cols(table, g):
    return table[:, bass.ds(g * G, G)] if not isinstance(g, int) else table[:, g * G:(g + 1) * G]


def tile_rows(view, g, lo=0, hi=P):
    return view[lo:hi, g * G:(g + 1) * G, :] if isinstance(g, int) else view[lo:hi, bass.ds(g * G, G), :]


def semaphores(nc, ctx, name):
    taken = []

    def sem(n):
        taken.append(nc.alloc_semaphore(f"{name}_{n}"))
        return taken[-1]

    def give_back():
        nc.clear_and_free_semaphores(taken)
        nc.all_engine_barrier()

    ctx.callback(give_back)
    return sem


def gather(e, out, table, index):
    return e.indirect_dma_start(out=out, out_offset=None, in_=table,
                                in_offset=bass.IndirectOffsetOnAxis(ap=index, axis=0))


class Core:

    def __init__(self, nc, s, ctx):
        self.nc, self.s, self.ctx = nc, s, ctx
        T = s.T
        sb = self.sb
        self.iota_free = sb("iota_free", [P, T], F16)
        self.iota_part = sb("iota_part", [P, 1], F32)
        self.node_f = sb("node_f", [P, T], F32)
        self.lower = sb("lower", [P, P], F32)
        self.before = sb("before", [P, P], F32)
        self.ident = sb("ident", [P, P], F32)
        self.identh = sb("identh", [P, P], F16)
        self.ones = sb("ones", [P, P], BF16)
        self.onesT = sb("onesT", [P, T], F32)
        self.zero_row = sb("zero_row", [1, D], F32)

    def sb(self, name, shape, dt):
        return self.ctx.enter_context(self.nc.sbuf_tensor(name, shape, dt))


def constants(nc, c, runs):
    s = c.s
    with ExitStack() as ctx:
        sem = semaphores(nc, ctx, "consts")
        num = ctx.enter_context(nc.sbuf_tensor("num", [P, s.T], I32))
        num2 = ctx.enter_context(nc.sbuf_tensor("num2", [P, s.T], I32))
        part = ctx.enter_context(nc.sbuf_tensor("part_no", [P, 1], I32))
        iotas = sem("iotas")
        blank = sem("blank")
        done = sem("consts_done")
        zeroed = sem("zeroed")
        zero_put = sem("zero_put")
        block = ctx.enter_context(nc.Block())

        @block.gpsimd
        def _(e):
            e.iota(num[:, :], pattern=[[1, s.T]], base=0, channel_multiplier=s.T)
            e.iota(num2[:, :], pattern=[[1, s.T]], base=0, channel_multiplier=0)
            e.iota(part[:, :], pattern=[[1, 1]], base=0, channel_multiplier=1).then_inc(iotas, 1)
            e.memset(c.lower[:, :], 1.0).then_inc(blank, 1)
            e.memset(c.before[:, :], 1.0).then_inc(blank, 1)
            e.memset(c.ident[:, :], 0.0).then_inc(blank, 1)
            e.wait_ge(blank, 3)
            e.affine_select(out=c.lower[:, :], in_=c.lower[:, :], compare_op=ALU.is_gt, fill=0.0,
                            base=0, pattern=[[1, P]], channel_multiplier=-1)
            e.affine_select(out=c.before[:, :], in_=c.before[:, :], compare_op=ALU.is_gt, fill=0.0,
                            base=0, pattern=[[-1, P]], channel_multiplier=1)
            e.affine_select(out=c.ident[:, :], in_=c.ident[:, :], compare_op=ALU.not_equal, fill=1.0,
                            base=0, pattern=[[-1, P]], channel_multiplier=1).then_inc(done, 1)

        @block.vector
        def _(e):
            e.memset(c.ones[:, :], 1.0)
            e.memset(c.onesT[:, :], 1.0)
            e.memset(c.zero_row[:, :], 0.0).then_inc(zeroed, 1)
            e.wait_ge(iotas, 1)
            e.tensor_copy(c.node_f[:, :], num[:, :])
            e.tensor_copy(c.iota_free[:, :], num2[:, :])
            e.tensor_copy(c.iota_part[:, :], part[:, :])
            e.wait_ge(done, 1)
            e.tensor_copy(c.identh[:, :], c.ident[:, :])


        @block.sync
        def _(e):
            e.wait_ge(zeroed, 1)
            e.dma_start(runs[s.NP:s.NP + 1, :], c.zero_row[0:1, :]).then_inc(zero_put, 16)
            e.wait_ge(zero_put, 16)


def sort_edges(nc, c, name, key_dram, other_dram, weight_dram, rec_dram, tabs, key_kept=None, other_kept=None):
    s = c.s
    T, NG = s.T, s.NG
    with ExitStack() as ctx:
        def sb(n, shape, dt):
            return ctx.enter_context(nc.sbuf_tensor(f"{name}_{n}", shape, dt))

        sem = semaphores(nc, ctx, f"{name}")

        key_i, other_i = sb("key_i", [P, T], I32), sb("other_i", [P, T], I32)
        key_f = sb("key_f", [P, T], F32)
        hi, lo, tmp = sb("hi", [P, T], F32), sb("lo", [P, T], F32), sb("tmp", [P, T], F32)
        rec = sb("rec", [P, T, 4], F32)
        rec_now = [sb(f"rec_now{b}", [P, G, 4], F32) for b in range(R)]
        pos_now = [sb(f"pos_now{b}", [P, G], I32) for b in range(R)]
        lh = [sb(f"lh{b}", [P, G, 3], F32) for b in range(R)]
        hot_hi = [sb(f"hot_hi{b}", [P, P], F16) for b in range(4)]
        hot_lo = [sb(f"hot_lo{b}", [P, T], F16) for b in range(4)]
        hot_hiT = [sb(f"hot_hiT{b}", [P, P], F32) for b in range(2)]
        same_key = [sb(f"same_key{b}", [P, P], F32) for b in range(2)]
        count = [sb(f"count{b}", [P, T], F32) for b in range(2)]
        offset = sb("offset", [P, T], F32)
        prod = sb("prod", [P, T], F32)
        picked = [sb(f"picked{b}", [P, T], F32) for b in range(2)]
        hit = [sb(f"hit{b}", [P, G], F32) for b in range(R)]
        rank = [sb(f"rank{b}", [P, G], F32) for b in range(R)]
        row_sum = sb("row_sum", [P, 1], F32)
        hist_ps = ctx.enter_context(nc.psum_tensor(f"{name}_hist", [P, 512], F32))
        hotT_bank = [ctx.enter_context(nc.psum_tensor(f"{name}_hotT{b}", [P, 1024], F16)) for b in range(2)]
        key_ps = [ctx.enter_context(nc.psum_tensor(f"{name}_key{b}", [P, 512], F32)) for b in range(2)]
        at_ps = [ctx.enter_context(nc.psum_tensor(f"{name}_at{b}", [P, 512], F32)) for b in range(2)]
        LATE = 3
        next_i = sb("next_i", [P, T], I32)
        falls = sb("falls", [P, 1], F32)

        own, loaded, link = sem("own"), sem("loaded"), sem("link")
        with nc.Block() as block:
            @block.vector
            def _(e):
                n = [0]

                def then(ins):
                    n[0] += 1
                    ins.then_inc(link, 1)
                    e.wait_ge(link, n[0])

                e.tensor_copy(key_i[:, :], c.node_f[:, :])
                e.memset(rec[:, :, :], 0.0)
                e.memset(tmp[:, :], 0.0)
                e.tensor_scalar(next_i[:, :], c.node_f[:, :], 1.0, None, ALU.add)
                then(e.memset(other_i[:, :], 0))
                e.sem_inc(own, 1)
                e.wait_ge(loaded, 16 * (12 if weight_dram is not None else 9))
                then(e.tensor_tensor(out=lo[:, :], in0=key_i[:, :], in1=next_i[:, :], op=ALU.is_gt))
                then(e.tensor_reduce(out=falls[:, :], in_=lo[:, :], axis=AX.X, op=ALU.add))
                e.tensor_copy(key_f[:, :], key_i[:, :]).then_inc(link, 1)
                n[0] += 1
                then(e.tensor_copy(rec[:, :, 1], other_i[:, :]))
                then(e.tensor_copy(rec[:, :, 2], tmp[:, :]))
                if key_kept is not None:
                    e.tensor_copy(key_kept[:, :], key_i[:, :])
                    e.tensor_copy(other_kept[:, :], other_i[:, :])
                then(e.tensor_scalar(tmp[:, :], key_f[:, :], (T - 1) / 2, 1.0 / T,
                                     ALU.subtract, ALU.mult))
                then(e.tensor_scalar(hi[:, :], tmp[:, :], ROUND, ROUND, ALU.add, ALU.subtract))
                e.scalar_tensor_tensor(out=lo[:, :], in0=hi[:, :], scalar=-float(T), in1=key_f[:, :],
                                       op0=ALU.mult, op1=ALU.add)
                e.tensor_copy(rec[:, :, 0], key_f[:, :])

            @block.sync
            def _(e):
                e.wait_ge(own, 1)
                pieces = [(key_dram, key_i, 0), (key_dram, next_i, 1), (other_dram, other_i, 0)]
                if weight_dram is not None:
                    pieces.append((weight_dram, tmp, 0))
                cut = (P - 1) * T
                for src, dst, ahead in pieces:
                    body = src[ahead:cut + ahead].rearrange("(p t) -> p t", t=T)
                    e.dma_start(dst[0:112, :], body[0:112, :]).then_inc(loaded, 16)
                    e.dma_start(dst[112:127, :], body[112:127, :]).then_inc(loaded, 16)
                    e.dma_start(dst[127:128, 0:s.last - ahead],
                                src[cut + ahead:s.N].rearrange("(a t) -> a t", a=1)).then_inc(loaded, 16)

        first_hot, counted, hist_done, link2, base_done = (sem("first_hot"), sem("counted"), sem("hist_done"),
                                                   sem("link2"), sem("base_done"))
        lh_ready = sem("lh_ready")
        with nc.Block() as block:
            @block.vector
            def _(e):
                def body(g, b):
                    if not first(g):
                        e.wait_ge(first_hot, (g - R + 1) * G)
                    e.tensor_copy(lh[b][:, :, 0], cols(hi, g))
                    e.tensor_copy(lh[b][:, :, 1], cols(lo, g)).then_inc(lh_ready, 1)
                    e.wait_ge(lh_ready, g + 1)
                    for t in range(G):
                        o = t % 4
                        if not (first(g) and g * G + t < 4):
                            e.wait_ge(counted, g * G + (t - 3))
                        e.tensor_scalar(hot_hi[o][:, :], c.iota_free[:, 0:P], lh[b][:, t, 0:1], None,
                                        ALU.is_equal)
                        e.tensor_scalar(hot_lo[o][:, :], c.iota_free[:, :], lh[b][:, t, 1:2], None,
                                        ALU.is_equal).then_inc(first_hot, 1)

                run_groups(e, s, body)
                n = [0]

                def then(ins):
                    n[0] += 1
                    ins.then_inc(link2, 1)
                    e.wait_ge(link2, n[0])

                e.wait_ge(counted, T)
                then(e.tensor_copy(count[1][:, :], hist_ps[:, 0:T]))
                then(e.tensor_tensor_scan(out=count[0][:, :], data0=c.onesT[:, :], data1=count[1][:, :],
                                          initial=0.0, op0=ALU.mult, op1=ALU.add))
                then(e.tensor_copy(row_sum[:, :], count[0][:, T - 1:T]))
                e.sem_inc(hist_done, 1)
                e.wait_ge(base_done, 1)
                then(e.tensor_copy(row_sum[:, :], at_ps[0][:, 0:1]))
                then(e.tensor_scalar(falls[:, :], at_ps[1][:, 0:1], 1.0, None, ALU.min))
                then(e.tensor_copy(tabs["unsorted"][:, :], falls[:, :]))
                then(e.tensor_scalar(count[0][:, :], count[0][:, :], row_sum[:, 0:1], None, ALU.add))
                then(e.tensor_tensor(out=offset[:, :], in0=count[0][:, :], in1=count[1][:, :],
                                     op=ALU.subtract))
                then(e.tensor_scalar(tmp[:, :], count[1][:, :], 0.0, None, ALU.is_equal))
                then(e.tensor_scalar(prod[:, :], count[0][:, :], -1.0, float(s.NP + 1), ALU.mult, ALU.add))
                then(e.tensor_tensor(out=prod[:, :], in0=prod[:, :], in1=tmp[:, :], op=ALU.mult))
                then(e.tensor_tensor(out=prod[:, :], in0=prod[:, :], in1=count[0][:, :], op=ALU.add))
                then(e.tensor_scalar(prod[:, :], prod[:, :], -1.0, None, ALU.add))
                then(e.tensor_copy(tabs["end"][:, :], prod[:, :]))
                if "degree" in tabs:
                    then(e.tensor_scalar(tabs["degree"][:, :], count[1][:, :], 1.0, None, ALU.add))

            @block.tensor
            def _(e):
                def body(g, b):
                    for t in range(G):
                        o = t % 4
                        e.wait_ge(first_hot, g * G + (t + 1))
                        e.matmul(hist_ps[:, 0:T], hot_hi[o][:, :], hot_lo[o][:, :],
                                 start=(first(g) and g == 0 and t == 0),
                                 stop=(isinstance(g, int) and g == NG - 1 and t == G - 1),
                                 skip_group_check=True).then_inc(counted, 1)

                run_groups(e, s, body)
                e.wait_ge(hist_done, 1)
                e.matmul(at_ps[1][:, 0:1], c.onesT[:, 0:P], falls[:, :], start=True, stop=True)
                e.matmul(at_ps[0][:, 0:1], c.lower[:, :], row_sum[:, :], start=True, stop=True
                         ).then_inc(base_done, 1)

        hot, counted2, snap, keyT_ps, hotT_ps, hotT, at, placed, put = (
            sem("hot"), sem("counted2"), sem("snap"), sem("keyT_ps"), sem("hotT_ps"),
            sem("hotT"), sem("at"), sem("placed"), [sem(f"put{b}") for b in range(R)])
        lh2, ranked, summed, kept = sem("lh2"), sem("ranked"), sem("summed"), sem("kept")
        unsorted = nc.values_load(tabs["unsorted"][0:1, 0:1], min_val=0, max_val=1,
                                  skip_runtime_bounds_check_because="VectorE wrote 0 or 1")
        with nc.If(unsorted > 0), nc.Block() as block:
            @block.vector
            def _(e):
                def pick(g, b, t):
                    n, o = g * G + t, t % 2
                    if not (first(g) and n < 2):
                        e.wait_ge(ranked, n - 1)
                        e.wait_ge(summed, n - 1)
                    e.wait_ge(keyT_ps, n + 1)
                    e.scalar_tensor_tensor(out=same_key[o][:, :], in0=key_ps[o][:, 0:P],
                                           scalar=lh[b][:, t, 2:3], in1=c.before[:, :],
                                           op0=ALU.is_equal, op1=ALU.mult,
                                           accum_out=rank[b][:, t:t + 1]).then_inc(ranked, 1)
                    e.wait_ge(at, n + 1)
                    e.scalar_tensor_tensor(out=picked[o][:, :], in0=at_ps[o][:, 0:T], scalar=0.0,
                                           in1=hot_lo[t % 4][:, :], op0=ALU.add, op1=ALU.mult,
                                           accum_out=hit[b][:, t:t + 1]).then_inc(summed, 1)

                def place(g, b):
                    e.wait_ge(summed, (g + 1) * G)
                    e.wait_ge(ranked, (g + 1) * G)
                    e.tensor_tensor(out=pos_now[b][:, :], in0=hit[b][:, :], in1=rank[b][:, :], op=ALU.add
                                    ).then_inc(placed, 1)

                def body(g, b):
                    if not first(g):
                        e.wait_ge(put[b], (g - b) * (16 * G // R))
                    e.tensor_copy(lh[b][:, :, 0], cols(hi, g))
                    e.tensor_copy(lh[b][:, :, 1], cols(lo, g))
                    e.tensor_copy(lh[b][:, :, 2], cols(key_f, g))
                    e.tensor_copy(rec_now[b][:, :, :],
                                  rec[:, bass.ds(g * G, G), :] if not isinstance(g, int)
                                  else rec[:, g * G:(g + 1) * G, :]).then_inc(lh2, 1)
                    e.wait_ge(lh2, g + 1)
                    for t in range(G):
                        n, o = g * G + t, t % 4
                        if not (first(g) and n < 4):
                            e.wait_ge(counted2, n - 2)
                            e.wait_ge(summed, n - 3)
                        e.tensor_scalar(hot_hi[o][:, :], c.iota_free[:, 0:P], lh[b][:, t, 0:1], None,
                                        ALU.is_equal)
                        e.tensor_scalar(hot_lo[o][:, :], c.iota_free[:, :], lh[b][:, t, 1:2], None,
                                        ALU.is_equal).then_inc(hot, 1)
                        late = back(g, b, t, LATE)
                        if late is not None:
                            pick(*late)
                            if late[2] == G - 1:
                                place(*late[:2])

                run_groups(e, s, body)
                behind(s, LATE, pick)
                place(NG - 1, (NG - 1) % R)

            @block.tensor
            def _(e):
                e.matmul(hist_ps[:, 0:T], c.ident[:, :], offset[:, :], start=True, stop=False,
                         skip_group_check=True).then_inc(counted2, 1)

                def count_tile(g, b, t, stop=False):
                    n, o = g * G + t, t % 2
                    if not (first(g) and n < 2):
                        e.wait_ge(ranked, n - 1)
                        e.wait_ge(summed, n - 1)
                    e.transpose(key_ps[o][:, 0:P], lh[b][:, t, 2:3].broadcast_to([P, P]), c.ident[:, :]
                                ).then_inc(keyT_ps, 1)
                    e.wait_ge(snap, n + 1)
                    e.matmul(hist_ps[:, 0:T], hot_hi[t % 4][:, :], hot_lo[t % 4][:, :], start=False,
                             stop=stop, skip_group_check=True).then_inc(counted2, 1)
                    e.wait_ge(hotT, n + 1)
                    e.matmul(at_ps[o][:, 0:T], hot_hiT[o][:, :], count[o][:, :], start=True,
                             stop=True).then_inc(at, 1)

                def body(g, b):
                    for t in range(G):
                        n, o = g * G + t, t % 2
                        e.wait_ge(hot, n + 1)
                        if not (first(g) and n < 2):
                            e.wait_ge(hotT, n - 1)
                        e.transpose(hotT_bank[o][:, 0:P], hot_hi[t % 4][:, :], c.identh[:, :]
                                    ).then_inc(hotT_ps, 1)
                        late = back(g, b, t, 1)
                        if late is not None:
                            count_tile(*late)

                run_groups(e, s, body)
                count_tile(NG - 1, (NG - 1) % R, G - 1, stop=True)

            @block.scalar
            def _(e):
                def snapshot(g, b, t):
                    n = g * G + t
                    e.wait_ge(counted2, n + 1)
                    if not (first(g) and n < 2):
                        e.wait_ge(at, n - 1)
                    e.activation(count[t % 2][:, :], hist_ps[:, 0:T], ACT.Copy).then_inc(snap, 1)

                def body(g, b):
                    for t in range(G):
                        n, o = g * G + t, t % 2
                        late = back(g, b, t, 1)
                        if late is not None:
                            snapshot(*late)
                        e.wait_ge(hotT_ps, n + 1)
                        if not (first(g) and n < 2):
                            e.wait_ge(at, n - 1)
                        e.activation(hot_hiT[o][:, :], hotT_bank[o][:, 0:P], ACT.Copy
                                     ).then_inc(hotT, 1)

                run_groups(e, s, body)
                behind(s, 1, snapshot)

            @block.gpsimd
            def _(e):
                def body(g, b):
                    e.wait_ge(placed, g + 1)
                    e.nop(nofuse=True)
                    for t in range(G):
                        e.indirect_dma_start(out=rec_dram[:, :],
                                             out_offset=bass.IndirectOffsetOnAxis(
                                                 ap=pos_now[b][:, t:t + 1], axis=0),
                                             in_=rec_now[b][:, t, :], in_offset=None).then_inc(put[b], 16)

                run_groups(e, s, body)
                for b in range(R):
                    e.wait_ge(put[b], 16 * G * uses(s, b))

        with nc.Else(), nc.Block() as block:
            @block.sync
            def _(e):
                e.dma_start(rec_dram[0:s.NP, :].rearrange("(p t) f -> p t f", t=T), rec[:, :, :]
                            ).then_inc(kept, 16)
                e.wait_ge(kept, 16)


def sorted_tables(nc, c, name, rec_dram, tabs):
    s = c.s
    T = s.T
    with ExitStack() as ctx:
        sem = semaphores(nc, ctx, f"{name}")

        rec = ctx.enter_context(nc.sbuf_tensor(f"{name}_sorted", [P, T, 4], F32))
        eq = ctx.enter_context(nc.sbuf_tensor(f"{name}_eq", [P, T], F32))
        last_key = ctx.enter_context(nc.sbuf_tensor(f"{name}_last_key", [P, 1], F32))
        first_key = ctx.enter_context(nc.sbuf_tensor(f"{name}_first_key", [P, 1], F32))
        length = ctx.enter_context(nc.sbuf_tensor(f"{name}_length", [P, 1], F32))
        row_ps = ctx.enter_context(nc.psum_tensor(f"{name}_row", [P, 512], F32))
        loaded, link, keys, row = sem("t_loaded"), sem("t_link"), sem("t_keys"), sem("t_row")
        with nc.Block() as block:
            @block.sync
            def _(e):
                e.dma_start(rec[:, :, :], rec_dram[0:s.NP, :].rearrange("(p t) f -> p t f", t=T)
                            ).then_inc(loaded, 16)

            @block.tensor
            def _(e):
                e.wait_ge(keys, 1)
                e.transpose(row_ps[:, 0:P], first_key[:, 0:1].broadcast_to([P, P]), c.ident[:, :]
                            ).then_inc(row, 1)

            @block.vector
            def _(e):
                n = [0]

                def then(ins):
                    n[0] += 1
                    ins.then_inc(link, 1)
                    e.wait_ge(link, n[0])

                e.wait_ge(loaded, 16)
                then(e.tensor_copy(first_key[:, :], rec[:, 0:1, 0]))
                e.sem_inc(keys, 1)
                then(e.tensor_copy(last_key[:, :], rec[:, T - 1:T, 0]))
                e.tensor_copy(tabs["other"][:, :], rec[:, :, 1])
                if "weight" in tabs:
                    e.tensor_copy(tabs["weight"][:, :], rec[:, :, 2])
                e.memset(tabs["same"][:, 0:1], 0.0)
                e.tensor_tensor(out=tabs["same"][:, 1:T], in0=rec[:, 1:T, 0], in1=rec[:, 0:T - 1, 0],
                                op=ALU.is_equal)
                then(e.tensor_scalar(eq[:, :], rec[:, :, 0], first_key[:, 0:1], None, ALU.is_equal))
                then(e.tensor_reduce(out=length[:, :], in_=eq[:, :], axis=AX.X, op=ALU.add))
                then(e.tensor_scalar(length[:, :], length[:, :], -1.0, None, ALU.add))
                e.tensor_tensor(out=tabs["fix_row"][:, :], in0=length[:, :], in1=c.node_f[:, 0:1],
                                op=ALU.add)
                e.wait_ge(row, 1)
                e.scalar_tensor_tensor(out=tabs["fix"][:, :], in0=row_ps[:, 0:P], scalar=last_key[:, 0:1],
                                       in1=c.lower[:, :], op0=ALU.is_equal, op1=ALU.mult)


def edge_phase(nc, c, name, table, tabs, runs, weighted=False):
    s = c.s
    T, NG = s.T, s.NG
    view = runs[0:s.NP, :].rearrange("(p t) d -> p t d", t=T)
    with ExitStack() as ctx:
        def sb(n, shape, dt):
            return ctx.enter_context(nc.sbuf_tensor(f"{name}_{n}", shape, dt))

        sem = semaphores(nc, ctx, f"{name}")

        index = [sb(f"index{b}", [P, G], I32) for b in range(R)]
        flag = [sb(f"flag{b}", [P, G], F32) for b in range(R)]
        rows = [sb(f"rows{b}", [P, G, D], F32) for b in range(R)]
        run = [sb(f"run{b}", [P, G, D], F32) for b in range(R)]
        fixed = sb("fixed", [P, D], F32)
        carry_ps = ctx.enter_context(nc.psum_tensor(f"{name}_carry", [P, 512], F32))
        indexed, flagged, summed, weighed, wrote = (sem("indexed"), sem("flagged"), sem("summed"),
                                                    sem("weighed"), sem("wrote"))
        got = [sem(f"got{b}") for b in range(R)]
        put = [sem(f"put{b}") for b in range(R)]
        fix_got, fix_sum, fix_put, carried = sem("fix_got"), sem("fix_sum"), sem("fix_put"), sem("carried")
        if weighted:
            weight_set = sem("weight_set")
            wcur = [sb(f"wcur{b}", [P, G], F32) for b in range(R)]

        with nc.Block() as block:
            @block.gpsimd
            def _(e):
                def body(g, b):
                    e.wait_ge(indexed, g + 1)
                    if not first(g):
                        e.wait_ge(summed, (g - R + 1) * G)
                    e.nop(nofuse=True)
                    for t in range(G):
                        gather(e, rows[b][:, t, :], table[:, :], index[b][:, t:t + 1]).then_inc(got[b], 16)

                run_groups(e, s, body)
                e.wait_ge(wrote, 1)
                gather(e, fixed[:, :], runs[:, :], tabs["fix_row"][:, 0:1]).then_inc(fix_got, 16)
                e.wait_ge(fix_sum, 1)
                e.indirect_dma_start(out=runs[:, :],
                                     out_offset=bass.IndirectOffsetOnAxis(ap=tabs["fix_row"][:, 0:1], axis=0),
                                     in_=fixed[:, :], in_offset=None).then_inc(fix_put, 16)
                e.wait_ge(fix_put, 16)

            @block.vector
            def _(e):
                e.memset(run[R - 1][:, G - 1, :], 0.0).then_inc(flagged, 1)

                def copies(g, b):
                    if not first(g):
                        e.wait_ge(got[b], (g - b) * (16 * G // R))
                    e.tensor_copy(index[b][:, :], cols(tabs["other"], g)).then_inc(indexed, 1)

                def body(g, b):
                    if isinstance(g, int):
                        if g == 0:
                            copies(0, 0)
                            e.wait_ge(flagged, 1)
                        if g + 1 < NG:
                            copies(g + 1, (b + 1) % R)
                    else:
                        copies(g + 1, (b + 1) % R)
                    e.tensor_copy(flag[b][:, :], cols(tabs["same"], g)).then_inc(flagged, 1)
                    e.wait_ge(flagged, g + 2)
                    if weighted:
                        e.wait_ge(weighed, (g + 1) * G)
                    else:
                        e.wait_ge(got[b], (g - b + R) * (16 * G // R))
                    if not first(g):
                        e.wait_ge(put[b], (g - b) * (16 // R))
                    for t in range(G):
                        before = run[b][:, t - 1, :] if t else run[(b - 1) % R][:, G - 1, :]
                        if not (isinstance(g, int) and g == 0 and t == 0):
                            e.wait_ge(summed, g * G + t)
                        e.scalar_tensor_tensor(out=run[b][:, t, :], in0=before, scalar=flag[b][:, t:t + 1],
                                               in1=rows[b][:, t, :], op0=ALU.mult, op1=ALU.add
                                               ).then_inc(summed, 1)

                run_groups(e, s, body)
                e.wait_ge(fix_got, 16)
                e.wait_ge(carried, 1)
                e.tensor_tensor(out=fixed[:, :], in0=carry_ps[:, 0:D], in1=fixed[:, :], op=ALU.add
                                ).then_inc(fix_sum, 1)

            if weighted:
                @block.scalar
                def _(e):
                    def body(g, b):
                        e.activation(wcur[b][:, :], cols(tabs["weight"], g), ACT.Copy).then_inc(weight_set, 1)
                        e.wait_ge(weight_set, g + 1)
                        e.wait_ge(got[b], (g - b + R) * (16 * G // R))
                        for t in range(G):
                            e.activation(rows[b][:, t, :], rows[b][:, t, :], ACT.Copy,
                                         scale=wcur[b][:, t:t + 1]).then_inc(weighed, 1)

                    run_groups(e, s, body)

            @block.sync
            def _(e):
                def body(g, b):
                    e.wait_ge(summed, (g + 1) * G)
                    e.dma_start(tile_rows(view, g), run[b][:, :, :]).then_inc(put[b], 16)

                run_groups(e, s, body)
                for b in range(R):
                    e.wait_ge(put[b], 16 * uses(s, b))
                e.sem_inc(wrote, 1)

            @block.tensor
            def _(e):
                e.wait_ge(summed, T)
                e.matmul(carry_ps[:, 0:D], tabs["fix"][:, :], run[(NG - 1) % R][:, G - 1, :], start=True,
                         stop=True).then_inc(carried, 1)


def back(g, b, t, lag):
    q = (t - lag) // G
    if isinstance(g, int) and g + q < 0:
        return None
    return (g + q if q else g), (b + q) % R, (t - lag) % G


def behind(s, lag, step):
    for t in range(lag):
        step(*back(s.NG, s.NG % R, t, lag))


def variance(e, chained, stats, small):
    mean2, diff, var = small[:, 0, :], small[:, 1, :], small[:, 2, :]
    chained(e.tensor_tensor(out=mean2, in0=stats[:, :, 1], in1=stats[:, :, 4], op=ALU.add))
    chained(e.tensor_tensor(out=diff, in0=stats[:, :, 1], in1=stats[:, :, 4], op=ALU.subtract))
    chained(e.tensor_tensor(out=var, in0=stats[:, :, 2], in1=stats[:, :, 5], op=ALU.add))
    chained(e.tensor_tensor(out=diff, in0=diff, in1=diff, op=ALU.mult))
    chained(e.scalar_tensor_tensor(out=var, in0=diff, scalar=D / 4.0, in1=var, op0=ALU.mult, op1=ALU.add))
    return e.tensor_scalar(var, var, 1.0 / D, EPS, ALU.mult, ALU.add)


def norm_factors(e, chained, small, scale, shift, dinv):
    chained(e.reciprocal(out=scale[:, :], in_=small[:, 3, :]))
    if dinv is not None:
        chained(e.tensor_tensor(out=scale[:, :], in0=scale[:, :], in1=dinv, op=ALU.mult))
    return e.scalar_tensor_tensor(out=shift[:, :], in0=small[:, 0, :], scalar=-0.5, in1=scale[:, :],
                                  op0=ALU.mult, op1=ALU.mult)


def node_phase(nc, c, name, kind, runs, end, x_in, out, weights, bias=None, y_in=None, z_out=None,
               ragged=0, tables=None):
    s = c.s
    T, NG = s.T, s.NG
    both = kind == "hop1"
    NS = 2 if both else 1
    summed_in = kind in ("gin", "gcn1", "gcn2")
    normed_out = kind in ("gin", "gcn2", "hop2")
    LEAD, NORM = 3, G + 6

    with ExitStack() as ctx:
        def sb(n, shape, dt):
            return ctx.enter_context(nc.sbuf_tensor(f"{name}_{n}", shape, dt))

        sem = semaphores(nc, ctx, f"{name}")

        def ring(n, shape, dt, k=R):
            return [sb(f"{n}{b}", shape, dt) for b in range(k)]

        index = ring("index", [P, G], I32)
        A, X, O = ring("A", [P, G, D], F32), ring("X", [P, G, D], F32), ring("O", [P, G, D], F32)
        Y = ring("Y", [P, G, D], F32) if kind == "gcn2" else None
        h = ring("h", [P, D], F32, 4) if summed_in else None
        hT = ring("hT", [P, NS * KC, P], F32, 2)
        half = ring("half", [P, D], F32, 2) if kind == "gcn2" else None
        stats = ring("stats", [P, G, 6], F32)
        small = ring("small", [P, 4, G], F32)
        scale, shift = ring("scale", [P, G], F32), ring("shift", [P, G], F32)
        factor = ring("factor", [P, 2, G], F32)
        hT_ps = [ctx.enter_context(nc.psum_tensor(f"{name}_hT_ps{b}", [P, 4, P], F32)) for b in range(2)]
        out_ps = [ctx.enter_context(nc.psum_tensor(f"{name}_out_ps{b}", [P, 512], F32)) for b in range(2)]
        indexed, added, turned, copied, multiplied, summed = (
            sem("indexed"), sem("added"), sem("turned"), sem("copied"), sem("multiplied"), sem("summed"))
        halved, measured, chain, root_asked, root_done, factors, normed = (
            sem("halved"), sem("measured"), sem("chain"), sem("root_asked"), sem("root_done"),
            sem("factors"), sem("normed"))
        got = [sem(f"got{b}") for b in range(R)]
        loaded = [sem(f"loaded{b}") for b in range(R)]
        put = [sem(f"put{b}") for b in range(R)]
        put_A = [sem(f"put_A{b}") for b in range(R)]
        loads = (48 if ragged else 16) + (16 if Y else 0)

        def in_rows(view, g, full, dst, e, sm):
            if not ragged:
                e.dma_start(dst, tile_rows(view, g)).then_inc(sm, 16)
                return
            top = view[0:(P - 1) * T, :].rearrange("(p t) d -> p t d", t=T)
            rest = view[(P - 1) * T:s.N, :].rearrange("(p t) d -> p t d", p=1)
            e.dma_start(dst[0:112], tile_rows(top, g, 0, 112)).then_inc(sm, 16)
            e.dma_start(dst[112:127], tile_rows(top, g, 112, 127)).then_inc(sm, 16)
            e.dma_start(dst[127:128], tile_rows(rest, g, 0, 1) if full else tile_rows(top, g, 126, 127)
                        ).then_inc(sm, 16)

        with nc.Block() as block:
            @block.gpsimd
            def _(e):
                def body(g, b):
                    e.wait_ge(indexed, g + 1)
                    if not first(g):
                        if summed_in:
                            e.wait_ge(added, (g - R + 1) * G)
                        else:
                            e.wait_ge(turned, (g - R + 1) * G)
                        if both:
                            e.wait_ge(put_A[b], (g - b) * (16 // R))
                    e.nop(nofuse=True)
                    for t in range(G):
                        gather(e, A[b][:, t, :], runs[:, :], index[b][:, t:t + 1]).then_inc(got[b], 16)

                run_groups(e, s, body)

            @block.sync
            def _(e):
                def load(g, b, full):
                    if not first(g):
                        if kind == "gcn1":
                            e.wait_ge(added, (g - R + 1) * G)
                        else:
                            e.wait_ge(summed, (g - R + 1) * G)
                    if both and not first(g):
                        e.wait_ge(turned, (g - R + 1) * G)
                    in_rows(x_in, g, full, X[b][:, :, :], e, loaded[b])
                    if Y:
                        e.dma_start(Y[b][:, :, :], tile_rows(y_in, g)).then_inc(loaded[b], 16)

                def store(g, b):
                    if both:
                        e.wait_ge(got[b], (g - b + R) * (16 * G // R))
                        e.dma_start(tile_rows(out, g), A[b][:, :, :]).then_inc(put_A[b], 16)
                        e.wait_ge(summed, (g + 1) * G)
                        e.dma_start(tile_rows(z_out, g), O[b][:, :, :]).then_inc(put[b], 16)
                    else:
                        e.wait_ge(normed, (g + 1) * G)
                        e.dma_start(tile_rows(out, g), O[b][:, :, :]).then_inc(put[b], 16)

                def body(g, b, full=True):
                    load(g, b, full)
                    late = back(g, b, 0, 3 * G)
                    if late is not None:
                        store(late[0], late[1])

                run_groups(e, s, body, ragged)
                for k in (3, 2, 1):
                    store(NG - k, (NG - k) % R)
                for b in range(R):
                    e.wait_ge(put[b], 16 * uses(s, b))
                    if both:
                        e.wait_ge(put_A[b], 16 * uses(s, b))

            @block.tensor
            def _(e):
                def turn(g, b, t):
                    n = g * G + t
                    o = t % 2
                    if summed_in:
                        e.wait_ge(added, n + 1)
                    elif t == 0:
                        e.wait_ge(got[b], (g - b + R) * (16 * G // R))
                        if both:
                            e.wait_ge(loaded[b], (g - b + R) * (loads // R))
                    if not (first(g) and n < 2):
                        e.wait_ge(copied, n - 1)
                    srcs = [h[t % 4][:, :]] if summed_in else (
                        [X[b][:, t, :], A[b][:, t, :]] if both else [A[b][:, t, :]])
                    for j, src in enumerate(srcs):
                        for k in range(KC):
                            last = e.transpose(hT_ps[o][:, j * KC + k, :], src[:, k * P:(k + 1) * P],
                                               c.ident[:, :])
                    last.then_inc(turned, 1)

                def product(g, b, t):
                    n = g * G + t
                    o = t % 2
                    e.wait_ge(copied, n + 1)
                    if not (first(g) and n < 2):
                        e.wait_ge({"gcn1": normed, "gcn2": halved}.get(kind, summed), n - 1)
                    dst = out_ps[o][:, 0:D]
                    if bias is not None:
                        e.matmul(dst, c.ones[:, :], bias[:, :], start=True, stop=False)
                    for k in range(NS * KC):
                        last = e.matmul(dst, hT[o][:, k, :], weights[k // KC][:, k % KC, :],
                                        start=(k == 0 and bias is None), stop=(k == NS * KC - 1))
                    last.then_inc(multiplied, 1)

                def body(g, b):
                    for t in range(G):
                        turn(g, b, t)
                        late = back(g, b, t, 1)
                        if late is not None:
                            product(*late)

                run_groups(e, s, body)
                behind(s, 1, product)

            @block.scalar
            def _(e):
                def norm(g, b, t):
                    n = g * G + t
                    if t == 0:
                        e.wait_ge(factors, g + 1)
                    e.activation(O[b][:, t, :], O[b][:, t, :], ACT.Identity, scale=scale[b][:, t:t + 1],
                                 bias=shift[b][:, t:t + 1]).then_inc(normed, 1)

                def roots(g, b):
                    e.wait_ge(root_asked, g + 1)
                    e.activation(small[b][:, 3, :], small[b][:, 2, :], ACT.Sqrt).then_inc(root_done, 1)

                def halve(g, b, t):
                    n = g * G + t
                    e.wait_ge(multiplied, n + 1)
                    if not (first(g) and n < 2):
                        e.wait_ge(summed, n - 1)
                    e.activation(half[t % 2][:, :], out_ps[t % 2][:, 0:D], ACT.Copy,
                                 scale=factor[b][:, 0, t:t + 1]).then_inc(halved, 1)

                def rectify(g, b, t):
                    n = g * G + t
                    if t == 0 and not first(g):
                        e.wait_ge(put[b], (g - b) * (16 // R))
                    e.wait_ge(multiplied, n + 1)
                    e.wait_ge(indexed, g + 1)
                    e.activation(O[b][:, t, :], out_ps[t % 2][:, 0:D], ACT.Relu,
                                 scale=factor[b][:, 0, t:t + 1]).then_inc(normed, 1)

                def body(g, b):
                    for t in range(G):
                        n = g * G + t
                        o = t % 2
                        e.wait_ge(turned, n + 1)
                        if not (first(g) and n < 2):
                            e.wait_ge(multiplied, n - 1)
                        e.activation(hT[o][:, :, :], hT_ps[o][:, 0:NS * KC, :], ACT.Copy).then_inc(copied, 1)
                        late = back(g, b, t, 2)
                        if late is not None and kind == "gcn1":
                            rectify(*late)
                        if late is not None and kind == "gcn2":
                            halve(*late)
                        if normed_out:
                            late = back(g, b, t, NORM)
                            if late is not None:
                                norm(*late)
                            if t == LEAD + 1 and back(g, b, 0, G) is not None:
                                roots(*back(g, b, 0, G)[:2])

                run_groups(e, s, body)
                if kind in ("gcn1", "gcn2"):
                    behind(s, 2, rectify if kind == "gcn1" else halve)
                if normed_out:
                    for t in range(NORM):
                        if t == LEAD + 1:
                            roots(NG - 1, (NG - 1) % R)
                        norm(*back(NG, NG % R, t, NORM))

            @block.vector
            def _(e):
                def copies(g, b):
                    if not first(g):
                        e.wait_ge(got[b], (g - b) * (16 * G // R))
                        if kind == "gcn1":
                            e.wait_ge(normed, (g - R + 1) * G)
                    if kind in ("gin", "gcn2"):
                        e.tensor_copy(factor[b][:, 0, :], cols(tables["dinv"], g))
                        if kind == "gcn2":
                            e.tensor_copy(factor[b][:, 1, :], cols(tables["root"], g))
                    if kind == "gcn1":
                        e.tensor_copy(factor[b][:, 0, :], cols(tables["dinv2"], g))
                    e.tensor_copy(index[b][:, :], cols(end, g)).then_inc(indexed, 1)

                def add(g, b, t):
                    n = g * G + t
                    if t == 0:
                        e.wait_ge(got[b], (g - b + R) * (16 * G // R))
                        e.wait_ge(loaded[b], (g - b + R) * (loads // R))
                    if not (first(g) and n < 4):
                        e.wait_ge(turned, n - 3)
                    e.tensor_tensor(out=h[t % 4][:, :], in0=A[b][:, t, :], in1=X[b][:, t, :], op=ALU.add
                                    ).then_inc(added, 1)

                def residual(g, b, t):
                    n = g * G + t
                    if t == 0 and not first(g):
                        e.wait_ge(put[b], (g - b) * (16 // R))
                    if t == 0 and kind == "hop2":
                        e.wait_ge(loaded[b], (g - b + R) * (loads // R))
                    e.wait_ge(multiplied, n + 1)
                    ps = out_ps[t % 2][:, 0:D]
                    if kind == "gcn2":
                        e.wait_ge(halved, n + 1)
                        e.scalar_tensor_tensor(out=O[b][:, t, :], in0=Y[b][:, t, :],
                                               scalar=factor[b][:, 1, t:t + 1], in1=half[t % 2][:, :],
                                               op0=ALU.mult, op1=ALU.add).then_inc(summed, 1)
                    else:
                        e.tensor_tensor(out=O[b][:, t, :], in0=ps, in1=X[b][:, t, :], op=ALU.add
                                        ).then_inc(summed, 1)

                def measure(g, b, t):
                    n = g * G + t
                    e.wait_ge(summed, n + 1)
                    e.bn_stats(out=stats[b][:, t, :], in_=O[b][:, t, :]).then_inc(measured, 1)

                per = 7 if kind == "gin" else 6

                def chained_from(g, k):
                    def chained(ins):
                        k[0] += 1
                        ins.then_inc(chain, 1)
                        e.wait_ge(chain, g * per + k[0])
                    return chained

                def ask(g, b):
                    e.wait_ge(measured, (g + 1) * G)
                    variance(e, chained_from(g, [0]), stats[b], small[b]).then_inc(root_asked, 1)

                def finish(g, b):
                    e.wait_ge(root_done, g + 1)
                    norm_factors(e, chained_from(g, [5]), small[b], scale[b], shift[b],
                                 factor[b][:, 0, :] if kind == "gin" else None).then_inc(factors, 1)

                def body(g, b):
                    if isinstance(g, int):
                        if g == 0:
                            copies(0, 0)
                        if g + 1 < NG:
                            copies(g + 1, (b + 1) % R)
                    else:
                        copies(g + 1, (b + 1) % R)
                    for t in range(G):
                        if summed_in:
                            add(g, b, t)
                        if kind != "gcn1":
                            late = back(g, b, t, LEAD)
                            if late is not None:
                                residual(*late)
                        if normed_out:
                            late = back(g, b, t, LEAD + 1)
                            if late is not None:
                                measure(*late)
                            if back(g, b, 0, G) is not None:
                                if t == LEAD + 1:
                                    ask(*back(g, b, 0, G)[:2])
                                if t == LEAD + 2:
                                    finish(*back(g, b, 0, G)[:2])

                run_groups(e, s, body)
                if kind != "gcn1":
                    for t in range(LEAD + 1):
                        if t < LEAD:
                            residual(*back(NG, NG % R, t, LEAD))
                        if normed_out:
                            measure(*back(NG, NG % R, t, LEAD + 1))
                if normed_out:
                    ask(NG - 1, (NG - 1) % R)
                    finish(NG - 1, (NG - 1) % R)


def degrees(nc, c, tabs):
    with ExitStack() as ctx:
        rooted = semaphores(nc, ctx, "degrees")("rooted")
        block = ctx.enter_context(nc.Block())

        @block.scalar
        def _(e):
            e.activation(tabs["root"][:, :], tabs["degree"][:, :], ACT.Sqrt).then_inc(rooted, 1)

        @block.vector
        def _(e):
            e.reciprocal(out=tabs["dinv2"][:, :], in_=tabs["degree"][:, :])
            e.wait_ge(rooted, 1)
            e.reciprocal(out=tabs["dinv"][:, :], in_=tabs["root"][:, :])


def prepare_weights(nc, c, a, w):
    with ExitStack() as ctx:
        def sb(n, shape, dt):
            return ctx.enter_context(nc.sbuf_tensor(f"prep_{n}", shape, dt))

        sem = semaphores(nc, ctx, "prep")

        HC = a["W1"].shape[1] // P
        w1 = sb("w1", [P, KC, HC * P], F32)
        w2 = sb("w2", [P, HC, D], F32)
        w1T = sb("w1T", [P, HC, D], F32)
        b1 = sb("b1", [P, HC], F32)
        rows = [sb(f"row{j}", [1, D], F32) for j in range(4)]
        heads = sb("heads", [P, 2, D], F32)
        mixed = sb("mixed", [P, 2, KC, D], F32)
        turn_ps = [ctx.enter_context(nc.psum_tensor(f"prep_turn_ps{j}", [P, 512], F32)) for j in range(KC)]
        w_ps = [ctx.enter_context(nc.psum_tensor(f"prep_w_ps{j}", [P, 512], F32)) for j in range(KC)]
        b_ps = ctx.enter_context(nc.psum_tensor("prep_b_ps", [P, 512], F32))
        loaded, turned, copied, multiplied, link, combined = (sem("loaded"), sem("turned"), sem("copied"),
                                                              sem("multiplied"), sem("link"), sem("combined"))
        LOADS = 13
        block = ctx.enter_context(nc.Block())

        def chunks(m):
            return m.rearrange("(k p) n -> p k n", p=P)

        @block.sync
        def _(e):
            for dst, src in ((w1, a["W1"]), (w2, a["W2"]), (w["gcn1"], a["G1"]), (w["gcn2"], a["G2"]),
                             (w["hop_x"], a["H"][0:D, :]), (w["hop_1"], a["H"][D:2 * D, :]),
                             (w["hop_2"], a["H"][2 * D:3 * D, :])):
                e.dma_start(dst[:, :, :], chunks(src)).then_inc(loaded, 16)
            e.dma_start(w["gat"][:, :, 0:D], chunks(a["A"])).then_inc(loaded, 16)
            with nc.allow_non_contiguous_dma(reason="a bias of 512 elements as columns"):
                e.dma_start(b1[:, :], a["b1"].rearrange("(k p) -> p k", p=P)).then_inc(loaded, 16)
            e.dma_start(rows[0][:, :], a["b2"].rearrange("(o d) -> o d", o=1)).then_inc(loaded, 16)
            e.dma_start(rows[1][:, :], a["b"].rearrange("(o d) -> o d", o=1)).then_inc(loaded, 16)
            for j, m in enumerate((a["al"], a["ar"])):
                e.dma_start(heads[:, j, :], m.rearrange("h d -> (h d)").rearrange("(o n) -> o n", o=1)
                            .broadcast_to([P, D])).then_inc(loaded, 16)

        @block.tensor
        def _(e):
            e.wait_ge(loaded, 16 * LOADS)
            for k in range(KC):
                for j in range(HC):
                    last = e.transpose(turn_ps[k][:, j * P:(j + 1) * P], w1[:, k, j * P:(j + 1) * P],
                                       c.ident[:, :])
            last.then_inc(turned, 1)
            e.wait_ge(copied, 1)
            for k in range(KC):
                for j in range(HC):
                    e.matmul(w_ps[k][:, 0:D], w1T[:, j, k * P:(k + 1) * P], w2[:, j, :],
                             start=(j == 0), stop=(j == HC - 1))
            for j in range(HC):
                last = e.matmul(b_ps[0:1, 0:D], b1[:, j:j + 1], w2[:, j, :], start=(j == 0),
                                stop=(j == HC - 1))
            last.then_inc(multiplied, 1)

        @block.vector
        def _(e):
            n = [0]

            def then(ins):
                n[0] += 1
                ins.then_inc(link, 1)
                e.wait_ge(link, n[0])

            e.memset(w["bias_gin"][:, :], 0.0)
            then(e.memset(w["bias_hop"][:, :], 0.0))
            e.wait_ge(turned, 1)
            for k in range(KC):
                last = e.tensor_copy(w1T[:, :, k * P:(k + 1) * P],
                                     turn_ps[k][:, :].rearrange("p (j m) -> p j m", j=HC))
            last.then_inc(copied, 1)
            e.wait_ge(multiplied, 1)
            for k in range(KC):
                e.tensor_copy(w["gin"][:, k, :], w_ps[k][:, 0:D])
            then(e.tensor_tensor(out=rows[0][:, :], in0=b_ps[0:1, 0:D], in1=rows[0][:, :], op=ALU.add))
            for row, dst in ((rows[0], w["bias_gin"]), (rows[1], w["bias_hop"])):
                left = row
                for part, rest in ((0, rows[2]), (32, rows[3]), (64, None)):
                    then(e.tensor_copy(dst[part:part + 1, :], left[:, :]))
                    if rest is not None:
                        then(e.tensor_tensor(out=rest[:, :], in0=left[:, :], in1=dst[part:part + 1, :]
                                             if part == 0 else dst[part:part + 1, :], op=ALU.subtract))
                        left = rest
            for j, dst in ((0, w["left"][:, :, :]), (1, w["gat"][:, :, D:D + 4])):
                for k in range(KC):
                    then(e.tensor_tensor(out=mixed[:, j, k, :], in0=w["gat"][:, k, 0:D], in1=heads[:, j, :],
                                         op=ALU.mult))
                    then(e.tensor_reduce(out=dst[:, k, :],
                                         in_=mixed[:, j, k, :].rearrange("p (h d) -> p h d", h=4),
                                         axis=AX.X, op=ALU.add))


def left_scores(nc, c, x_view, left, scores):
    s = c.s
    T, NG = s.T, s.NG
    with ExitStack() as ctx:
        sem = semaphores(nc, ctx, "left")

        X = [ctx.enter_context(nc.sbuf_tensor(f"left_X{b}", [P, G, D], F32)) for b in range(R)]
        hT = [ctx.enter_context(nc.sbuf_tensor(f"left_hT{b}", [P, KC, P], F32)) for b in range(2)]
        made = [ctx.enter_context(nc.sbuf_tensor(f"left_made{b}", [P, G, 4], F32)) for b in range(R)]
        hT_ps = [ctx.enter_context(nc.psum_tensor(f"left_hT_ps{b}", [P, 4, P], F32)) for b in range(2)]
        out_ps = [ctx.enter_context(nc.psum_tensor(f"left_out_ps{b}", [P, 512], F32)) for b in range(2)]
        turned, copied, multiplied, kept = sem("turned"), sem("copied"), sem("multiplied"), sem("kept")
        loaded = [sem(f"loaded{b}") for b in range(R)]
        put = [sem(f"put{b}") for b in range(R)]
        out_view = scores[0:s.NP, :].rearrange("(p t) h -> p t h", t=T)
        block = ctx.enter_context(nc.Block())

        @block.sync
        def _(e):
            def body(g, b):
                if not first(g):
                    e.wait_ge(turned, (g - R + 1) * G)
                e.dma_start(X[b][:, :, :], tile_rows(x_view, g)).then_inc(loaded[b], 16)
                late = back(g, b, 0, 3 * G)
                if late is not None:
                    store(*late[:2])

            def store(g, b):
                e.wait_ge(kept, (g + 1) * G)
                e.dma_start(tile_rows(out_view, g), made[b][:, :, :]).then_inc(put[b], 16)

            run_groups(e, s, body)
            for k in (3, 2, 1):
                store(NG - k, (NG - k) % R)
            for b in range(R):
                e.wait_ge(put[b], 16 * uses(s, b))

        @block.tensor
        def _(e):
            def product(g, b, t):
                n = g * G + t
                e.wait_ge(copied, n + 1)
                if not (first(g) and n < 2):
                    e.wait_ge(kept, n - 1)
                for k in range(KC):
                    last = e.matmul(out_ps[t % 2][:, 0:4], hT[t % 2][:, k, :], left[:, k, :],
                                    start=(k == 0), stop=(k == KC - 1))
                last.then_inc(multiplied, 1)

            def body(g, b):
                e.wait_ge(loaded[b], (g - b + R) * (16 // R))
                for t in range(G):
                    n = g * G + t
                    if not (first(g) and n < 2):
                        e.wait_ge(copied, n - 1)
                    for k in range(KC):
                        last = e.transpose(hT_ps[t % 2][:, k, :], X[b][:, t, k * P:(k + 1) * P], c.ident[:, :])
                    last.then_inc(turned, 1)
                    late = back(g, b, t, 1)
                    if late is not None:
                        product(*late)

            run_groups(e, s, body)
            behind(s, 1, product)

        @block.scalar
        def _(e):
            def body(g, b):
                for t in range(G):
                    n = g * G + t
                    e.wait_ge(turned, n + 1)
                    if not (first(g) and n < 2):
                        e.wait_ge(multiplied, n - 1)
                    e.activation(hT[t % 2][:, :, :], hT_ps[t % 2][:, 0:KC, :], ACT.Copy).then_inc(copied, 1)

            run_groups(e, s, body)

        @block.vector
        def _(e):
            def body(g, b):
                if not first(g):
                    e.wait_ge(put[b], (g - b) * (16 // R))
                for t in range(G):
                    e.wait_ge(multiplied, g * G + (t + 1))
                    e.tensor_copy(made[b][:, t, :], out_ps[t % 2][:, 0:4]).then_inc(kept, 1)

            run_groups(e, s, body)


def gat_phase(nc, c, x_rows, x_view, scores, left_end, right_end, weight, out, spill):
    s = c.s
    T, NG = s.T, s.NG
    H = 4
    DH = D // H
    WIDE = D + H
    with ExitStack() as ctx:
        def sb(n, shape, dt):
            return ctx.enter_context(nc.sbuf_tensor(f"gat_{n}", shape, dt))

        sem = semaphores(nc, ctx, "gat")

        def ring(n, shape, dt, k=R):
            return [sb(f"{n}{b}", shape, dt) for b in range(k)]

        index = ring("index", [P, 2, G], I32)
        A, X, O = ring("A", [P, G, D], F32), ring("X", [P, G, D], F32), ring("O", [P, G, D], F32)
        L = ring("L", [P, G, H], F32)
        XT = ring("XT", [P, G, WIDE], F32, 2)
        hT = ring("hT", [P, KC, P], F32, 2)
        score = ring("score", [P, 3, G, H], F32, 2)
        top = ring("top", [P, 3, G], F32, 2)
        prod = sb("prod", [P, G, D], F32)
        mix = sb("mix", [P, G, DH], F32)
        stats = ring("stats", [P, G, 6], F32)
        small = ring("small", [P, 4, G], F32)
        scale, shift = ring("scale", [P, G], F32), ring("shift", [P, G], F32)
        hT_ps = [ctx.enter_context(nc.psum_tensor(f"gat_hT_ps{b}", [P, 4, P], F32)) for b in range(2)]
        out_ps = [ctx.enter_context(nc.psum_tensor(f"gat_out_ps{b}", [P, 512], F32)) for b in range(2)]
        indexed, turned, copied, multiplied, kept = (sem("indexed"), sem("turned"), sem("copied"),
                                                     sem("multiplied"), sem("kept"))
        chain, exp_asked, exp_done, added, measured, root_asked, root_done, factors, normed = (
            sem("chain"), sem("exp_asked"), sem("exp_done"), sem("added"), sem("measured"),
            sem("root_asked"), sem("root_done"), sem("factors"), sem("normed"))
        got = [sem(f"got{b}") for b in range(R)]
        loaded = [sem(f"loaded{b}") for b in range(R)]
        put = [sem(f"put{b}") for b in range(R)]
        NORM = 2 * G + 4
        WAITS = 2 * 16 * G
        out_top = out[0:(P - 1) * T, :].rearrange("(p t) d -> p t d", t=T)
        out_rest = out[(P - 1) * T:s.N, :].rearrange("(p t) d -> p t d", p=1)
        spill_view = spill[:, :].rearrange("(p t) d -> p t d", p=1)

        with nc.Block() as block:
            @block.gpsimd
            def _(e):
                def body(g, b):
                    e.wait_ge(indexed, g + 1)
                    if not first(g):
                        e.wait_ge(turned, (g - R + 1) * G)
                        e.wait_ge(exp_asked, g - R + 1)
                    e.nop(nofuse=True)
                    for t in range(G):
                        gather(e, A[b][:, t, :], x_rows[:, :], index[b][:, 0, t:t + 1]).then_inc(got[b], 16)
                        gather(e, L[b][:, t, :], scores[:, :], index[b][:, 1, t:t + 1]).then_inc(got[b], 16)

                run_groups(e, s, body)

            @block.sync
            def _(e):
                def store(g, b, full):
                    e.wait_ge(normed, (g + 1) * G)
                    e.dma_start(tile_rows(out_top, g, 0, 112), O[b][0:112]).then_inc(put[b], 16)
                    e.dma_start(tile_rows(out_top, g, 112, 127), O[b][112:127]).then_inc(put[b], 16)
                    e.dma_start(tile_rows(out_rest if full else spill_view, g, 0, 1), O[b][127:128]
                                ).then_inc(put[b], 16)

                def body(g, b, full):
                    if not first(g):
                        e.wait_ge(added, g - R + 1)
                    e.dma_start(X[b][:, :, :], tile_rows(x_view, g)).then_inc(loaded[b], 16)
                    late = back(g, b, 0, 4 * G)
                    if late is not None:
                        store(late[0], late[1], late[0] < s.full if isinstance(late[0], int) else full)

                run_groups(e, s, body, 2)
                for k in (4, 3, 2, 1):
                    store(NG - k, (NG - k) % R, False)
                for b in range(R):
                    e.wait_ge(put[b], 48 * uses(s, b))

            @block.tensor
            def _(e):
                def product(g, b, t):
                    n = g * G + t
                    e.wait_ge(copied, n + 1)
                    if not (first(g) and n < 2):
                        e.wait_ge(kept, n - 1)
                    for k in range(KC):
                        last = e.matmul(out_ps[t % 2][:, 0:WIDE], hT[t % 2][:, k, :], weight[:, k, :],
                                        start=(k == 0), stop=(k == KC - 1))
                    last.then_inc(multiplied, 1)

                def body(g, b):
                    e.wait_ge(got[b], (g - b + R) * (WAITS // R))
                    for t in range(G):
                        n = g * G + t
                        if not (first(g) and n < 2):
                            e.wait_ge(copied, n - 1)
                        for k in range(KC):
                            last = e.transpose(hT_ps[t % 2][:, k, :], A[b][:, t, k * P:(k + 1) * P],
                                               c.ident[:, :])
                        last.then_inc(turned, 1)
                        late = back(g, b, t, 1)
                        if late is not None:
                            product(*late)

                run_groups(e, s, body)
                behind(s, 1, product)

            @block.scalar
            def _(e):
                def keep(g, b, t):
                    n = g * G + t
                    if t == 0 and not (isinstance(g, int) and g < 2):
                        e.wait_ge(added, g - 1)
                    e.wait_ge(multiplied, n + 1)
                    e.activation(XT[b % 2][:, t, :], out_ps[t % 2][:, 0:WIDE], ACT.Copy).then_inc(kept, 1)

                def roots(g, b):
                    e.wait_ge(root_asked, g + 1)
                    e.activation(small[b][:, 3, :], small[b][:, 2, :], ACT.Sqrt).then_inc(root_done, 1)

                def exponents(g, b):
                    e.wait_ge(exp_asked, g + 1)
                    e.activation(score[b % 2][:, 2, :, :], score[b % 2][:, 1, :, :], ACT.Exp
                                 ).then_inc(exp_done, 1)

                def norm(g, b, t):
                    if t == 0:
                        e.wait_ge(factors, g + 1)
                    e.activation(O[b][:, t, :], O[b][:, t, :], ACT.Identity, scale=scale[b][:, t:t + 1],
                                 bias=shift[b][:, t:t + 1]).then_inc(normed, 1)

                def body(g, b):
                    for t in range(G):
                        n = g * G + t
                        e.wait_ge(turned, n + 1)
                        if not (first(g) and n < 2):
                            e.wait_ge(multiplied, n - 1)
                        e.activation(hT[t % 2][:, :, :], hT_ps[t % 2][:, 0:KC, :], ACT.Copy).then_inc(copied, 1)
                        late = back(g, b, t, 2)
                        if late is not None:
                            keep(*late)
                        if t == 2 and back(g, b, 0, 2 * G) is not None:
                            roots(*back(g, b, 0, 2 * G)[:2])
                        if t == 3 and back(g, b, 0, G) is not None:
                            exponents(*back(g, b, 0, G)[:2])
                        late = back(g, b, t, NORM)
                        if late is not None:
                            norm(*late)

                run_groups(e, s, body)
                behind(s, 2, keep)
                for t in range(2):
                    norm(*back(NG, NG % R, t, NORM))
                roots(NG - 2, (NG - 2) % R)
                exponents(NG - 1, (NG - 1) % R)
                for t in range(2, NORM):
                    if t == G + 4:
                        roots(NG - 1, (NG - 1) % R)
                    norm(*back(NG, NG % R, t, NORM))

            @block.vector
            def _(e):
                PER = 14

                def chained_from(g, k):
                    def chained(ins):
                        k[0] += 1
                        ins.then_inc(chain, 1)
                        e.wait_ge(chain, g * PER + k[0])
                    return chained

                def copies(g, b):
                    if not first(g):
                        e.wait_ge(got[b], (g - b) * (WAITS // R))
                    e.tensor_copy(index[b][:, 0, :], cols(right_end, g))
                    e.tensor_copy(index[b][:, 1, :], cols(left_end, g)).then_inc(indexed, 1)

                def finish(g, b):
                    e.wait_ge(root_done, g + 1)
                    norm_factors(e, chained_from(g, [PER - 1]), small[b], scale[b], shift[b], None
                                 ).then_inc(factors, 1)

                def attend(g, b):
                    chained = chained_from(g, [0])
                    raw, low, high = (score[b % 2][:, j, :, :] for j in range(3))
                    best, total, inverse = (top[b % 2][:, j, :] for j in range(3))
                    e.wait_ge(kept, (g + 1) * G)
                    e.wait_ge(got[b], (g - b + R) * (WAITS // R))
                    chained(e.tensor_tensor(out=raw, in0=XT[b % 2][:, :, D:WIDE], in1=L[b][:, :, :], op=ALU.add))
                    chained(e.scalar_tensor_tensor(out=raw, in0=raw, scalar=0.01, in1=raw, op0=ALU.mult,
                                                   op1=ALU.max))
                    chained(e.tensor_reduce(out=best, in_=raw, axis=AX.X, op=ALU.max))
                    e.tensor_tensor(out=low, in0=raw, in1=best.unsqueeze(2).broadcast_to([P, G, H]),
                                    op=ALU.subtract).then_inc(exp_asked, 1)
                    e.wait_ge(exp_done, g + 1)
                    chained(e.tensor_reduce(out=total, in_=high, axis=AX.X, op=ALU.add))
                    chained(e.reciprocal(out=inverse, in_=total))
                    chained(e.tensor_tensor(out=low, in0=high, in1=inverse.unsqueeze(2).broadcast_to([P, G, H]),
                                            op=ALU.mult))
                    for t in range(G):
                        ins = e.tensor_tensor(out=prod[:, t, :].rearrange("p (h d) -> p h d", h=H),
                                              in0=XT[b % 2][:, t, 0:D].rearrange("p (h d) -> p h d", h=H),
                                              in1=low[:, t, :].unsqueeze(2).broadcast_to([P, H, DH]), op=ALU.mult)
                    chained(ins)
                    chained(e.tensor_reduce(out=mix[:, :, :], in_=prod[:, :, :].rearrange("p g (h d) -> p g d h", h=H),
                                            axis=AX.X, op=ALU.add))
                    e.wait_ge(loaded[b], (g - b + R) * (16 // R))
                    if not first(g):
                        e.wait_ge(put[b], (g - b) * (48 // R))
                    e.tensor_tensor(out=O[b][:, :, :].rearrange("p g (h d) -> p g h d", h=H),
                                    in0=X[b][:, :, :].rearrange("p g (h d) -> p g h d", h=H),
                                    in1=mix[:, :, :].unsqueeze(2).broadcast_to([P, G, H, DH]), op=ALU.add
                                    ).then_inc(added, 1)
                    e.wait_ge(added, g + 1)
                    for t in range(G):
                        e.bn_stats(out=stats[b][:, t, :], in_=O[b][:, t, :]).then_inc(measured, 1)
                    e.wait_ge(measured, (g + 1) * G)
                    variance(e, chained_from(g, [8]), stats[b], small[b]).then_inc(root_asked, 1)

                def body(g, b):
                    if isinstance(g, int):
                        if g == 0:
                            copies(0, 0)
                        if g + 1 < NG:
                            copies(g + 1, (b + 1) % R)
                    else:
                        copies(g + 1, (b + 1) % R)
                    if back(g, b, 0, 2 * G) is not None:
                        finish(*back(g, b, 0, 2 * G)[:2])
                    if back(g, b, 0, G) is not None:
                        attend(*back(g, b, 0, G)[:2])

                run_groups(e, s, body)
                finish(NG - 2, (NG - 2) % R)
                attend(NG - 1, (NG - 1) % R)
                finish(NG - 1, (NG - 1) % R)


def gnn_stack(nc, a, out):
    s = Shape(a["x"].shape[0])
    T = s.T

    def dram(name, shape):
        return nc.dram_tensor(name, shape, F32).ap()

    with ExitStack() as ctx:
        c = Core(nc, s, ctx)
        runs = dram("runs", (s.NP + 1, D))
        sorted_src, sorted_dst = dram("sorted_src", (s.NP, 4)), dram("sorted_dst", (s.NP, 4))
        z1, z2, x2, hop, part, x3 = (dram(n, (s.NP, D)) for n in ("z1", "z2", "x2", "hop", "part", "x3"))
        scores = dram("scores", (s.NP, 4))
        spill = dram("spill", (T, D))

        def tiled(rows):
            return rows[0:s.NP, :].rearrange("(p t) d -> p t d", t=T)

        def table(name, dt, shape=None):
            return c.sb(name, shape or [P, T], dt)

        unsorted = table("unsorted", I32, [P, 1])
        by_src = {"unsorted": unsorted, "end": table("src_end", I32), "other": table("src_other", I32),
                  "weight": table("src_weight", F32), "same": table("src_same", F32),
                  "fix_row": table("src_fix_row", I32, [P, 1]), "fix": table("src_fix", F32, [P, P])}
        by_dst = {"unsorted": unsorted, "end": table("dst_end", I32), "other": table("dst_other", I32),
                  "same": table("dst_same", F32), "degree": table("degree", F32),
                  "root": table("root", F32), "dinv": table("dinv", F32), "dinv2": table("dinv2", F32),
                  "fix_row": table("dst_fix_row", I32, [P, 1]), "fix": table("dst_fix", F32, [P, P])}
        edge_src, edge_dst = table("edge_src", I32), table("edge_dst", I32)
        w = {n: c.sb(f"w_{n}", [P, KC, D], F32) for n in ("gin", "gcn1", "gcn2", "hop_x", "hop_1", "hop_2")}
        w["gat"] = c.sb("w_gat", [P, KC, D + 4], F32)
        w["left"] = c.sb("w_left", [P, KC, 4], F32)
        w["bias_gin"], w["bias_hop"] = c.sb("bias_gin", [P, D], BF16), c.sb("bias_hop", [P, D], BF16)

        constants(nc, c, runs)
        prepare_weights(nc, c, a, w)
        sort_edges(nc, c, "src", a["src"], a["dst"], a["edge_weight"], sorted_src, by_src, edge_src, edge_dst)
        sorted_tables(nc, c, "src", sorted_src, by_src)
        edge_phase(nc, c, "gin_e", a["x"], by_src, runs)
        sort_edges(nc, c, "dst", a["dst"], a["src"], None, sorted_dst, by_dst)
        sorted_tables(nc, c, "dst", sorted_dst, by_dst)
        degrees(nc, c, by_dst)
        node_phase(nc, c, "gin_n", "gin", runs, by_src["end"], a["x"], tiled(z1), [w["gin"]],
                   bias=w["bias_gin"], ragged=1, tables=by_dst)
        edge_phase(nc, c, "gcn1_e", z1, by_dst, runs)
        node_phase(nc, c, "gcn1_n", "gcn1", runs, by_dst["end"], tiled(z1), tiled(z2), [w["gcn1"]],
                   tables=by_dst)
        edge_phase(nc, c, "gcn2_e", z2, by_dst, runs)
        node_phase(nc, c, "gcn2_n", "gcn2", runs, by_dst["end"], tiled(z2), tiled(x2), [w["gcn2"]],
                   y_in=tiled(z1), tables=by_dst)
        edge_phase(nc, c, "hop1_e", x2, by_src, runs, weighted=True)
        node_phase(nc, c, "hop1_n", "hop1", runs, by_src["end"], tiled(x2), tiled(hop),
                   [w["hop_x"], w["hop_1"]], bias=w["bias_hop"], z_out=tiled(part))
        edge_phase(nc, c, "hop2_e", hop, by_src, runs, weighted=True)
        node_phase(nc, c, "hop2_n", "hop2", runs, by_src["end"], tiled(part), tiled(x3), [w["hop_2"]])
        left_scores(nc, c, tiled(x3), w["left"], scores)
        gat_phase(nc, c, x3, tiled(x3), scores, edge_src, edge_dst, w["gat"], out, spill)


INPUTS = {"x": "x", "src": "src", "dst": "dst", "edge_weight": "edge_weight", "W1": "L0_gnn_W1",
          "b1": "L0_gnn_b1", "W2": "L0_gnn_W2", "b2": "L0_gnn_b2", "G1": "L1_gnn_W1", "G2": "L1_gnn_W2",
          "H": "L2_gnn_W", "b": "L2_gnn_b", "A": "L3_gnn_weight", "al": "L3_gnn_attn_l",
          "ar": "L3_gnn_attn_r"}


def kernel(**inputs):
    import concourse.bacc as bacc
    from concourse.bass_utils import run_bass_kernel_spmd

    nc = bacc.Bacc("TRN2", target_bir_lowering=False, num_devices=1)
    arrays, aps = {}, {}
    for short, name in INPUTS.items():
        v = np.ascontiguousarray(inputs[name])
        arrays[f"in_{name}"] = v
        aps[short] = nc.dram_tensor(f"in_{name}", v.shape, mybir.dt.from_np(v.dtype), kind="ExternalInput").ap()
    out = nc.dram_tensor("out_x", inputs["x"].shape, F32, kind="ExternalOutput").ap()
    gnn_stack(nc, aps, out)
    r = run_bass_kernel_spmd(nc, [arrays], core_ids=[0])
    return r.results[0]["out_x"]
```

```python
from contextlib import ExitStack

import numpy as np
import concourse.bass as bass
from concourse import mybir

F32 = mybir.dt.float32
F16 = mybir.dt.float16
BF16 = mybir.dt.bfloat16
I32 = mybir.dt.int32
ALU = mybir.AluOpType
ACT = mybir.ActivationFunctionType
AX = mybir.AxisListType
P = 128
D = 256
KC = D // P
H = 4
WIDE = D + H
G = 8
R = 4
EPS = 1e-5
ROUND = float(3 << 22)


class Shape:

    def __init__(self, n):
        self.N = n
        self.T = -(-n // (P * G)) * G
        self.NP = P * self.T
        self.NG = self.T // G
        self.last = n - (P - 1) * self.T
        self.full = self.last // G
        assert self.last == self.full * G and self.full % R == R - 1 and self.full >= 2 * R
        assert self.NG % R == 1 and self.NG > self.full + 2 * R


def run_groups(e, s, body, ragged=0):
    args = (lambda g: (g, g % R, g < s.full)) if ragged else (lambda g: (g, g % R))
    for g in range(R):
        body(*args(g))
    if ragged:
        turn = (s.full + 1) // R
        with e.Fori(1, turn - 1) as i:
            for b in range(R):
                body(i * R + b, b, True)
        for g in range((turn - 1) * R, (turn + ragged - 1) * R):
            body(*args(g))
        with e.Fori(turn + ragged - 1, s.NG // R) as i:
            for b in range(R):
                body(i * R + b, b, False)
    else:
        with e.Fori(1, s.NG // R) as i:
            for b in range(R):
                body(i * R + b, b)
    body(*args(s.NG - 1))


def first(g):
    return isinstance(g, int) and g < R


def uses(s, b):
    return (s.NG - 1 - b) // R + 1


def cols(table, g):
    return table[:, bass.ds(g * G, G)] if not isinstance(g, int) else table[:, g * G:(g + 1) * G]


def tile_rows(view, g, lo=0, hi=P):
    return view[lo:hi, g * G:(g + 1) * G, :] if isinstance(g, int) else view[lo:hi, bass.ds(g * G, G), :]


def semaphores(nc, ctx, name):
    taken = []

    def sem(n):
        taken.append(nc.alloc_semaphore(f"{name}_{n}"))
        return taken[-1]

    def give_back():
        nc.clear_and_free_semaphores(taken)
        nc.all_engine_barrier()

    ctx.callback(give_back)
    return sem


def gather(e, out, table, index):
    return e.indirect_dma_start(out=out, out_offset=None, in_=table,
                                in_offset=bass.IndirectOffsetOnAxis(ap=index, axis=0))


class Core:

    def __init__(self, nc, s, ctx):
        self.nc, self.s, self.ctx = nc, s, ctx
        T = s.T
        sb = self.sb
        self.iota_free = sb("iota_free", [P, T], F16)
        self.iota_part = sb("iota_part", [P, 1], F32)
        self.node_f = sb("node_f", [P, T], F32)
        self.lower = sb("lower", [P, P], F32)
        self.before = sb("before", [P, P], F32)
        self.ident = sb("ident", [P, P], F32)
        self.identh = sb("identh", [P, P], F16)
        self.ones = sb("ones", [P, P], BF16)
        self.onesT = sb("onesT", [P, T], F32)
        self.zero_row = sb("zero_row", [1, WIDE], F32)

    def sb(self, name, shape, dt):
        return self.ctx.enter_context(self.nc.sbuf_tensor(name, shape, dt))


def constants(nc, c, runs, hops):
    s = c.s
    with ExitStack() as ctx:
        sem = semaphores(nc, ctx, "consts")
        num = ctx.enter_context(nc.sbuf_tensor("num", [P, s.T], I32))
        num2 = ctx.enter_context(nc.sbuf_tensor("num2", [P, s.T], I32))
        part = ctx.enter_context(nc.sbuf_tensor("part_no", [P, 1], I32))
        iotas = sem("iotas")
        blank = sem("blank")
        done = sem("consts_done")
        zeroed = sem("zeroed")
        zero_put = sem("zero_put")
        block = ctx.enter_context(nc.Block())

        @block.gpsimd
        def _(e):
            e.iota(num[:, :], pattern=[[1, s.T]], base=0, channel_multiplier=s.T)
            e.iota(num2[:, :], pattern=[[1, s.T]], base=0, channel_multiplier=0)
            e.iota(part[:, :], pattern=[[1, 1]], base=0, channel_multiplier=1).then_inc(iotas, 1)
            e.memset(c.lower[:, :], 1.0).then_inc(blank, 1)
            e.memset(c.before[:, :], 1.0).then_inc(blank, 1)
            e.memset(c.ident[:, :], 0.0).then_inc(blank, 1)
            e.wait_ge(blank, 3)
            e.affine_select(out=c.lower[:, :], in_=c.lower[:, :], compare_op=ALU.is_gt, fill=0.0,
                            base=0, pattern=[[1, P]], channel_multiplier=-1)
            e.affine_select(out=c.before[:, :], in_=c.before[:, :], compare_op=ALU.is_gt, fill=0.0,
                            base=0, pattern=[[-1, P]], channel_multiplier=1)
            e.affine_select(out=c.ident[:, :], in_=c.ident[:, :], compare_op=ALU.not_equal, fill=1.0,
                            base=0, pattern=[[-1, P]], channel_multiplier=1).then_inc(done, 1)

        @block.vector
        def _(e):
            e.memset(c.ones[:, :], 1.0)
            e.memset(c.onesT[:, :], 1.0)
            e.memset(c.zero_row[:, :], 0.0).then_inc(zeroed, 1)
            e.wait_ge(iotas, 1)
            e.tensor_copy(c.node_f[:, :], num[:, :])
            e.tensor_copy(c.iota_free[:, :], num2[:, :])
            e.tensor_copy(c.iota_part[:, :], part[:, :])
            e.wait_ge(done, 1)
            e.tensor_copy(c.identh[:, :], c.ident[:, :])


        @block.sync
        def _(e):
            e.wait_ge(zeroed, 1)
            e.dma_start(runs[s.NP:s.NP + 1, :], c.zero_row[0:1, 0:D]).then_inc(zero_put, 16)
            e.dma_start(hops[s.NP:s.NP + 1, :], c.zero_row[0:1, :]).then_inc(zero_put, 16)
            e.wait_ge(zero_put, 32)


def sort_edges(nc, c, name, key_dram, other_dram, weight_dram, rec_dram, tabs, key_kept=None, other_kept=None):
    s = c.s
    T, NG = s.T, s.NG
    with ExitStack() as ctx:
        def sb(n, shape, dt):
            return ctx.enter_context(nc.sbuf_tensor(f"{name}_{n}", shape, dt))

        sem = semaphores(nc, ctx, f"{name}")

        key_i, other_i = sb("key_i", [P, T], I32), sb("other_i", [P, T], I32)
        key_f = sb("key_f", [P, T], F32)
        hi, lo, tmp = sb("hi", [P, T], F32), sb("lo", [P, T], F32), sb("tmp", [P, T], F32)
        rec = sb("rec", [P, T, 4], F32)
        rec_now = [sb(f"rec_now{b}", [P, G, 4], F32) for b in range(R)]
        pos_now = [sb(f"pos_now{b}", [P, G], I32) for b in range(R)]
        lh = [sb(f"lh{b}", [P, G, 3], F32) for b in range(R)]
        hot_hi = [sb(f"hot_hi{b}", [P, P], F16) for b in range(4)]
        hot_lo = [sb(f"hot_lo{b}", [P, T], F16) for b in range(4)]
        hot_hiT = [sb(f"hot_hiT{b}", [P, P], F32) for b in range(2)]
        same_key = [sb(f"same_key{b}", [P, P], F32) for b in range(2)]
        count = [sb(f"count{b}", [P, T], F32) for b in range(2)]
        offset = sb("offset", [P, T], F32)
        prod = sb("prod", [P, T], F32)
        picked = [sb(f"picked{b}", [P, T], F32) for b in range(2)]
        hit = [sb(f"hit{b}", [P, G], F32) for b in range(R)]
        rank = [sb(f"rank{b}", [P, G], F32) for b in range(R)]
        row_sum = sb("row_sum", [P, 1], F32)
        hist_ps = ctx.enter_context(nc.psum_tensor(f"{name}_hist", [P, 512], F32))
        hotT_bank = [ctx.enter_context(nc.psum_tensor(f"{name}_hotT{b}", [P, 1024], F16)) for b in range(2)]
        key_ps = [ctx.enter_context(nc.psum_tensor(f"{name}_key{b}", [P, 512], F32)) for b in range(2)]
        at_ps = [ctx.enter_context(nc.psum_tensor(f"{name}_at{b}", [P, 512], F32)) for b in range(2)]
        LATE = 3
        next_i = sb("next_i", [P, T], I32)
        falls = sb("falls", [P, 1], F32)

        own, loaded, link = sem("own"), sem("loaded"), sem("link")
        with nc.Block() as block:
            @block.vector
            def _(e):
                n = [0]

                def then(ins):
                    n[0] += 1
                    ins.then_inc(link, 1)
                    e.wait_ge(link, n[0])

                e.tensor_copy(key_i[:, :], c.node_f[:, :])
                e.memset(rec[:, :, :], 0.0)
                e.memset(tmp[:, :], 0.0)
                e.tensor_scalar(next_i[:, :], c.node_f[:, :], 1.0, None, ALU.add)
                then(e.memset(other_i[:, :], 0))
                e.sem_inc(own, 1)
                e.wait_ge(loaded, 16 * (12 if weight_dram is not None else 9))
                then(e.tensor_tensor(out=lo[:, :], in0=key_i[:, :], in1=next_i[:, :], op=ALU.is_gt))
                then(e.tensor_reduce(out=falls[:, :], in_=lo[:, :], axis=AX.X, op=ALU.add))
                e.tensor_copy(key_f[:, :], key_i[:, :]).then_inc(link, 1)
                n[0] += 1
                then(e.tensor_copy(rec[:, :, 1], other_i[:, :]))
                then(e.tensor_copy(rec[:, :, 2], tmp[:, :]))
                if key_kept is not None:
                    e.tensor_copy(key_kept[:, :], key_i[:, :])
                    e.tensor_copy(other_kept[:, :], other_i[:, :])
                then(e.tensor_scalar(tmp[:, :], key_f[:, :], (T - 1) / 2, 1.0 / T,
                                     ALU.subtract, ALU.mult))
                then(e.tensor_scalar(hi[:, :], tmp[:, :], ROUND, ROUND, ALU.add, ALU.subtract))
                e.scalar_tensor_tensor(out=lo[:, :], in0=hi[:, :], scalar=-float(T), in1=key_f[:, :],
                                       op0=ALU.mult, op1=ALU.add)
                e.tensor_copy(rec[:, :, 0], key_f[:, :])

            @block.sync
            def _(e):
                e.wait_ge(own, 1)
                pieces = [(key_dram, key_i, 0), (key_dram, next_i, 1), (other_dram, other_i, 0)]
                if weight_dram is not None:
                    pieces.append((weight_dram, tmp, 0))
                cut = (P - 1) * T
                for src, dst, ahead in pieces:
                    body = src[ahead:cut + ahead].rearrange("(p t) -> p t", t=T)
                    e.dma_start(dst[0:112, :], body[0:112, :]).then_inc(loaded, 16)
                    e.dma_start(dst[112:127, :], body[112:127, :]).then_inc(loaded, 16)
                    e.dma_start(dst[127:128, 0:s.last - ahead],
                                src[cut + ahead:s.N].rearrange("(a t) -> a t", a=1)).then_inc(loaded, 16)

        first_hot, counted, hist_done, link2, base_done = (sem("first_hot"), sem("counted"), sem("hist_done"),
                                                   sem("link2"), sem("base_done"))
        lh_ready = sem("lh_ready")
        with nc.Block() as block:
            @block.vector
            def _(e):
                def body(g, b):
                    if not first(g):
                        e.wait_ge(first_hot, (g - R + 1) * G)
                    e.tensor_copy(lh[b][:, :, 0], cols(hi, g))
                    e.tensor_copy(lh[b][:, :, 1], cols(lo, g)).then_inc(lh_ready, 1)
                    e.wait_ge(lh_ready, g + 1)
                    for t in range(G):
                        o = t % 4
                        if not (first(g) and g * G + t < 4):
                            e.wait_ge(counted, g * G + (t - 3))
                        e.tensor_scalar(hot_hi[o][:, :], c.iota_free[:, 0:P], lh[b][:, t, 0:1], None,
                                        ALU.is_equal)
                        e.tensor_scalar(hot_lo[o][:, :], c.iota_free[:, :], lh[b][:, t, 1:2], None,
                                        ALU.is_equal).then_inc(first_hot, 1)

                run_groups(e, s, body)
                n = [0]

                def then(ins):
                    n[0] += 1
                    ins.then_inc(link2, 1)
                    e.wait_ge(link2, n[0])

                e.wait_ge(counted, T)
                then(e.tensor_copy(count[1][:, :], hist_ps[:, 0:T]))
                then(e.tensor_tensor_scan(out=count[0][:, :], data0=c.onesT[:, :], data1=count[1][:, :],
                                          initial=0.0, op0=ALU.mult, op1=ALU.add))
                then(e.tensor_copy(row_sum[:, :], count[0][:, T - 1:T]))
                e.sem_inc(hist_done, 1)
                e.wait_ge(base_done, 1)
                then(e.tensor_copy(row_sum[:, :], at_ps[0][:, 0:1]))
                then(e.tensor_scalar(falls[:, :], at_ps[1][:, 0:1], 1.0, None, ALU.min))
                then(e.tensor_copy(tabs["unsorted"][:, :], falls[:, :]))
                then(e.tensor_scalar(count[0][:, :], count[0][:, :], row_sum[:, 0:1], None, ALU.add))
                then(e.tensor_tensor(out=offset[:, :], in0=count[0][:, :], in1=count[1][:, :],
                                     op=ALU.subtract))
                then(e.tensor_scalar(tmp[:, :], count[1][:, :], 0.0, None, ALU.is_equal))
                then(e.tensor_scalar(prod[:, :], count[0][:, :], -1.0, float(s.NP + 1), ALU.mult, ALU.add))
                then(e.tensor_tensor(out=prod[:, :], in0=prod[:, :], in1=tmp[:, :], op=ALU.mult))
                then(e.tensor_tensor(out=prod[:, :], in0=prod[:, :], in1=count[0][:, :], op=ALU.add))
                then(e.tensor_scalar(prod[:, :], prod[:, :], -1.0, None, ALU.add))
                then(e.tensor_copy(tabs["end"][:, :], prod[:, :]))
                if "degree" in tabs:
                    then(e.tensor_scalar(tabs["degree"][:, :], count[1][:, :], 1.0, None, ALU.add))

            @block.tensor
            def _(e):
                def body(g, b):
                    for t in range(G):
                        o = t % 4
                        e.wait_ge(first_hot, g * G + (t + 1))
                        e.matmul(hist_ps[:, 0:T], hot_hi[o][:, :], hot_lo[o][:, :],
                                 start=(first(g) and g == 0 and t == 0),
                                 stop=(isinstance(g, int) and g == NG - 1 and t == G - 1),
                                 skip_group_check=True).then_inc(counted, 1)

                run_groups(e, s, body)
                e.wait_ge(hist_done, 1)
                e.matmul(at_ps[1][:, 0:1], c.onesT[:, 0:P], falls[:, :], start=True, stop=True)
                e.matmul(at_ps[0][:, 0:1], c.lower[:, :], row_sum[:, :], start=True, stop=True
                         ).then_inc(base_done, 1)

        hot, counted2, snap, keyT_ps, hotT_ps, hotT, at, placed, put = (
            sem("hot"), sem("counted2"), sem("snap"), sem("keyT_ps"), sem("hotT_ps"),
            sem("hotT"), sem("at"), sem("placed"), [sem(f"put{b}") for b in range(R)])
        lh2, ranked, summed, kept = sem("lh2"), sem("ranked"), sem("summed"), sem("kept")
        unsorted = nc.values_load(tabs["unsorted"][0:1, 0:1], min_val=0, max_val=1,
                                  skip_runtime_bounds_check_because="VectorE wrote 0 or 1")
        with nc.If(unsorted > 0), nc.Block() as block:
            @block.vector
            def _(e):
                def pick(g, b, t):
                    n, o = g * G + t, t % 2
                    if not (first(g) and n < 2):
                        e.wait_ge(ranked, n - 1)
                        e.wait_ge(summed, n - 1)
                    e.wait_ge(keyT_ps, n + 1)
                    e.scalar_tensor_tensor(out=same_key[o][:, :], in0=key_ps[o][:, 0:P],
                                           scalar=lh[b][:, t, 2:3], in1=c.before[:, :],
                                           op0=ALU.is_equal, op1=ALU.mult,
                                           accum_out=rank[b][:, t:t + 1]).then_inc(ranked, 1)
                    e.wait_ge(at, n + 1)
                    e.scalar_tensor_tensor(out=picked[o][:, :], in0=at_ps[o][:, 0:T], scalar=0.0,
                                           in1=hot_lo[t % 4][:, :], op0=ALU.add, op1=ALU.mult,
                                           accum_out=hit[b][:, t:t + 1]).then_inc(summed, 1)

                def place(g, b):
                    e.wait_ge(summed, (g + 1) * G)
                    e.wait_ge(ranked, (g + 1) * G)
                    e.tensor_tensor(out=pos_now[b][:, :], in0=hit[b][:, :], in1=rank[b][:, :], op=ALU.add
                                    ).then_inc(placed, 1)

                def body(g, b):
                    if not first(g):
                        e.wait_ge(put[b], (g - b) * (16 * G // R))
                    e.tensor_copy(lh[b][:, :, 0], cols(hi, g))
                    e.tensor_copy(lh[b][:, :, 1], cols(lo, g))
                    e.tensor_copy(lh[b][:, :, 2], cols(key_f, g))
                    e.tensor_copy(rec_now[b][:, :, :],
                                  rec[:, bass.ds(g * G, G), :] if not isinstance(g, int)
                                  else rec[:, g * G:(g + 1) * G, :]).then_inc(lh2, 1)
                    e.wait_ge(lh2, g + 1)
                    for t in range(G):
                        n, o = g * G + t, t % 4
                        if not (first(g) and n < 4):
                            e.wait_ge(counted2, n - 2)
                            e.wait_ge(summed, n - 3)
                        e.tensor_scalar(hot_hi[o][:, :], c.iota_free[:, 0:P], lh[b][:, t, 0:1], None,
                                        ALU.is_equal)
                        e.tensor_scalar(hot_lo[o][:, :], c.iota_free[:, :], lh[b][:, t, 1:2], None,
                                        ALU.is_equal).then_inc(hot, 1)
                        late = back(g, b, t, LATE)
                        if late is not None:
                            pick(*late)
                            if late[2] == G - 1:
                                place(*late[:2])

                run_groups(e, s, body)
                behind(s, LATE, pick)
                place(NG - 1, (NG - 1) % R)

            @block.tensor
            def _(e):
                e.matmul(hist_ps[:, 0:T], c.ident[:, :], offset[:, :], start=True, stop=False,
                         skip_group_check=True).then_inc(counted2, 1)

                def count_tile(g, b, t, stop=False):
                    n, o = g * G + t, t % 2
                    if not (first(g) and n < 2):
                        e.wait_ge(ranked, n - 1)
                        e.wait_ge(summed, n - 1)
                    e.transpose(key_ps[o][:, 0:P], lh[b][:, t, 2:3].broadcast_to([P, P]), c.ident[:, :]
                                ).then_inc(keyT_ps, 1)
                    e.wait_ge(snap, n + 1)
                    e.matmul(hist_ps[:, 0:T], hot_hi[t % 4][:, :], hot_lo[t % 4][:, :], start=False,
                             stop=stop, skip_group_check=True).then_inc(counted2, 1)
                    e.wait_ge(hotT, n + 1)
                    e.matmul(at_ps[o][:, 0:T], hot_hiT[o][:, :], count[o][:, :], start=True,
                             stop=True).then_inc(at, 1)

                def body(g, b):
                    for t in range(G):
                        n, o = g * G + t, t % 2
                        e.wait_ge(hot, n + 1)
                        if not (first(g) and n < 2):
                            e.wait_ge(hotT, n - 1)
                        e.transpose(hotT_bank[o][:, 0:P], hot_hi[t % 4][:, :], c.identh[:, :]
                                    ).then_inc(hotT_ps, 1)
                        late = back(g, b, t, 1)
                        if late is not None:
                            count_tile(*late)

                run_groups(e, s, body)
                count_tile(NG - 1, (NG - 1) % R, G - 1, stop=True)

            @block.scalar
            def _(e):
                def snapshot(g, b, t):
                    n = g * G + t
                    e.wait_ge(counted2, n + 1)
                    if not (first(g) and n < 2):
                        e.wait_ge(at, n - 1)
                    e.activation(count[t % 2][:, :], hist_ps[:, 0:T], ACT.Copy).then_inc(snap, 1)

                def body(g, b):
                    for t in range(G):
                        n, o = g * G + t, t % 2
                        late = back(g, b, t, 1)
                        if late is not None:
                            snapshot(*late)
                        e.wait_ge(hotT_ps, n + 1)
                        if not (first(g) and n < 2):
                            e.wait_ge(at, n - 1)
                        e.activation(hot_hiT[o][:, :], hotT_bank[o][:, 0:P], ACT.Copy
                                     ).then_inc(hotT, 1)

                run_groups(e, s, body)
                behind(s, 1, snapshot)

            @block.gpsimd
            def _(e):
                def body(g, b):
                    e.wait_ge(placed, g + 1)
                    e.nop(nofuse=True)
                    for t in range(G):
                        e.indirect_dma_start(out=rec_dram[:, :],
                                             out_offset=bass.IndirectOffsetOnAxis(
                                                 ap=pos_now[b][:, t:t + 1], axis=0),
                                             in_=rec_now[b][:, t, :], in_offset=None).then_inc(put[b], 16)

                run_groups(e, s, body)
                for b in range(R):
                    e.wait_ge(put[b], 16 * G * uses(s, b))

        with nc.Else(), nc.Block() as block:
            @block.sync
            def _(e):
                e.dma_start(rec_dram[0:s.NP, :].rearrange("(p t) f -> p t f", t=T), rec[:, :, :]
                            ).then_inc(kept, 16)
                e.wait_ge(kept, 16)


def sorted_tables(nc, c, name, rec_dram, tabs):
    s = c.s
    T = s.T
    with ExitStack() as ctx:
        sem = semaphores(nc, ctx, f"{name}")

        rec = ctx.enter_context(nc.sbuf_tensor(f"{name}_sorted", [P, T, 4], F32))
        eq = ctx.enter_context(nc.sbuf_tensor(f"{name}_eq", [P, T], F32))
        last_key = ctx.enter_context(nc.sbuf_tensor(f"{name}_last_key", [P, 1], F32))
        first_key = ctx.enter_context(nc.sbuf_tensor(f"{name}_first_key", [P, 1], F32))
        length = ctx.enter_context(nc.sbuf_tensor(f"{name}_length", [P, 1], F32))
        row_ps = ctx.enter_context(nc.psum_tensor(f"{name}_row", [P, 512], F32))
        loaded, link, keys, row = sem("t_loaded"), sem("t_link"), sem("t_keys"), sem("t_row")
        with nc.Block() as block:
            @block.sync
            def _(e):
                e.dma_start(rec[:, :, :], rec_dram[0:s.NP, :].rearrange("(p t) f -> p t f", t=T)
                            ).then_inc(loaded, 16)

            @block.tensor
            def _(e):
                e.wait_ge(keys, 1)
                e.transpose(row_ps[:, 0:P], first_key[:, 0:1].broadcast_to([P, P]), c.ident[:, :]
                            ).then_inc(row, 1)

            @block.vector
            def _(e):
                n = [0]

                def then(ins):
                    n[0] += 1
                    ins.then_inc(link, 1)
                    e.wait_ge(link, n[0])

                e.wait_ge(loaded, 16)
                then(e.tensor_copy(first_key[:, :], rec[:, 0:1, 0]))
                e.sem_inc(keys, 1)
                then(e.tensor_copy(last_key[:, :], rec[:, T - 1:T, 0]))
                e.tensor_copy(tabs["other"][:, :], rec[:, :, 1])
                if "weight" in tabs:
                    e.tensor_copy(tabs["weight"][:, :], rec[:, :, 2])
                e.memset(tabs["same"][:, 0:1], 0.0)
                e.tensor_tensor(out=tabs["same"][:, 1:T], in0=rec[:, 1:T, 0], in1=rec[:, 0:T - 1, 0],
                                op=ALU.is_equal)
                then(e.tensor_scalar(eq[:, :], rec[:, :, 0], first_key[:, 0:1], None, ALU.is_equal))
                then(e.tensor_reduce(out=length[:, :], in_=eq[:, :], axis=AX.X, op=ALU.add))
                then(e.tensor_scalar(length[:, :], length[:, :], -1.0, None, ALU.add))
                e.tensor_tensor(out=tabs["fix_row"][:, :], in0=length[:, :], in1=c.node_f[:, 0:1],
                                op=ALU.add)
                e.wait_ge(row, 1)
                e.scalar_tensor_tensor(out=tabs["fix"][:, :], in0=row_ps[:, 0:P], scalar=last_key[:, 0:1],
                                       in1=c.lower[:, :], op0=ALU.is_equal, op1=ALU.mult)


def edge_phase(nc, c, name, table, tabs, runs):
    s = c.s
    T, NG = s.T, s.NG
    view = runs[0:s.NP, :].rearrange("(p t) d -> p t d", t=T)
    with ExitStack() as ctx:
        def sb(n, shape, dt):
            return ctx.enter_context(nc.sbuf_tensor(f"{name}_{n}", shape, dt))

        sem = semaphores(nc, ctx, f"{name}")

        index = [sb(f"index{b}", [P, G], I32) for b in range(R)]
        flag = [sb(f"flag{b}", [P, G], F32) for b in range(R)]
        rows = [sb(f"rows{b}", [P, G, D], F32) for b in range(R)]
        run = [sb(f"run{b}", [P, G, D], F32) for b in range(R)]
        fixed = sb("fixed", [P, D], F32)
        carry_ps = ctx.enter_context(nc.psum_tensor(f"{name}_carry", [P, 512], F32))
        indexed, flagged, summed, wrote = sem("indexed"), sem("flagged"), sem("summed"), sem("wrote")
        got = [sem(f"got{b}") for b in range(R)]
        put = [sem(f"put{b}") for b in range(R)]
        fix_got, fix_sum, fix_put, carried = sem("fix_got"), sem("fix_sum"), sem("fix_put"), sem("carried")
        with nc.Block() as block:
            @block.gpsimd
            def _(e):
                def body(g, b):
                    if not first(g):
                        e.wait_ge(summed, (g - R + 1) * G)
                    e.tensor_copy(index[b][:, :], cols(tabs["other"], g)).then_inc(indexed, 1)
                    e.wait_ge(indexed, g + 1)
                    e.nop(nofuse=True)
                    for t in range(G):
                        gather(e, rows[b][:, t, :], table[:, :], index[b][:, t:t + 1]).then_inc(got[b], 16)

                run_groups(e, s, body)
                e.wait_ge(wrote, 1)
                gather(e, fixed[:, :], runs[:, :], tabs["fix_row"][:, 0:1]).then_inc(fix_got, 16)
                e.wait_ge(fix_sum, 1)
                e.indirect_dma_start(out=runs[:, :],
                                     out_offset=bass.IndirectOffsetOnAxis(ap=tabs["fix_row"][:, 0:1], axis=0),
                                     in_=fixed[:, :], in_offset=None).then_inc(fix_put, 16)
                e.wait_ge(fix_put, 16)

            @block.vector
            def _(e):
                e.memset(run[R - 1][:, G - 1, :], 0.0).then_inc(flagged, 1)

                def body(g, b):
                    e.tensor_copy(flag[b][:, :], cols(tabs["same"], g)).then_inc(flagged, 1)
                    e.wait_ge(flagged, g + 2)
                    e.wait_ge(got[b], (g - b + R) * (16 * G // R))
                    if not first(g):
                        e.wait_ge(put[b], (g - b) * (16 // R))
                    for t in range(G):
                        before = run[b][:, t - 1, :] if t else run[(b - 1) % R][:, G - 1, :]
                        if not (isinstance(g, int) and g == 0 and t == 0):
                            e.wait_ge(summed, g * G + t)
                        e.scalar_tensor_tensor(out=run[b][:, t, :], in0=before, scalar=flag[b][:, t:t + 1],
                                               in1=rows[b][:, t, :], op0=ALU.mult, op1=ALU.add
                                               ).then_inc(summed, 1)

                run_groups(e, s, body)
                e.wait_ge(fix_got, 16)
                e.wait_ge(carried, 1)
                e.tensor_tensor(out=fixed[:, :], in0=carry_ps[:, 0:D], in1=fixed[:, :], op=ALU.add
                                ).then_inc(fix_sum, 1)

            @block.sync
            def _(e):
                def body(g, b):
                    e.wait_ge(summed, (g + 1) * G)
                    e.dma_start(tile_rows(view, g), run[b][:, :, :]).then_inc(put[b], 16)

                run_groups(e, s, body)
                for b in range(R):
                    e.wait_ge(put[b], 16 * uses(s, b))
                e.sem_inc(wrote, 1)

            @block.tensor
            def _(e):
                e.wait_ge(summed, T)
                e.matmul(carry_ps[:, 0:D], tabs["fix"][:, :], run[(NG - 1) % R][:, G - 1, :], start=True,
                         stop=True).then_inc(carried, 1)


def hop_phase(nc, c, name, table, index_of, tabs, weight, out, runs=None, next_index=None, passed=None):
    s = c.s
    T, NG = s.T, s.NG
    first_hop = runs is not None
    LEAD = 3
    W = WIDE if first_hop else D

    def rows_of(m):
        return m[0:s.NP, :].rearrange("(p t) d -> p t d", t=T)

    with ExitStack() as ctx:
        def sb(n, shape, dt):
            return ctx.enter_context(nc.sbuf_tensor(f"{name}_{n}", shape, dt))

        sem = semaphores(nc, ctx, f"{name}")

        def ring(n, shape, dt, k=R):
            return [sb(f"{n}{b}", shape, dt) for b in range(k)]

        index, flag, factor = ring("index", [P, G], I32), ring("flag", [P, G], F32), ring("factor", [P, G], F32)
        rows, run, made = ring("rows", [P, G, W], F32), ring("run", [P, G, D], F32), ring("made", [P, G, WIDE], F32)
        Q = None if first_hop else ring("Q", [P, G, WIDE], F32)
        hT = ring("hT", [P, KC, P], F32, 2)
        mend = runs if first_hop else out
        MW = D if first_hop else WIDE
        fixed = sb("fixed", [P, MW], F32)
        hT_ps = [ctx.enter_context(nc.psum_tensor(f"{name}_hT_ps{b}", [P, 4, P], F32)) for b in range(2)]
        out_ps = [ctx.enter_context(nc.psum_tensor(f"{name}_out_ps{b}", [P, 512], F32)) for b in range(2)]
        carry_ps = ctx.enter_context(nc.psum_tensor(f"{name}_carry", [P, 512], F32))
        indexed, flagged, weight_set, weighed, summed, turned, copied, multiplied, kept, wrote = (
            sem("indexed"), sem("flagged"), sem("weight_set"), sem("weighed"), sem("summed"), sem("turned"),
            sem("copied"), sem("multiplied"), sem("kept"), sem("wrote"))
        got = [sem(f"got{b}") for b in range(R)]
        loaded = [sem(f"loaded{b}") for b in range(R)]
        put_run = [sem(f"put_run{b}") for b in range(R)]
        put = [sem(f"put{b}") for b in range(R)]
        fix_got, fix_sum, fix_put, carried = sem("fix_got"), sem("fix_sum"), sem("fix_put"), sem("carried")

        with nc.Block() as block:
            @block.gpsimd
            def _(e):
                def body(g, b):
                    if not first(g):
                        e.wait_ge(summed, (g - R + 1) * G)
                    e.tensor_copy(index[b][:, :], cols(index_of, g)).then_inc(indexed, 1)
                    e.wait_ge(indexed, g + 1)
                    e.nop(nofuse=True)
                    for t in range(G):
                        gather(e, rows[b][:, t, :], table[:, :], index[b][:, t:t + 1]).then_inc(got[b], 16)

                run_groups(e, s, body)
                e.wait_ge(wrote, 1)
                gather(e, fixed[:, :], mend[:, :], tabs["fix_row"][:, 0:1]).then_inc(fix_got, 16)
                e.wait_ge(fix_sum, 1)
                e.indirect_dma_start(out=mend[:, :],
                                     out_offset=bass.IndirectOffsetOnAxis(ap=tabs["fix_row"][:, 0:1], axis=0),
                                     in_=fixed[:, :], in_offset=None).then_inc(fix_put, 16)
                e.wait_ge(fix_put, 16)

            @block.sync
            def _(e):
                def store(g, b):
                    e.wait_ge(kept, (g + 1) * G)
                    e.dma_start(tile_rows(rows_of(out), g), made[b][:, :, :]).then_inc(put[b], 16)

                def body(g, b):
                    if not first_hop:
                        if not first(g):
                            e.wait_ge(kept, (g - R + 1) * G)
                        e.dma_start(Q[b][:, :, :], tile_rows(rows_of(passed), g)).then_inc(loaded[b], 16)
                    late = back(g, b, 0, 3 * G)
                    if late is not None:
                        lg, lb = late[:2]
                        if first_hop:
                            e.wait_ge(summed, (lg + 1) * G)
                            e.dma_start(tile_rows(rows_of(runs), lg), run[lb][:, :, :]).then_inc(put_run[lb], 16)
                        store(lg, lb)

                run_groups(e, s, body)
                for k in (3, 2, 1):
                    lg, lb = NG - k, (NG - k) % R
                    if first_hop:
                        e.wait_ge(summed, (lg + 1) * G)
                        e.dma_start(tile_rows(rows_of(runs), lg), run[lb][:, :, :]).then_inc(put_run[lb], 16)
                    store(lg, lb)
                for b in range(R):
                    e.wait_ge(put[b], 16 * uses(s, b))
                    if first_hop:
                        e.wait_ge(put_run[b], 16 * uses(s, b))
                e.sem_inc(wrote, 1)

            @block.tensor
            def _(e):
                def product(g, b, t):
                    n, o = g * G + t, t % 2
                    e.wait_ge(copied, n + 1)
                    if not (first(g) and n < 2):
                        e.wait_ge(kept, n - 1)
                    for k in range(KC):
                        last = e.matmul(out_ps[o][:, 0:WIDE], hT[o][:, k, :], weight[:, k, :],
                                        start=(k == 0), stop=(k == KC - 1))
                    last.then_inc(multiplied, 1)

                def body(g, b):
                    for t in range(G):
                        n, o = g * G + t, t % 2
                        e.wait_ge(summed, n + 1)
                        if not (first(g) and n < 2):
                            e.wait_ge(copied, n - 1)
                        for k in range(KC):
                            last = e.transpose(hT_ps[o][:, k, :], run[b][:, t, k * P:(k + 1) * P], c.ident[:, :])
                        last.then_inc(turned, 1)
                        late = back(g, b, t, 1)
                        if late is not None:
                            product(*late)

                run_groups(e, s, body)
                behind(s, 1, product)
                e.wait_ge(kept, T)
                last_rows = run[(NG - 1) % R] if first_hop else made[(NG - 1) % R]
                e.matmul(carry_ps[:, 0:MW], tabs["fix"][:, :], last_rows[:, G - 1, :], start=True,
                         stop=True).then_inc(carried, 1)

            @block.scalar
            def _(e):
                def copy_turned(g, b, t):
                    n, o = g * G + t, t % 2
                    e.wait_ge(turned, n + 1)
                    if not (first(g) and n < 2):
                        e.wait_ge(multiplied, n - 1)
                    e.activation(hT[o][:, :, :], hT_ps[o][:, 0:KC, :], ACT.Copy).then_inc(copied, 1)

                def body(g, b):
                    e.activation(factor[b][:, :], cols(tabs["weight"], g), ACT.Copy).then_inc(weight_set, 1)
                    e.wait_ge(weight_set, g + 1)
                    e.wait_ge(got[b], (g - b + R) * (16 * G // R))
                    for t in range(G):
                        e.activation(rows[b][:, t, 0:D], rows[b][:, t, 0:D], ACT.Copy,
                                     scale=factor[b][:, t:t + 1]).then_inc(weighed, 1)
                        late = back(g, b, t, 2)
                        if late is not None:
                            copy_turned(*late)

                run_groups(e, s, body)
                behind(s, 2, copy_turned)

            @block.vector
            def _(e):
                e.memset(run[R - 1][:, G - 1, :], 0.0).then_inc(flagged, 1)

                def keep(g, b, t):
                    n, o = g * G + t, t % 2
                    if t == 0 and not first(g):
                        e.wait_ge(put[b], (g - b) * (16 // R))
                    if t == 0 and not first_hop:
                        e.wait_ge(loaded[b], (g - b + R) * (16 // R))
                    e.wait_ge(multiplied, n + 1)
                    ps, dst = out_ps[o][:, 0:WIDE], made[b][:, t, :]
                    if first_hop:
                        e.tensor_copy(dst, ps).then_inc(kept, 1)
                    else:
                        e.tensor_tensor(out=dst, in0=ps, in1=Q[b][:, t, :], op=ALU.add).then_inc(kept, 1)

                def body(g, b):
                    e.tensor_copy(flag[b][:, :], cols(tabs["same"], g)).then_inc(flagged, 1)
                    e.wait_ge(flagged, g + 2)
                    if first_hop:
                        e.wait_ge(got[b], (g - b + R) * (16 * G // R))
                        e.tensor_copy(cols(next_index, g), rows[b][:, :, D])
                    if not first(g):
                        if first_hop:
                            e.wait_ge(put_run[b], (g - b) * (16 // R))
                        e.wait_ge(turned, (g - R + 1) * G)
                    for t in range(G):
                        e.wait_ge(weighed, g * G + (t + 1))
                        before = run[b][:, t - 1, :] if t else run[(b - 1) % R][:, G - 1, :]
                        if not (isinstance(g, int) and g == 0 and t == 0):
                            e.wait_ge(summed, g * G + t)
                        e.scalar_tensor_tensor(out=run[b][:, t, :], in0=before, scalar=flag[b][:, t:t + 1],
                                               in1=rows[b][:, t, 0:D], op0=ALU.mult, op1=ALU.add
                                               ).then_inc(summed, 1)
                        late = back(g, b, t, LEAD)
                        if late is not None:
                            keep(*late)

                run_groups(e, s, body)
                behind(s, LEAD, keep)
                e.wait_ge(fix_got, 16)
                e.wait_ge(carried, 1)
                e.tensor_tensor(out=fixed[:, :], in0=carry_ps[:, 0:MW], in1=fixed[:, :], op=ALU.add
                                ).then_inc(fix_sum, 1)


def back(g, b, t, lag):
    q = (t - lag) // G
    if isinstance(g, int) and g + q < 0:
        return None
    return (g + q if q else g), (b + q) % R, (t - lag) % G


def behind(s, lag, step):
    for t in range(lag):
        step(*back(s.NG, s.NG % R, t, lag))


def variance(e, chained, stats, small):
    mean2, diff, var = small[:, 0, :], small[:, 1, :], small[:, 2, :]
    chained(e.tensor_tensor(out=mean2, in0=stats[:, :, 1], in1=stats[:, :, 4], op=ALU.add))
    chained(e.tensor_tensor(out=diff, in0=stats[:, :, 1], in1=stats[:, :, 4], op=ALU.subtract))
    chained(e.tensor_tensor(out=var, in0=stats[:, :, 2], in1=stats[:, :, 5], op=ALU.add))
    chained(e.tensor_tensor(out=diff, in0=diff, in1=diff, op=ALU.mult))
    chained(e.scalar_tensor_tensor(out=var, in0=diff, scalar=D / 4.0, in1=var, op0=ALU.mult, op1=ALU.add))
    return e.tensor_scalar(var, var, 1.0 / D, EPS, ALU.mult, ALU.add)


def norm_factors(e, chained, small, scale, shift, dinv):
    chained(e.reciprocal(out=scale[:, :], in_=small[:, 3, :]))
    if dinv is not None:
        chained(e.tensor_tensor(out=scale[:, :], in0=scale[:, :], in1=dinv, op=ALU.mult))
    return e.scalar_tensor_tensor(out=shift[:, :], in0=small[:, 0, :], scalar=-0.5, in1=scale[:, :],
                                  op0=ALU.mult, op1=ALU.mult)


def node_phase(nc, c, name, kind, runs, end, x_in, out, weight, bias=None, y_in=None, ragged=0,
               tables=None, next_end=None, head_sums=None, scores=None):
    s = c.s
    T, NG = s.T, s.NG
    hop = kind == "hop"
    AW = XW = WIDE if hop else D
    OW = WIDE if kind in ("hop", "gcn2") else D
    PW = WIDE if hop else D
    summed_in = kind in ("gin", "gcn1", "gcn2")
    normed_out = kind in ("gin", "gcn2", "hop")
    LEAD, NORM = 3, G + 6

    with ExitStack() as ctx:
        def sb(n, shape, dt):
            return ctx.enter_context(nc.sbuf_tensor(f"{name}_{n}", shape, dt))

        sem = semaphores(nc, ctx, f"{name}")

        def ring(n, shape, dt, k=R):
            return [sb(f"{n}{b}", shape, dt) for b in range(k)]

        index = ring("index", [P, G], I32)
        A, X, O = ring("A", [P, G, AW], F32), ring("X", [P, G, XW], F32), ring("O", [P, G, OW], F32)
        head = ring("head", [P, 3, G, H], F32) if hop else None
        Y = ring("Y", [P, G, D], F32) if kind == "gcn2" else None
        h = ring("h", [P, D], F32, 4) if summed_in else None
        hT = ring("hT", [P, KC, P], F32, 2)
        half = ring("half", [P, D], F32, 2) if kind == "gcn2" else None
        stats = ring("stats", [P, G, 6], F32)
        small = ring("small", [P, 4, G], F32)
        scale, shift = ring("scale", [P, G], F32), ring("shift", [P, G], F32)
        factor = ring("factor", [P, 2, G], F32)
        hT_ps = [ctx.enter_context(nc.psum_tensor(f"{name}_hT_ps{b}", [P, 4, P], F32)) for b in range(2)]
        out_ps = [ctx.enter_context(nc.psum_tensor(f"{name}_out_ps{b}", [P, 512], F32)) for b in range(2)]
        indexed, factored, added, turned, copied, multiplied, summed = (
            sem("indexed"), sem("factored"), sem("added"), sem("turned"), sem("copied"), sem("multiplied"), sem("summed"))
        halved, measured, chain, root_asked, root_done, factors, normed = (
            sem("halved"), sem("measured"), sem("chain"), sem("root_asked"), sem("root_done"),
            sem("factors"), sem("normed"))
        got = [sem(f"got{b}") for b in range(R)]
        loaded = [sem(f"loaded{b}") for b in range(R)]
        put = [sem(f"put{b}") for b in range(R)]
        scored, put_scores = sem("scored"), [sem(f"put_scores{b}") for b in range(R)]
        loads = (48 if ragged else 16) + (16 if Y else 0)

        def in_rows(view, g, full, dst, e, sm):
            if not ragged:
                e.dma_start(dst, tile_rows(view, g)).then_inc(sm, 16)
                return
            top = view[0:(P - 1) * T, :].rearrange("(p t) d -> p t d", t=T)
            rest = view[(P - 1) * T:s.N, :].rearrange("(p t) d -> p t d", p=1)
            e.dma_start(dst[0:112], tile_rows(top, g, 0, 112)).then_inc(sm, 16)
            e.dma_start(dst[112:127], tile_rows(top, g, 112, 127)).then_inc(sm, 16)
            e.dma_start(dst[127:128], tile_rows(rest, g, 0, 1) if full else tile_rows(top, g, 126, 127)
                        ).then_inc(sm, 16)

        with nc.Block() as block:
            @block.gpsimd
            def _(e):
                def body(g, b):
                    if not first(g):
                        e.wait_ge(added if summed_in else summed, (g - R + 1) * G)
                    e.tensor_copy(index[b][:, :], cols(end, g)).then_inc(indexed, 1)
                    e.wait_ge(indexed, g + 1)
                    e.nop(nofuse=True)
                    for t in range(G):
                        gather(e, A[b][:, t, :], runs[:, :], index[b][:, t:t + 1]).then_inc(got[b], 16)

                run_groups(e, s, body)

            @block.sync
            def _(e):
                def load(g, b, full):
                    if not first(g):
                        if kind == "gcn1":
                            e.wait_ge(added, (g - R + 1) * G)
                        elif hop:
                            e.wait_ge(turned, (g - R + 1) * G)
                        else:
                            e.wait_ge(summed, (g - R + 1) * G)
                    in_rows(x_in, g, full, X[b][:, :, :], e, loaded[b])
                    if Y:
                        e.dma_start(Y[b][:, :, :], tile_rows(y_in, g)).then_inc(loaded[b], 16)

                def store(g, b):
                    if hop:
                        e.wait_ge(scored, g + 1)
                        e.dma_start(tile_rows(scores, g), head[b][:, 2, :, :]).then_inc(put_scores[b], 16)
                    e.wait_ge(normed, (g + 1) * G)
                    e.dma_start(tile_rows(out, g), O[b][:, :, 0:D] if hop else O[b][:, :, :]
                                ).then_inc(put[b], 16)

                def body(g, b, full=True):
                    load(g, b, full)
                    late = back(g, b, 0, 3 * G)
                    if late is not None:
                        store(late[0], late[1])

                run_groups(e, s, body, ragged)
                for k in (3, 2, 1):
                    store(NG - k, (NG - k) % R)
                for b in range(R):
                    e.wait_ge(put[b], 16 * uses(s, b))
                    if hop:
                        e.wait_ge(put_scores[b], 16 * uses(s, b))

            @block.tensor
            def _(e):
                def turn(g, b, t):
                    n = g * G + t
                    o = t % 2
                    if summed_in:
                        e.wait_ge(added, n + 1)
                    elif t == 0:
                        e.wait_ge(loaded[b], (g - b + R) * (loads // R))
                    if not (first(g) and n < 2):
                        e.wait_ge(copied, n - 1)
                    src = h[t % 4][:, :] if summed_in else X[b][:, t, :]
                    for k in range(KC):
                        last = e.transpose(hT_ps[o][:, k, :], src[:, k * P:(k + 1) * P], c.ident[:, :])
                    last.then_inc(turned, 1)

                def product(g, b, t):
                    n = g * G + t
                    o = t % 2
                    e.wait_ge(copied, n + 1)
                    if not (first(g) and n < 2):
                        e.wait_ge({"gcn1": normed, "gcn2": halved}.get(kind, summed), n - 1)
                    dst = out_ps[o][:, 0:PW]
                    if bias is not None:
                        e.matmul(dst, c.ones[:, :], bias[:, :], start=True, stop=False)
                    for k in range(KC):
                        last = e.matmul(dst, hT[o][:, k, :], weight[:, k, :],
                                        start=(k == 0 and bias is None), stop=(k == KC - 1))
                    last.then_inc(multiplied, 1)

                def body(g, b):
                    for t in range(G):
                        turn(g, b, t)
                        late = back(g, b, t, 1)
                        if late is not None:
                            product(*late)

                run_groups(e, s, body)
                behind(s, 1, product)

            @block.scalar
            def _(e):
                def norm(g, b, t):
                    n = g * G + t
                    if t == 0:
                        e.wait_ge(factors, g + 1)
                    e.activation(O[b][:, t, 0:D], O[b][:, t, 0:D], ACT.Identity, scale=scale[b][:, t:t + 1],
                                 bias=shift[b][:, t:t + 1]).then_inc(normed, 1)

                def roots(g, b):
                    e.wait_ge(root_asked, g + 1)
                    e.activation(small[b][:, 3, :], small[b][:, 2, :], ACT.Sqrt).then_inc(root_done, 1)

                def halve(g, b, t):
                    n = g * G + t
                    e.wait_ge(multiplied, n + 1)
                    e.wait_ge(factored, g + 1)
                    if not (first(g) and n < 2):
                        e.wait_ge(summed, n - 1)
                    e.activation(half[t % 2][:, :], out_ps[t % 2][:, 0:D], ACT.Copy,
                                 scale=factor[b][:, 0, t:t + 1]).then_inc(halved, 1)

                def rectify(g, b, t):
                    n = g * G + t
                    if t == 0 and not first(g):
                        e.wait_ge(put[b], (g - b) * (16 // R))
                    e.wait_ge(multiplied, n + 1)
                    e.wait_ge(factored, g + 1)
                    e.activation(O[b][:, t, :], out_ps[t % 2][:, 0:D], ACT.Relu,
                                 scale=factor[b][:, 0, t:t + 1]).then_inc(normed, 1)

                def body(g, b):
                    for t in range(G):
                        n = g * G + t
                        o = t % 2
                        e.wait_ge(turned, n + 1)
                        if not (first(g) and n < 2):
                            e.wait_ge(multiplied, n - 1)
                        e.activation(hT[o][:, :, :], hT_ps[o][:, 0:KC, :], ACT.Copy).then_inc(copied, 1)
                        late = back(g, b, t, 2)
                        if late is not None and kind == "gcn1":
                            rectify(*late)
                        if late is not None and kind == "gcn2":
                            halve(*late)
                        if normed_out:
                            late = back(g, b, t, NORM)
                            if late is not None:
                                norm(*late)
                            if t == LEAD + 1 and back(g, b, 0, G) is not None:
                                roots(*back(g, b, 0, G)[:2])

                run_groups(e, s, body)
                if kind in ("gcn1", "gcn2"):
                    behind(s, 2, rectify if kind == "gcn1" else halve)
                if normed_out:
                    for t in range(NORM):
                        if t == LEAD + 1:
                            roots(NG - 1, (NG - 1) % R)
                        norm(*back(NG, NG % R, t, NORM))

            @block.vector
            def _(e):
                def copies(g, b):
                    if kind == "gcn1" and not first(g):
                        e.wait_ge(normed, (g - R + 1) * G)
                    name = {"gin": "dinv", "gcn1": "dinv2", "gcn2": "dinv"}[kind]
                    if kind == "gcn2":
                        e.tensor_copy(factor[b][:, 1, :], cols(tables["root"], g))
                    e.tensor_copy(factor[b][:, 0, :], cols(tables[name], g)).then_inc(factored, 1)

                def add(g, b, t):
                    n = g * G + t
                    if t == 0:
                        e.wait_ge(got[b], (g - b + R) * (16 * G // R))
                        e.wait_ge(loaded[b], (g - b + R) * (loads // R))
                    if not (first(g) and n < 4):
                        e.wait_ge(turned, n - 3)
                    e.tensor_tensor(out=h[t % 4][:, :], in0=A[b][:, t, :], in1=X[b][:, t, :], op=ALU.add
                                    ).then_inc(added, 1)

                def residual(g, b, t):
                    n = g * G + t
                    if t == 0 and not first(g):
                        e.wait_ge(put[b], (g - b) * (16 // R))
                    if t == 0 and hop:
                        e.wait_ge(got[b], (g - b + R) * (16 * G // R))
                    if t == 0 and next_end is not None:
                        e.tensor_copy(O[b][:, :, D:OW], cols(next_end, g).unsqueeze(2).broadcast_to([P, G, H]))
                    e.wait_ge(multiplied, n + 1)
                    ps = out_ps[t % 2][:, 0:PW]
                    if kind == "gcn2":
                        e.wait_ge(halved, n + 1)
                        e.scalar_tensor_tensor(out=O[b][:, t, 0:D], in0=Y[b][:, t, :],
                                               scalar=factor[b][:, 1, t:t + 1], in1=half[t % 2][:, :],
                                               op0=ALU.mult, op1=ALU.add).then_inc(summed, 1)
                    else:
                        e.tensor_tensor(out=O[b][:, t, :], in0=ps, in1=(A if hop else X)[b][:, t, :],
                                        op=ALU.add).then_inc(summed, 1)

                def measure(g, b, t):
                    n = g * G + t
                    e.wait_ge(summed, n + 1)
                    e.bn_stats(out=stats[b][:, t, :], in_=O[b][:, t, 0:D]).then_inc(measured, 1)

                per = 6 if kind == "gcn2" else 7

                def chained_from(g, k):
                    def chained(ins):
                        k[0] += 1
                        ins.then_inc(chain, 1)
                        e.wait_ge(chain, g * per + k[0])
                    return chained

                def ask(g, b):
                    e.wait_ge(measured, (g + 1) * G)
                    variance(e, chained_from(g, [0]), stats[b], small[b]).then_inc(root_asked, 1)

                def finish(g, b):
                    e.wait_ge(root_done, g + 1)
                    norm_factors(e, chained_from(g, [5]), small[b], scale[b], shift[b],
                                 factor[b][:, 0, :] if kind == "gin" else None).then_inc(factors, 1)
                    if hop:
                        e.wait_ge(factors, g + 1)
                        if not first(g):
                            e.wait_ge(put_scores[b], (g - b) * (16 // R))
                        raw, low, high = O[b][:, :, D:WIDE], head[b][:, 0, :, :], head[b][:, 1, :, :]
                        e.tensor_tensor(out=low, in0=raw, in1=scale[b][:, :].unsqueeze(2).broadcast_to([P, G, H]),
                                        op=ALU.mult)
                        chained_from(g, [6])(
                            e.tensor_tensor(out=high, in0=head_sums[:, :].unsqueeze(1).broadcast_to([P, G, H]),
                                            in1=shift[b][:, :].unsqueeze(2).broadcast_to([P, G, H]), op=ALU.mult))
                        e.tensor_tensor(out=head[b][:, 2, :, :], in0=low, in1=high, op=ALU.add).then_inc(scored, 1)

                def body(g, b):
                    if summed_in:
                        copies(g, b)
                    for t in range(G):
                        if summed_in:
                            add(g, b, t)
                        if kind != "gcn1":
                            late = back(g, b, t, LEAD)
                            if late is not None:
                                residual(*late)
                        if normed_out:
                            late = back(g, b, t, LEAD + 1)
                            if late is not None:
                                measure(*late)
                            if back(g, b, 0, G) is not None:
                                if t == LEAD + 1:
                                    ask(*back(g, b, 0, G)[:2])
                                if t == LEAD + 2:
                                    finish(*back(g, b, 0, G)[:2])

                run_groups(e, s, body)
                if kind != "gcn1":
                    for t in range(LEAD + 1):
                        if t < LEAD:
                            residual(*back(NG, NG % R, t, LEAD))
                        if normed_out:
                            measure(*back(NG, NG % R, t, LEAD + 1))
                if normed_out:
                    ask(NG - 1, (NG - 1) % R)
                    finish(NG - 1, (NG - 1) % R)


def degrees(nc, c, tabs):
    with ExitStack() as ctx:
        rooted = semaphores(nc, ctx, "degrees")("rooted")
        block = ctx.enter_context(nc.Block())

        @block.scalar
        def _(e):
            e.activation(tabs["root"][:, :], tabs["degree"][:, :], ACT.Sqrt).then_inc(rooted, 1)

        @block.vector
        def _(e):
            e.reciprocal(out=tabs["dinv2"][:, :], in_=tabs["degree"][:, :])
            e.wait_ge(rooted, 1)
            e.reciprocal(out=tabs["dinv"][:, :], in_=tabs["root"][:, :])


def prepare_weights(nc, c, a, w):
    with ExitStack() as ctx:
        def sb(n, shape, dt):
            return ctx.enter_context(nc.sbuf_tensor(f"prep_{n}", shape, dt))

        sem = semaphores(nc, ctx, "prep")

        HC = a["W1"].shape[1] // P
        w1 = sb("w1", [P, KC, HC * P], F32)
        w2 = sb("w2", [P, HC, D], F32)
        w1T = sb("w1T", [P, HC, D], F32)
        b1, b = sb("b1", [P, HC], F32), sb("b", [P, KC], F32)
        rows = [sb(f"row{j}", [1, WIDE], F32) for j in range(4)]
        hopT = [sb(f"hopT{j}", [P, KC, D], F32) for j in range(3)]
        heads = sb("heads", [P, 2, D], F32)
        mixed = sb("mixed", [P, 2, KC, D], F32)
        turn_ps = [ctx.enter_context(nc.psum_tensor(f"prep_turn_ps{j}", [P, 512], F32)) for j in range(KC)]
        w_ps = [ctx.enter_context(nc.psum_tensor(f"prep_w_ps{j}", [P, 512], F32)) for j in range(KC)]
        b_ps = ctx.enter_context(nc.psum_tensor("prep_b_ps", [P, 512], F32))
        hopT_ps = [ctx.enter_context(nc.psum_tensor(f"prep_hopT_ps{j}", [P, KC, D], F32)) for j in range(2)]
        head_ps = ctx.enter_context(nc.psum_tensor("prep_head_ps", [P, 8, H], F32))
        loaded, turned, copied, multiplied, link, combined = (sem("loaded"), sem("turned"), sem("copied"),
                                                              sem("multiplied"), sem("link"), sem("combined"))
        hop_summed, hop_turned, hop_copied, heads_made, heads_used = (
            sem("hop_summed"), sem("hop_turned"), sem("hop_copied"), sem("heads_made"), sem("heads_used"))
        hops = [w["hop_x"], w["hop_1"], w["hop_2"]]
        LOADS = 14
        block = ctx.enter_context(nc.Block())

        def chunks(m):
            return m.rearrange("(k p) n -> p k n", p=P)

        @block.sync
        def _(e):
            for dst, src in ((w1, a["W1"]), (w2, a["W2"]), (w["gcn1"], a["G1"]), (w["gcn2"], a["G2"]),
                             (w["hop_x"], a["H"][0:D, :]), (w["hop_1"], a["H"][D:2 * D, :]),
                             (w["hop_2"], a["H"][2 * D:3 * D, :]), (w["gat"], a["A"])):
                e.dma_start(dst[:, :, 0:src.shape[1]] if dst is not w2 and dst is not w1 else dst[:, :, :],
                            chunks(src)).then_inc(loaded, 16)
            with nc.allow_non_contiguous_dma(reason="biases of 512 and 256 elements as columns"):
                e.dma_start(b1[:, :], a["b1"].rearrange("(k p) -> p k", p=P)).then_inc(loaded, 16)
                e.dma_start(b[:, :], a["b"].rearrange("(k p) -> p k", p=P)).then_inc(loaded, 16)
            e.dma_start(rows[0][:, 0:D], a["b2"].rearrange("(o d) -> o d", o=1)).then_inc(loaded, 16)
            e.dma_start(rows[1][:, 0:D], a["b"].rearrange("(o d) -> o d", o=1)).then_inc(loaded, 16)
            for j, m in enumerate((a["al"], a["ar"])):
                e.dma_start(heads[:, j, :], m.rearrange("h d -> (h d)").rearrange("(o n) -> o n", o=1)
                            .broadcast_to([P, D])).then_inc(loaded, 16)

        @block.tensor
        def _(e):
            e.wait_ge(loaded, 16 * LOADS)
            for k in range(KC):
                for j in range(HC):
                    last = e.transpose(turn_ps[k][:, j * P:(j + 1) * P], w1[:, k, j * P:(j + 1) * P],
                                       c.ident[:, :])
            last.then_inc(turned, 1)
            e.wait_ge(copied, 1)
            for k in range(KC):
                for j in range(HC):
                    e.matmul(w_ps[k][:, 0:D], w1T[:, j, k * P:(k + 1) * P], w2[:, j, :],
                             start=(j == 0), stop=(j == HC - 1))
            for j in range(HC):
                last = e.matmul(b_ps[0:1, 0:D], b1[:, j:j + 1], w2[:, j, :], start=(j == 0),
                                stop=(j == HC - 1))
            last.then_inc(multiplied, 1)
            e.wait_ge(hop_summed, 1)
            for m in range(3):
                if m == 2:
                    e.wait_ge(hop_copied, 1)
                for k in range(KC):
                    for j in range(KC):
                        last = e.transpose(hopT_ps[m % 2][:, j, k * P:(k + 1) * P],
                                           hops[m][:, k, j * P:(j + 1) * P], c.ident[:, :])
                last.then_inc(hop_turned, 1)
            e.wait_ge(hop_copied, 3)
            for j in range(3 * KC + 2):
                for k in range(KC):
                    if j < 3 * KC:
                        lhsT, to = hopT[j // KC][:, k, (j % KC) * P:(j % KC + 1) * P], head_ps[:, j, :]
                    elif j == 3 * KC:
                        lhsT, to = b[:, k:k + 1], head_ps[0:1, j, :]
                    else:
                        lhsT, to = c.onesT[:, 0:P], head_ps[:, j, :]
                    last = e.matmul(to, lhsT, w["left"][:, k, :], start=(k == 0), stop=(k == KC - 1))
            last.then_inc(heads_made, 1)

        @block.vector
        def _(e):
            n = [0]

            def then(ins):
                n[0] += 1
                ins.then_inc(link, 1)
                e.wait_ge(link, n[0])

            e.memset(w["bias_gin"][:, :], 0.0)
            then(e.memset(w["bias_hop"][:, :], 0.0))
            e.wait_ge(turned, 1)
            for k in range(KC):
                last = e.tensor_copy(w1T[:, :, k * P:(k + 1) * P],
                                     turn_ps[k][:, :].rearrange("p (j m) -> p j m", j=HC))
            last.then_inc(copied, 1)
            for k in range(KC):
                e.tensor_tensor(out=w["hop_x"][:, k, k * P:(k + 1) * P], in0=w["hop_x"][:, k, k * P:(k + 1) * P],
                                in1=c.ident[:, :], op=ALU.add)
            for j, dst in ((0, w["left"][:, :, :]), (1, w["gat"][:, :, D:WIDE])):
                for k in range(KC):
                    then(e.tensor_tensor(out=mixed[:, j, k, :], in0=w["gat"][:, k, 0:D], in1=heads[:, j, :],
                                         op=ALU.mult))
                    then(e.tensor_reduce(out=dst[:, k, :],
                                         in_=mixed[:, j, k, :].rearrange("p (h d) -> p h d", h=H),
                                         axis=AX.X, op=ALU.add))
            e.sem_inc(hop_summed, 1)
            for m in range(3):
                e.wait_ge(hop_turned, m + 1)
                e.tensor_copy(hopT[m][:, :, :], hopT_ps[m % 2][:, :, :]).then_inc(hop_copied, 1)
            e.wait_ge(heads_made, 1)
            for m in range(3):
                e.tensor_copy(hops[m][:, :, D:WIDE], head_ps[:, m * KC:(m + 1) * KC, :])
            e.tensor_copy(w["head_sums"][:, :], head_ps[:, 3 * KC + 1, :])
            e.memset(rows[0][:, D:WIDE], 0.0)
            then(e.tensor_copy(rows[1][:, D:WIDE], head_ps[0:1, 3 * KC, :]))
            e.wait_ge(multiplied, 1)
            for k in range(KC):
                e.tensor_copy(w["gin"][:, k, :], w_ps[k][:, 0:D])
            then(e.tensor_tensor(out=rows[0][:, 0:D], in0=b_ps[0:1, 0:D], in1=rows[0][:, 0:D], op=ALU.add))
            for row, dst in ((rows[0], w["bias_gin"]), (rows[1], w["bias_hop"])):
                left = row
                for part, rest in ((0, rows[2]), (32, rows[3]), (64, None)):
                    n_cols = dst.shape[1]
                    then(e.tensor_copy(dst[part:part + 1, :], left[:, 0:n_cols]))
                    if rest is not None:
                        then(e.tensor_tensor(out=rest[:, 0:n_cols], in0=left[:, 0:n_cols],
                                             in1=dst[part:part + 1, :], op=ALU.subtract))
                        left = rest


def gat_phase(nc, c, x_rows, x_view, scores, left_end, right_end, weight, out, spill):
    s = c.s
    T, NG = s.T, s.NG
    DH = D // H
    with ExitStack() as ctx:
        def sb(n, shape, dt):
            return ctx.enter_context(nc.sbuf_tensor(f"gat_{n}", shape, dt))

        sem = semaphores(nc, ctx, "gat")

        def ring(n, shape, dt, k=R):
            return [sb(f"{n}{b}", shape, dt) for b in range(k)]

        index = ring("index", [P, 2, G], I32)
        A, X, O = ring("A", [P, G, D], F32), ring("X", [P, G, D], F32), ring("O", [P, G, D], F32)
        L = ring("L", [P, G, H], F32)
        XT = ring("XT", [P, G, WIDE], F32, 2)
        hT = ring("hT", [P, KC, P], F32, 2)
        score = ring("score", [P, 3, G, H], F32, 2)
        top = ring("top", [P, 3, G], F32, 2)
        prod = sb("prod", [P, G, D], F32)
        mix = sb("mix", [P, G, DH], F32)
        stats = ring("stats", [P, G, 6], F32)
        small = ring("small", [P, 4, G], F32)
        scale, shift = ring("scale", [P, G], F32), ring("shift", [P, G], F32)
        hT_ps = [ctx.enter_context(nc.psum_tensor(f"gat_hT_ps{b}", [P, 4, P], F32)) for b in range(2)]
        out_ps = [ctx.enter_context(nc.psum_tensor(f"gat_out_ps{b}", [P, 512], F32)) for b in range(2)]
        indexed, turned, copied, multiplied, kept = (sem("indexed"), sem("turned"), sem("copied"),
                                                     sem("multiplied"), sem("kept"))
        chain, exp_asked, exp_done, added, measured, root_asked, root_done, factors, normed = (
            sem("chain"), sem("exp_asked"), sem("exp_done"), sem("added"), sem("measured"),
            sem("root_asked"), sem("root_done"), sem("factors"), sem("normed"))
        got = [sem(f"got{b}") for b in range(R)]
        loaded = [sem(f"loaded{b}") for b in range(R)]
        put = [sem(f"put{b}") for b in range(R)]
        NORM = 2 * G + 4
        WAITS = 2 * 16 * G
        out_top = out[0:(P - 1) * T, :].rearrange("(p t) d -> p t d", t=T)
        out_rest = out[(P - 1) * T:s.N, :].rearrange("(p t) d -> p t d", p=1)
        spill_view = spill[:, :].rearrange("(p t) d -> p t d", p=1)

        with nc.Block() as block:
            @block.gpsimd
            def _(e):
                def body(g, b):
                    if not first(g):
                        e.wait_ge(turned, (g - R + 1) * G)
                        e.wait_ge(exp_asked, g - R + 1)
                    e.tensor_copy(index[b][:, 0, :], cols(right_end, g))
                    e.tensor_copy(index[b][:, 1, :], cols(left_end, g)).then_inc(indexed, 1)
                    e.wait_ge(indexed, g + 1)
                    e.nop(nofuse=True)
                    for t in range(G):
                        gather(e, A[b][:, t, :], x_rows[:, :], index[b][:, 0, t:t + 1]).then_inc(got[b], 16)
                        gather(e, L[b][:, t, :], scores[:, :], index[b][:, 1, t:t + 1]).then_inc(got[b], 16)

                run_groups(e, s, body)

            @block.sync
            def _(e):
                def store(g, b, full):
                    e.wait_ge(normed, (g + 1) * G)
                    e.dma_start(tile_rows(out_top, g, 0, 112), O[b][0:112]).then_inc(put[b], 16)
                    e.dma_start(tile_rows(out_top, g, 112, 127), O[b][112:127]).then_inc(put[b], 16)
                    e.dma_start(tile_rows(out_rest if full else spill_view, g, 0, 1), O[b][127:128]
                                ).then_inc(put[b], 16)

                def body(g, b, full):
                    if not first(g):
                        e.wait_ge(added, g - R + 1)
                    e.dma_start(X[b][:, :, :], tile_rows(x_view, g)).then_inc(loaded[b], 16)
                    late = back(g, b, 0, 4 * G)
                    if late is not None:
                        store(late[0], late[1], late[0] < s.full if isinstance(late[0], int) else full)

                run_groups(e, s, body, 2)
                for k in (4, 3, 2, 1):
                    store(NG - k, (NG - k) % R, False)
                for b in range(R):
                    e.wait_ge(put[b], 48 * uses(s, b))

            @block.tensor
            def _(e):
                def product(g, b, t):
                    n = g * G + t
                    e.wait_ge(copied, n + 1)
                    if not (first(g) and n < 2):
                        e.wait_ge(kept, n - 1)
                    for k in range(KC):
                        last = e.matmul(out_ps[t % 2][:, 0:WIDE], hT[t % 2][:, k, :], weight[:, k, :],
                                        start=(k == 0), stop=(k == KC - 1))
                    last.then_inc(multiplied, 1)

                def body(g, b):
                    e.wait_ge(got[b], (g - b + R) * (WAITS // R))
                    for t in range(G):
                        n = g * G + t
                        if not (first(g) and n < 2):
                            e.wait_ge(copied, n - 1)
                        for k in range(KC):
                            last = e.transpose(hT_ps[t % 2][:, k, :], A[b][:, t, k * P:(k + 1) * P],
                                               c.ident[:, :])
                        last.then_inc(turned, 1)
                        late = back(g, b, t, 1)
                        if late is not None:
                            product(*late)

                run_groups(e, s, body)
                behind(s, 1, product)

            @block.scalar
            def _(e):
                def keep(g, b, t):
                    n = g * G + t
                    if t == 0 and not (isinstance(g, int) and g < 2):
                        e.wait_ge(added, g - 1)
                    e.wait_ge(multiplied, n + 1)
                    e.activation(XT[b % 2][:, t, :], out_ps[t % 2][:, 0:WIDE], ACT.Copy).then_inc(kept, 1)

                def roots(g, b):
                    e.wait_ge(root_asked, g + 1)
                    e.activation(small[b][:, 3, :], small[b][:, 2, :], ACT.Sqrt).then_inc(root_done, 1)

                def exponents(g, b):
                    e.wait_ge(exp_asked, g + 1)
                    e.activation(score[b % 2][:, 2, :, :], score[b % 2][:, 1, :, :], ACT.Exp
                                 ).then_inc(exp_done, 1)

                def norm(g, b, t):
                    if t == 0:
                        e.wait_ge(factors, g + 1)
                    e.activation(O[b][:, t, :], O[b][:, t, :], ACT.Identity, scale=scale[b][:, t:t + 1],
                                 bias=shift[b][:, t:t + 1]).then_inc(normed, 1)

                def body(g, b):
                    for t in range(G):
                        n = g * G + t
                        e.wait_ge(turned, n + 1)
                        if not (first(g) and n < 2):
                            e.wait_ge(multiplied, n - 1)
                        e.activation(hT[t % 2][:, :, :], hT_ps[t % 2][:, 0:KC, :], ACT.Copy).then_inc(copied, 1)
                        late = back(g, b, t, 2)
                        if late is not None:
                            keep(*late)
                        if t == 2 and back(g, b, 0, 2 * G) is not None:
                            roots(*back(g, b, 0, 2 * G)[:2])
                        if t == 3 and back(g, b, 0, G) is not None:
                            exponents(*back(g, b, 0, G)[:2])
                        late = back(g, b, t, NORM)
                        if late is not None:
                            norm(*late)

                run_groups(e, s, body)
                behind(s, 2, keep)
                for t in range(2):
                    norm(*back(NG, NG % R, t, NORM))
                roots(NG - 2, (NG - 2) % R)
                exponents(NG - 1, (NG - 1) % R)
                for t in range(2, NORM):
                    if t == G + 4:
                        roots(NG - 1, (NG - 1) % R)
                    norm(*back(NG, NG % R, t, NORM))

            @block.vector
            def _(e):
                PER = 14

                def chained_from(g, k):
                    def chained(ins):
                        k[0] += 1
                        ins.then_inc(chain, 1)
                        e.wait_ge(chain, g * PER + k[0])
                    return chained

                def finish(g, b):
                    e.wait_ge(root_done, g + 1)
                    norm_factors(e, chained_from(g, [PER - 1]), small[b], scale[b], shift[b], None
                                 ).then_inc(factors, 1)

                def attend(g, b):
                    chained = chained_from(g, [0])
                    raw, low, high = (score[b % 2][:, j, :, :] for j in range(3))
                    best, total, inverse = (top[b % 2][:, j, :] for j in range(3))
                    e.wait_ge(kept, (g + 1) * G)
                    e.wait_ge(got[b], (g - b + R) * (WAITS // R))
                    chained(e.tensor_tensor(out=raw, in0=XT[b % 2][:, :, D:WIDE], in1=L[b][:, :, :], op=ALU.add))
                    chained(e.scalar_tensor_tensor(out=raw, in0=raw, scalar=0.01, in1=raw, op0=ALU.mult,
                                                   op1=ALU.max))
                    chained(e.tensor_reduce(out=best, in_=raw, axis=AX.X, op=ALU.max))
                    e.tensor_tensor(out=low, in0=raw, in1=best.unsqueeze(2).broadcast_to([P, G, H]),
                                    op=ALU.subtract).then_inc(exp_asked, 1)
                    e.wait_ge(exp_done, g + 1)
                    chained(e.tensor_reduce(out=total, in_=high, axis=AX.X, op=ALU.add))
                    chained(e.reciprocal(out=inverse, in_=total))
                    chained(e.tensor_tensor(out=low, in0=high, in1=inverse.unsqueeze(2).broadcast_to([P, G, H]),
                                            op=ALU.mult))
                    for t in range(G):
                        ins = e.tensor_tensor(out=prod[:, t, :].rearrange("p (h d) -> p h d", h=H),
                                              in0=XT[b % 2][:, t, 0:D].rearrange("p (h d) -> p h d", h=H),
                                              in1=low[:, t, :].unsqueeze(2).broadcast_to([P, H, DH]), op=ALU.mult)
                    chained(ins)
                    chained(e.tensor_reduce(out=mix[:, :, :], in_=prod[:, :, :].rearrange("p g (h d) -> p g d h", h=H),
                                            axis=AX.X, op=ALU.add))
                    e.wait_ge(loaded[b], (g - b + R) * (16 // R))
                    if not first(g):
                        e.wait_ge(put[b], (g - b) * (48 // R))
                    e.tensor_tensor(out=O[b][:, :, :].rearrange("p g (h d) -> p g h d", h=H),
                                    in0=X[b][:, :, :].rearrange("p g (h d) -> p g h d", h=H),
                                    in1=mix[:, :, :].unsqueeze(2).broadcast_to([P, G, H, DH]), op=ALU.add
                                    ).then_inc(added, 1)
                    e.wait_ge(added, g + 1)
                    for t in range(G):
                        e.bn_stats(out=stats[b][:, t, :], in_=O[b][:, t, :]).then_inc(measured, 1)
                    e.wait_ge(measured, (g + 1) * G)
                    variance(e, chained_from(g, [8]), stats[b], small[b]).then_inc(root_asked, 1)

                def body(g, b):
                    if back(g, b, 0, 2 * G) is not None:
                        finish(*back(g, b, 0, 2 * G)[:2])
                    if back(g, b, 0, G) is not None:
                        attend(*back(g, b, 0, G)[:2])

                run_groups(e, s, body)
                finish(NG - 2, (NG - 2) % R)
                attend(NG - 1, (NG - 1) % R)
                finish(NG - 1, (NG - 1) % R)


def gnn_stack(nc, a, out):
    s = Shape(a["x"].shape[0])
    T = s.T

    def dram(name, shape):
        return nc.dram_tensor(name, shape, F32).ap()

    with ExitStack() as ctx:
        c = Core(nc, s, ctx)
        runs = dram("runs", (s.NP + 1, D))
        sorted_src, sorted_dst = dram("sorted_src", (s.NP, 4)), dram("sorted_dst", (s.NP, 4))
        z1, z2, x3 = (dram(n, (s.NP, D)) for n in ("z1", "z2", "x3"))
        x2, hop1, hops = dram("x2", (s.NP, WIDE)), dram("hop1", (s.NP, WIDE)), dram("hops", (s.NP + 1, WIDE))
        scores = dram("scores", (s.NP, H))
        spill = dram("spill", (T, D))

        def tiled(rows):
            return rows[0:s.NP, :].rearrange("(p t) d -> p t d", t=T)

        def table(name, dt, shape=None):
            return c.sb(name, shape or [P, T], dt)

        unsorted = table("unsorted", I32, [P, 1])
        by_src = {"unsorted": unsorted, "end": table("src_end", I32), "other": table("src_other", I32),
                  "weight": table("src_weight", F32), "same": table("src_same", F32),
                  "fix_row": table("src_fix_row", I32, [P, 1]), "fix": table("src_fix", F32, [P, P])}
        by_dst = {"unsorted": unsorted, "end": table("dst_end", I32), "other": table("dst_other", I32),
                  "same": table("dst_same", F32), "degree": table("degree", F32),
                  "root": table("root", F32), "dinv": table("dinv", F32), "dinv2": table("dinv2", F32),
                  "fix_row": table("dst_fix_row", I32, [P, 1]), "fix": table("dst_fix", F32, [P, P])}
        edge_src, edge_dst = table("edge_src", I32), table("edge_dst", I32)
        hop_index = table("hop_index", I32)
        w = {n: c.sb(f"w_{n}", [P, KC, D], F32) for n in ("gin", "gcn1", "gcn2")}
        w.update({n: c.sb(f"w_{n}", [P, KC, WIDE], F32) for n in ("hop_x", "hop_1", "hop_2", "gat")})
        w["left"], w["head_sums"] = c.sb("w_left", [P, KC, H], F32), c.sb("head_sums", [P, H], F32)
        w["bias_gin"], w["bias_hop"] = c.sb("bias_gin", [P, D], BF16), c.sb("bias_hop", [P, WIDE], BF16)

        constants(nc, c, runs, hops)
        prepare_weights(nc, c, a, w)
        sort_edges(nc, c, "src", a["src"], a["dst"], a["edge_weight"], sorted_src, by_src, edge_src, edge_dst)
        sorted_tables(nc, c, "src", sorted_src, by_src)
        edge_phase(nc, c, "gin_e", a["x"], by_src, runs)
        sort_edges(nc, c, "dst", a["dst"], a["src"], None, sorted_dst, by_dst)
        sorted_tables(nc, c, "dst", sorted_dst, by_dst)
        degrees(nc, c, by_dst)
        node_phase(nc, c, "gin_n", "gin", runs, by_src["end"], a["x"], tiled(z1), w["gin"],
                   bias=w["bias_gin"], ragged=1, tables=by_dst)
        edge_phase(nc, c, "gcn1_e", z1, by_dst, runs)
        node_phase(nc, c, "gcn1_n", "gcn1", runs, by_dst["end"], tiled(z1), tiled(z2), w["gcn1"],
                   tables=by_dst)
        edge_phase(nc, c, "gcn2_e", z2, by_dst, runs)
        node_phase(nc, c, "gcn2_n", "gcn2", runs, by_dst["end"], tiled(z2), tiled(x2), w["gcn2"],
                   y_in=tiled(z1), tables=by_dst, next_end=by_src["end"])
        hop_phase(nc, c, "hop1_e", x2, by_src["other"], by_src, w["hop_1"], hop1, runs=runs, next_index=hop_index)
        hop_phase(nc, c, "hop2_e", runs, hop_index, by_src, w["hop_2"], hops, passed=hop1)
        node_phase(nc, c, "hop_n", "hop", hops, by_src["end"], tiled(x2), tiled(x3), w["hop_x"],
                   bias=w["bias_hop"], head_sums=w["head_sums"], scores=tiled(scores))
        gat_phase(nc, c, x3, tiled(x3), scores, edge_src, edge_dst, w["gat"], out, spill)


INPUTS = {"x": "x", "src": "src", "dst": "dst", "edge_weight": "edge_weight", "W1": "L0_gnn_W1",
          "b1": "L0_gnn_b1", "W2": "L0_gnn_W2", "b2": "L0_gnn_b2", "G1": "L1_gnn_W1", "G2": "L1_gnn_W2",
          "H": "L2_gnn_W", "b": "L2_gnn_b", "A": "L3_gnn_weight", "al": "L3_gnn_attn_l",
          "ar": "L3_gnn_attn_r"}


def kernel(**inputs):
    import concourse.bacc as bacc
    from concourse.bass_utils import run_bass_kernel_spmd

    nc = bacc.Bacc("TRN2", target_bir_lowering=False, num_devices=1)
    arrays, aps = {}, {}
    for short, name in INPUTS.items():
        v = np.ascontiguousarray(inputs[name])
        arrays[f"in_{name}"] = v
        aps[short] = nc.dram_tensor(f"in_{name}", v.shape, mybir.dt.from_np(v.dtype), kind="ExternalInput").ap()
    out = nc.dram_tensor("out_x", inputs["x"].shape, F32, kind="ExternalOutput").ap()
    gnn_stack(nc, aps, out)
    r = run_bass_kernel_spmd(nc, [arrays], core_ids=[0])
    return r.results[0]["out_x"]
```

```python
from contextlib import ExitStack

import numpy as np
import concourse.bass as bass
from concourse import mybir

F32 = mybir.dt.float32
F16 = mybir.dt.float16
BF16 = mybir.dt.bfloat16
I32 = mybir.dt.int32
ALU = mybir.AluOpType
ACT = mybir.ActivationFunctionType
AX = mybir.AxisListType
P = 128
D = 256
KC = D // P
H = 4
WIDE = D + H
G = 8
R = 4
Q = 2
EPS = 1e-5
ROUND = float(3 << 22)


class Shape:

    def __init__(self, n):
        self.N = n
        self.T = -(-n // (P * G)) * G
        self.NP = P * self.T
        self.NG = self.T // G
        self.last = n - (P - 1) * self.T
        self.full = self.last // G
        assert self.last == self.full * G and self.full % R == R - 1 and self.full >= 2 * R
        assert self.NG % R == 1 and self.NG > self.full + 2 * R


def run_groups(e, s, body, ragged=0):
    args = (lambda g: (g, g % R, g < s.full)) if ragged else (lambda g: (g, g % R))
    for g in range(R):
        body(*args(g))
    if ragged:
        turn = (s.full + 1) // R
        with e.Fori(1, turn - 1) as i:
            for b in range(R):
                body(i * R + b, b, True)
        for g in range((turn - 1) * R, (turn + ragged - 1) * R):
            body(*args(g))
        with e.Fori(turn + ragged - 1, s.NG // R) as i:
            for b in range(R):
                body(i * R + b, b, False)
    else:
        with e.Fori(1, s.NG // R) as i:
            for b in range(R):
                body(i * R + b, b)
    body(*args(s.NG - 1))


def first(g):
    return isinstance(g, int) and g < R


def later(g):
    return not (isinstance(g, int) and g == 0)


def uses(s, b):
    return (s.NG - 1 - b) // R + 1


def copy_ahead(s, g, b, copies):
    if isinstance(g, int):
        for k in ((0, 1, 2) if g == 0 else (2,)):
            if g + k < s.NG:
                copies(g + k, (b + k) % R)
    else:
        copies(g + 2, (b + 2) % R)


def cols(table, g):
    return table[:, bass.ds(g * G, G)] if not isinstance(g, int) else table[:, g * G:(g + 1) * G]


def tile_rows(view, g, lo=0, hi=P):
    return view[lo:hi, g * G:(g + 1) * G, :] if isinstance(g, int) else view[lo:hi, bass.ds(g * G, G), :]


def semaphores(nc, ctx, name):
    taken = []

    def sem(n):
        taken.append(nc.alloc_semaphore(f"{name}_{n}"))
        return taken[-1]

    def give_back():
        nc.clear_and_free_semaphores(taken)
        nc.all_engine_barrier()

    ctx.callback(give_back)
    return sem


def got_semaphores(sem):
    return [[sem(f"got{b}_{q}") for q in range(G // Q)] for b in range(R)]


def wait_rows(e, got, g, b, t, per_tile=1):
    if t % Q == 0:
        e.wait_ge(got[b][t // Q], (g - b + R) * (16 * Q * per_tile // R))


def wait_group(e, got, g, b, per_tile=1):
    for t in range(0, G, Q):
        wait_rows(e, got, g, b, t, per_tile)


def wait_free(e, got, g, b, per_tile=1):
    for q in range(G // Q):
        e.wait_ge(got[b][q], (g - b) * (16 * Q * per_tile // R))


def gather(e, out, table, index):
    return e.indirect_dma_start(out=out, out_offset=None, in_=table,
                                in_offset=bass.IndirectOffsetOnAxis(ap=index, axis=0))


class Core:

    def __init__(self, nc, s, ctx):
        self.nc, self.s, self.ctx = nc, s, ctx
        T = s.T
        sb = self.sb
        self.iota_free = sb("iota_free", [P, T], F16)
        self.iota_part = sb("iota_part", [P, 1], F32)
        self.node_f = sb("node_f", [P, T], F32)
        self.lower = sb("lower", [P, P], F32)
        self.before = sb("before", [P, P], F32)
        self.ident = sb("ident", [P, P], F32)
        self.identh = sb("identh", [P, P], F16)
        self.ones = sb("ones", [P, P], BF16)
        self.onesT = sb("onesT", [P, T], F32)
        self.zero_row = sb("zero_row", [1, D], F32)

    def sb(self, name, shape, dt):
        return self.ctx.enter_context(self.nc.sbuf_tensor(name, shape, dt))


def constants(nc, c, runs, tables):
    s = c.s
    with ExitStack() as ctx:
        sem = semaphores(nc, ctx, "consts")
        num = ctx.enter_context(nc.sbuf_tensor("num", [P, s.T], I32))
        num2 = ctx.enter_context(nc.sbuf_tensor("num2", [P, s.T], I32))
        part = ctx.enter_context(nc.sbuf_tensor("part_no", [P, 1], I32))
        iotas = sem("iotas")
        blank = sem("blank")
        done = sem("consts_done")
        zeroed = sem("zeroed")
        zero_put = sem("zero_put")
        block = ctx.enter_context(nc.Block())

        @block.gpsimd
        def _(e):
            e.iota(num[:, :], pattern=[[1, s.T]], base=0, channel_multiplier=s.T)
            e.iota(num2[:, :], pattern=[[1, s.T]], base=0, channel_multiplier=0)
            e.iota(part[:, :], pattern=[[1, 1]], base=0, channel_multiplier=1).then_inc(iotas, 1)
            e.memset(c.lower[:, :], 1.0).then_inc(blank, 1)
            e.memset(c.before[:, :], 1.0).then_inc(blank, 1)
            e.memset(c.ident[:, :], 0.0).then_inc(blank, 1)
            e.wait_ge(blank, 3)
            e.affine_select(out=c.lower[:, :], in_=c.lower[:, :], compare_op=ALU.is_gt, fill=0.0,
                            base=0, pattern=[[1, P]], channel_multiplier=-1)
            e.affine_select(out=c.before[:, :], in_=c.before[:, :], compare_op=ALU.is_gt, fill=0.0,
                            base=0, pattern=[[-1, P]], channel_multiplier=1)
            e.affine_select(out=c.ident[:, :], in_=c.ident[:, :], compare_op=ALU.not_equal, fill=1.0,
                            base=0, pattern=[[-1, P]], channel_multiplier=1).then_inc(done, 1)

        @block.vector
        def _(e):
            e.memset(c.ones[:, :], 1.0)
            e.memset(c.onesT[:, :], 1.0)
            for table in tables:
                e.memset(table[:, s.T:], 0)
            e.memset(c.zero_row[:, :], 0.0).then_inc(zeroed, 1)
            e.wait_ge(iotas, 1)
            e.tensor_copy(c.node_f[:, :], num[:, :])
            e.tensor_copy(c.iota_free[:, :], num2[:, :])
            e.tensor_copy(c.iota_part[:, :], part[:, :])
            e.wait_ge(done, 1)
            e.tensor_copy(c.identh[:, :], c.ident[:, :])


        @block.sync
        def _(e):
            e.wait_ge(zeroed, 1)
            e.dma_start(runs[s.NP:s.NP + 1, :], c.zero_row[0:1, :]).then_inc(zero_put, 16)
            e.wait_ge(zero_put, 16)


class EdgeSort:

    def __init__(self, nc, c, name, tabs, rec_dram, ctx):
        self.nc, self.c, self.s, self.tabs, self.rec_dram = nc, c, c.s, tabs, rec_dram
        T = c.s.T
        self.sem = semaphores(nc, ctx, name)

        def sb(n, shape, dt):
            return ctx.enter_context(nc.sbuf_tensor(f"{name}_{n}", shape, dt))

        def bank(n, width=512, dt=F32):
            return ctx.enter_context(nc.psum_tensor(f"{name}_{n}", [P, width], dt))

        self.key_i, self.other_i = sb("key_i", [P, T], I32), sb("other_i", [P, T], I32)
        self.next_i = sb("next_i", [P, T], I32)
        self.falls = sb("falls", [P, 1], F32)
        self.key_f = sb("key_f", [P, T], F32)
        self.hi, self.lo, self.tmp = sb("hi", [P, T], F32), sb("lo", [P, T], F32), sb("tmp", [P, T], F32)
        self.rec = sb("rec", [P, T, 4], F32)
        self.lh = [sb(f"lh{b}", [P, G, 3], F32) for b in range(R)]
        self.hot_hi = [sb(f"hot_hi{b}", [P, P], F16) for b in range(G)]
        self.hot_lo = [sb(f"hot_lo{b}", [P, T], F16) for b in range(G)]
        self.count = [sb(f"count{b}", [P, T], F32) for b in range(4)]
        self.offset, self.prod = sb("offset", [P, T], F32), sb("prod", [P, T], F32)
        self.row_sum = sb("row_sum", [P, 1], F32)
        self.hist_ps = bank("hist")
        self.at_ps = [bank(f"at{b}") for b in range(2)]
        self.name, self.sb, self.bank = name, sb, bank
        sem = self.sem
        self.first_hot, self.counted, self.hist_done, self.base_done, self.link, self.lh_ready = (
            sem("first_hot"), sem("counted"), sem("hist_done"), sem("base_done"), sem("prefix_link"), sem("lh_ready"))

    def split(self, key_dram, other_dram, weight_dram=None, key_kept=None, other_kept=None):
        nc, c, s, sem = self.nc, self.c, self.s, self.sem
        T = s.T
        key_i, other_i, next_i, falls, key_f = self.key_i, self.other_i, self.next_i, self.falls, self.key_f
        hi, lo, tmp, rec = self.hi, self.lo, self.tmp, self.rec
        own, loaded, link = sem("own"), sem("loaded"), sem("link")
        with nc.Block() as block:
            @block.vector
            def _(e):
                n = [0]

                def then(ins):
                    n[0] += 1
                    ins.then_inc(link, 1)
                    e.wait_ge(link, n[0])

                e.tensor_copy(key_i[:, :], c.node_f[:, :])
                e.memset(rec[:, :, :], 0.0)
                e.memset(tmp[:, :], 0.0)
                e.tensor_scalar(next_i[:, :], c.node_f[:, :], 1.0, None, ALU.add)
                then(e.memset(other_i[:, :], 0))
                e.sem_inc(own, 1)
                e.wait_ge(loaded, 16 * (12 if weight_dram is not None else 9))
                then(e.tensor_tensor(out=lo[:, :], in0=key_i[:, :], in1=next_i[:, :], op=ALU.is_gt))
                then(e.tensor_reduce(out=falls[:, :], in_=lo[:, :], axis=AX.X, op=ALU.add))
                e.tensor_copy(key_f[:, :], key_i[:, :]).then_inc(link, 1)
                n[0] += 1
                then(e.tensor_copy(rec[:, :, 1], other_i[:, :]))
                then(e.tensor_copy(rec[:, :, 2], tmp[:, :]))
                if key_kept is not None:
                    e.tensor_copy(key_kept[:, 0:T], key_i[:, :])
                    e.tensor_copy(other_kept[:, 0:T], other_i[:, :])
                then(e.tensor_scalar(tmp[:, :], key_f[:, :], (T - 1) / 2, 1.0 / T,
                                     ALU.subtract, ALU.mult))
                then(e.tensor_scalar(hi[:, :], tmp[:, :], ROUND, ROUND, ALU.add, ALU.subtract))
                e.scalar_tensor_tensor(out=lo[:, :], in0=hi[:, :], scalar=-float(T), in1=key_f[:, :],
                                       op0=ALU.mult, op1=ALU.add)
                e.tensor_copy(rec[:, :, 0], key_f[:, :])

            @block.sync
            def _(e):
                e.wait_ge(own, 1)
                pieces = [(key_dram, key_i, 0), (key_dram, next_i, 1), (other_dram, other_i, 0)]
                if weight_dram is not None:
                    pieces.append((weight_dram, tmp, 0))
                cut = (P - 1) * T
                for src, dst, ahead in pieces:
                    body = src[ahead:cut + ahead].rearrange("(p t) -> p t", t=T)
                    e.dma_start(dst[0:112, :], body[0:112, :]).then_inc(loaded, 16)
                    e.dma_start(dst[112:127, :], body[112:127, :]).then_inc(loaded, 16)
                    e.dma_start(dst[127:128, 0:s.last - ahead],
                                src[cut + ahead:s.N].rearrange("(a t) -> a t", a=1)).then_inc(loaded, 16)

    def hot_group(self, e, g, b):
        if not first(g):
            e.wait_ge(self.first_hot, (g - R + 1) * G)
        e.tensor_copy(self.lh[b][:, :, 0], cols(self.hi, g))
        e.tensor_copy(self.lh[b][:, :, 1], cols(self.lo, g)).then_inc(self.lh_ready, 1)
        e.wait_ge(self.lh_ready, g + 1)

    def hot_tile(self, e, g, b, t):
        if later(g):
            e.wait_ge(self.counted, g * G + (t + 1 - G))
        e.tensor_scalar(self.hot_hi[t][:, :], self.c.iota_free[:, 0:P], self.lh[b][:, t, 0:1], None, ALU.is_equal)
        e.tensor_scalar(self.hot_lo[t][:, :], self.c.iota_free[:, :], self.lh[b][:, t, 1:2], None,
                        ALU.is_equal).then_inc(self.first_hot, 1)

    def count_group(self, e, g, b):
        for t in range(G):
            e.wait_ge(self.first_hot, g * G + (t + 1))
            e.matmul(self.hist_ps[:, 0:self.s.T], self.hot_hi[t][:, :], self.hot_lo[t][:, :],
                     start=(first(g) and g == 0 and t == 0),
                     stop=(isinstance(g, int) and g == self.s.NG - 1 and t == G - 1),
                     skip_group_check=True).then_inc(self.counted, 1)

    def prefix(self, e):
        s, tabs, count, offset, prod, tmp = self.s, self.tabs, self.count, self.offset, self.prod, self.tmp
        row_sum, falls = self.row_sum, self.falls
        T = s.T
        n = [0]

        def then(ins):
            n[0] += 1
            ins.then_inc(self.link, 1)
            e.wait_ge(self.link, n[0])

        e.wait_ge(self.counted, T)
        then(e.tensor_copy(count[1][:, :], self.hist_ps[:, 0:T]))
        then(e.tensor_tensor_scan(out=count[0][:, :], data0=self.c.onesT[:, :], data1=count[1][:, :],
                                  initial=0.0, op0=ALU.mult, op1=ALU.add))
        then(e.tensor_copy(row_sum[:, :], count[0][:, T - 1:T]))
        e.sem_inc(self.hist_done, 1)
        e.wait_ge(self.base_done, 1)
        then(e.tensor_copy(row_sum[:, :], self.at_ps[0][:, 0:1]))
        then(e.tensor_scalar(falls[:, :], self.at_ps[1][:, 0:1], 1.0, None, ALU.min))
        then(e.tensor_copy(tabs["unsorted"][:, :], falls[:, :]))
        then(e.tensor_scalar(count[0][:, :], count[0][:, :], row_sum[:, 0:1], None, ALU.add))
        then(e.tensor_tensor(out=offset[:, :], in0=count[0][:, :], in1=count[1][:, :], op=ALU.subtract))
        then(e.tensor_scalar(tmp[:, :], count[1][:, :], 0.0, None, ALU.is_equal))
        then(e.tensor_scalar(prod[:, :], count[0][:, :], -1.0, float(s.NP + 1), ALU.mult, ALU.add))
        then(e.tensor_tensor(out=prod[:, :], in0=prod[:, :], in1=tmp[:, :], op=ALU.mult))
        then(e.tensor_tensor(out=prod[:, :], in0=prod[:, :], in1=count[0][:, :], op=ALU.add))
        then(e.tensor_scalar(prod[:, :], prod[:, :], -1.0, None, ALU.add))
        then(e.tensor_copy(tabs["end"][:, 0:T], prod[:, :]))
        if "degree" in tabs:
            then(e.tensor_scalar(tabs["degree"][:, :], count[1][:, :], 1.0, None, ALU.add))

    def totals(self, e):
        e.wait_ge(self.hist_done, 1)
        e.matmul(self.at_ps[1][:, 0:1], self.c.onesT[:, 0:P], self.falls[:, :], start=True, stop=True)
        e.matmul(self.at_ps[0][:, 0:1], self.c.lower[:, :], self.row_sum[:, :], start=True, stop=True
                 ).then_inc(self.base_done, 1)

    def histogram(self):
        s = self.s
        with self.nc.Block() as block:
            @block.vector
            def _(e):
                def body(g, b):
                    self.hot_group(e, g, b)
                    for t in range(G):
                        self.hot_tile(e, g, b, t)

                run_groups(e, s, body)
                self.prefix(e)

            @block.tensor
            def _(e):
                run_groups(e, s, lambda g, b: self.count_group(e, g, b))
                self.totals(e)

    def place(self):
        nc, c, s, sem, sb, bank = self.nc, self.c, self.s, self.sem, self.sb, self.bank
        tabs, rec_dram = self.tabs, self.rec_dram
        T, NG = s.T, s.NG
        FOURTH, OTHERS = G // 4, G - G // 4
        LATE = 5
        hi, lo, key_f, rec, lh, hot_hi, hot_lo = (self.hi, self.lo, self.key_f, self.rec, self.lh, self.hot_hi,
                                                  self.hot_lo)
        count, offset, hist_ps, at_ps = self.count, self.offset, self.hist_ps, self.at_ps
        rec_now = [sb(f"rec_now{b}", [P, G, 4], F32) for b in range(R)]
        pos_now = [sb(f"pos_now{b}", [P, G], I32) for b in range(R)]
        apart = [sb(f"apart{b}", [P, P], F16) for b in range(3)]
        hot_hiT = [sb(f"hot_hiT{b}", [P, P], F32) for b in range(4)]
        same_key = [sb(f"same_key{b}", [P, P], F32) for b in range(2)]
        picked = [sb(f"picked{b}", [P, T], F32) for b in range(2)]
        hit = [sb(f"hit{b}", [P, G], F32) for b in range(R)]
        rank = [sb(f"rank{b}", [P, G], F32) for b in range(R)]
        hotT_bank = [bank(f"hotT{b}", 1024, F16) for b in range(2)]
        key_ps = [bank(f"key{b}") for b in range(2)]
        hot, counted2, snap, keyT_ps, hotT_ps, hotT, at, placed, put = (
            sem("hot"), sem("counted2"), sem("snap"), sem("keyT_ps"), sem("hotT_ps"),
            sem("hotT"), sem("at"), sem("placed"), [sem(f"put{b}") for b in range(R)])
        squared, high, high_fourth = sem("squared"), sem("high"), sem("high_fourth")
        lh2, ranked, summed, kept = sem("lh2"), sem("ranked"), sem("summed"), sem("kept")
        unsorted = nc.values_load(tabs["unsorted"][0:1, 0:1], min_val=0, max_val=1,
                                  skip_runtime_bounds_check_because="VectorE wrote 0 or 1")
        with nc.If(unsorted > 0), nc.Block() as block:
            @block.vector
            def _(e):
                def pick(g, b, t):
                    n, o = g * G + t, t % 2
                    if not (first(g) and n < 2):
                        e.wait_ge(ranked, n - 1)
                        e.wait_ge(summed, n - 1)
                    e.wait_ge(keyT_ps, n + 1)
                    e.scalar_tensor_tensor(out=same_key[o][:, :], in0=key_ps[o][:, 0:P],
                                           scalar=lh[b][:, t, 2:3], in1=c.before[:, :],
                                           op0=ALU.is_equal, op1=ALU.mult,
                                           accum_out=rank[b][:, t:t + 1]).then_inc(ranked, 1)
                    e.wait_ge(at, n + 1)
                    e.scalar_tensor_tensor(out=picked[o][:, :], in0=at_ps[o][:, 0:T], scalar=0.0,
                                           in1=hot_lo[t][:, :], op0=ALU.add, op1=ALU.mult,
                                           accum_out=hit[b][:, t:t + 1]).then_inc(summed, 1)

                def place(g, b):
                    e.wait_ge(summed, (g + 1) * G)
                    e.wait_ge(ranked, (g + 1) * G)
                    e.tensor_tensor(out=pos_now[b][:, :], in0=hit[b][:, :], in1=rank[b][:, :], op=ALU.add
                                    ).then_inc(placed, 1)

                def body(g, b):
                    if not first(g):
                        e.wait_ge(put[b], (g - b) * (16 * G // R))
                    e.tensor_copy(lh[b][:, :, 0], cols(hi, g))
                    e.tensor_copy(lh[b][:, :, 1], cols(lo, g))
                    e.tensor_copy(lh[b][:, :, 2], cols(key_f, g))
                    e.tensor_copy(rec_now[b][:, :, :],
                                  rec[:, bass.ds(g * G, G), :] if not isinstance(g, int)
                                  else rec[:, g * G:(g + 1) * G, :]).then_inc(lh2, 1)
                    e.wait_ge(lh2, g + 1)
                    for t in range(G):
                        n = g * G + t
                        if later(g):
                            e.wait_ge(counted2, n + 2 - G)
                            e.wait_ge(summed, n + 1 - G)
                        if t % 4 == 3:
                            e.tensor_scalar(hot_hi[t][:, :], c.iota_free[:, 0:P], lh[b][:, t, 0:1], None,
                                            ALU.is_equal).then_inc(high_fourth, 1)
                        e.tensor_scalar(hot_lo[t][:, :], c.iota_free[:, :], lh[b][:, t, 1:2], None,
                                        ALU.is_equal).then_inc(hot, 1)
                        late = back(g, b, t, LATE)
                        if late is not None:
                            pick(*late)
                            if late[2] == G - 1:
                                place(*late[:2])

                run_groups(e, s, body)
                behind(s, LATE, pick)
                place(NG - 1, (NG - 1) % R)

            @block.tensor
            def _(e):
                e.matmul(hist_ps[:, 0:T], c.ident[:, :], offset[:, :], start=True, stop=False,
                         skip_group_check=True).then_inc(counted2, 1)

                def count_tile(g, b, t, stop=False):
                    n, o = g * G + t, t % 2
                    if not (first(g) and n < 2):
                        e.wait_ge(ranked, n - 1)
                        e.wait_ge(summed, n - 1)
                    e.transpose(key_ps[o][:, 0:P], lh[b][:, t, 2:3].broadcast_to([P, P]), c.ident[:, :]
                                ).then_inc(keyT_ps, 1)
                    e.wait_ge(snap, n + 1)
                    e.wait_ge(hot, n + 1)
                    e.matmul(hist_ps[:, 0:T], hot_hi[t][:, :], hot_lo[t][:, :], start=False,
                             stop=stop, skip_group_check=True).then_inc(counted2, 1)
                    e.wait_ge(hotT, n + 1)
                    e.matmul(at_ps[o][:, 0:T], hot_hiT[t % 4][:, :], count[t % 4][:, :], start=True,
                             stop=True).then_inc(at, 1)

                def body(g, b):
                    for t in range(G):
                        n, o = g * G + t, t % 2
                        if t % 4 == 3:
                            e.wait_ge(high_fourth, g * FOURTH + (t // 4 + 1))
                        else:
                            e.wait_ge(high, g * OTHERS + (t - t // 4 + 1))
                        if not (first(g) and n < 2):
                            e.wait_ge(hotT, n - 1)
                        e.transpose(hotT_bank[o][:, 0:P], hot_hi[t][:, :], c.identh[:, :]
                                    ).then_inc(hotT_ps, 1)
                        late = back(g, b, t, 1)
                        if late is not None:
                            count_tile(*late)

                run_groups(e, s, body)
                count_tile(NG - 1, (NG - 1) % R, G - 1, stop=True)

            @block.scalar
            def _(e):
                def snapshot(g, b, t):
                    n = g * G + t
                    e.wait_ge(counted2, n + 1)
                    if not (first(g) and n < 4):
                        e.wait_ge(at, n - 3)
                    e.activation(count[t % 4][:, :], hist_ps[:, 0:T], ACT.Copy).then_inc(snap, 1)

                def copy_turned(g, b, t):
                    n, o = g * G + t, t % 2
                    e.wait_ge(hotT_ps, n + 1)
                    if not (first(g) and n < 4):
                        e.wait_ge(at, n - 3)
                    e.activation(hot_hiT[t % 4][:, :], hotT_bank[o][:, 0:P], ACT.Copy).then_inc(hotT, 1)

                def square(g, b, t):
                    if t == 0:
                        e.wait_ge(lh2, g + 1)
                    if t % 4 == 3:
                        return
                    if not first(g) or g * OTHERS + (t - t // 4) >= 3:
                        e.wait_ge(high, g * OTHERS + (t - t // 4 - 2))
                    e.activation(apart[t % 4][:, :], c.iota_free[:, 0:P], ACT.Square, scale=-1.0,
                                 bias=lh[b][:, t, 0:1]).then_inc(squared, 1)

                def one_hot(g, b, t):
                    if t % 4 == 3:
                        return
                    e.wait_ge(squared, g * OTHERS + (t - t // 4 + 1))
                    if later(g):
                        e.wait_ge(counted2, g * G + (t + 2 - G))
                    e.activation(hot_hi[t][:, :], apart[t % 4][:, :], ACT.Relu, scale=-1.0,
                                 bias=c.onesT[:, 0:1]).then_inc(high, 1)

                steps = ((0, square), (1, one_hot), (3, snapshot), (2, copy_turned))

                def body(g, b):
                    for t in range(G):
                        for lag, step in steps:
                            late = back(g, b, t, lag)
                            if late is not None:
                                step(*late)

                run_groups(e, s, body)
                for t in range(3):
                    for lag, step in steps:
                        if t < lag:
                            step(*back(NG, NG % R, t, lag))

            @block.gpsimd
            def _(e):
                def body(g, b):
                    e.wait_ge(placed, g + 1)
                    e.nop(nofuse=True)
                    for t in range(G):
                        e.indirect_dma_start(out=rec_dram[:, :],
                                             out_offset=bass.IndirectOffsetOnAxis(
                                                 ap=pos_now[b][:, t:t + 1], axis=0),
                                             in_=rec_now[b][:, t, :], in_offset=None).then_inc(put[b], 16)

                run_groups(e, s, body)
                for b in range(R):
                    e.wait_ge(put[b], 16 * G * uses(s, b))

        with nc.Else(), nc.Block() as block:
            @block.sync
            def _(e):
                e.dma_start(rec_dram[0:s.NP, :].rearrange("(p t) f -> p t f", t=T), rec[:, :, :]
                            ).then_inc(kept, 16)
                e.wait_ge(kept, 16)


def sorted_tables(nc, c, name, rec_dram, tabs):
    s = c.s
    T = s.T
    with ExitStack() as ctx:
        sem = semaphores(nc, ctx, f"{name}")

        rec = ctx.enter_context(nc.sbuf_tensor(f"{name}_sorted", [P, T, 4], F32))
        eq = ctx.enter_context(nc.sbuf_tensor(f"{name}_eq", [P, T], F32))
        last_key = ctx.enter_context(nc.sbuf_tensor(f"{name}_last_key", [P, 1], F32))
        first_key = ctx.enter_context(nc.sbuf_tensor(f"{name}_first_key", [P, 1], F32))
        length = ctx.enter_context(nc.sbuf_tensor(f"{name}_length", [P, 1], F32))
        row_ps = ctx.enter_context(nc.psum_tensor(f"{name}_row", [P, 512], F32))
        loaded, link, keys, row = sem("t_loaded"), sem("t_link"), sem("t_keys"), sem("t_row")
        with nc.Block() as block:
            @block.sync
            def _(e):
                e.dma_start(rec[:, :, :], rec_dram[0:s.NP, :].rearrange("(p t) f -> p t f", t=T)
                            ).then_inc(loaded, 16)

            @block.tensor
            def _(e):
                e.wait_ge(keys, 1)
                e.transpose(row_ps[:, 0:P], first_key[:, 0:1].broadcast_to([P, P]), c.ident[:, :]
                            ).then_inc(row, 1)

            @block.vector
            def _(e):
                n = [0]

                def then(ins):
                    n[0] += 1
                    ins.then_inc(link, 1)
                    e.wait_ge(link, n[0])

                e.wait_ge(loaded, 16)
                then(e.tensor_copy(first_key[:, :], rec[:, 0:1, 0]))
                e.sem_inc(keys, 1)
                then(e.tensor_copy(last_key[:, :], rec[:, T - 1:T, 0]))
                e.tensor_copy(tabs["other"][:, 0:T], rec[:, :, 1])
                if "weight" in tabs:
                    e.tensor_copy(tabs["weight"][:, :], rec[:, :, 2])
                e.memset(tabs["same"][:, 0:1], 0.0)
                e.tensor_tensor(out=tabs["same"][:, 1:T], in0=rec[:, 1:T, 0], in1=rec[:, 0:T - 1, 0],
                                op=ALU.is_equal)
                then(e.tensor_scalar(eq[:, :], rec[:, :, 0], first_key[:, 0:1], None, ALU.is_equal))
                then(e.tensor_reduce(out=length[:, :], in_=eq[:, :], axis=AX.X, op=ALU.add))
                then(e.tensor_scalar(length[:, :], length[:, :], -1.0, None, ALU.add))
                e.tensor_tensor(out=tabs["fix_row"][:, :], in0=length[:, :], in1=c.node_f[:, 0:1],
                                op=ALU.add)
                e.wait_ge(row, 1)
                e.scalar_tensor_tensor(out=tabs["fix"][:, :], in0=row_ps[:, 0:P], scalar=last_key[:, 0:1],
                                       in1=c.lower[:, :], op0=ALU.is_equal, op1=ALU.mult)


def edge_phase(nc, c, name, table, tabs, runs, beside=None, prepare=None):
    s = c.s
    T, NG = s.T, s.NG
    view = runs[0:s.NP, :].rearrange("(p t) d -> p t d", t=T)
    with ExitStack() as ctx:
        def sb(n, shape, dt):
            return ctx.enter_context(nc.sbuf_tensor(f"{name}_{n}", shape, dt))

        sem = semaphores(nc, ctx, f"{name}")

        index = [sb(f"index{b}", [P, G], I32) for b in range(R)]
        flag = [sb(f"flag{b}", [P, G], F32) for b in range(R)]
        rows = [sb(f"rows{b}", [P, G, D], F32) for b in range(R)]
        run = [sb(f"run{b}", [P, G, D], F32) for b in range(R)]
        fixed = sb("fixed", [P, D], F32)
        carry_ps = beside.at_ps[1] if beside else ctx.enter_context(nc.psum_tensor(f"{name}_carry", [P, 512], F32))
        indexed, flagged, summed, wrote = sem("indexed"), sem("flagged"), sem("summed"), sem("wrote")
        got = got_semaphores(sem)
        put = [sem(f"put{b}") for b in range(R)]
        fix_got, fix_sum, fix_put, carried = sem("fix_got"), sem("fix_sum"), sem("fix_put"), sem("carried")
        with nc.Block() as block:
            @block.gpsimd
            def _(e):
                def body(g, b):
                    if not first(g):
                        e.wait_ge(summed, (g - R + 1) * G)
                    e.wait_ge(indexed, g + 1)
                    e.nop(nofuse=True)
                    for t in range(G):
                        gather(e, rows[b][:, t, :], table[:, :], index[b][:, t:t + 1]).then_inc(got[b][t // Q], 16)

                run_groups(e, s, body)
                e.wait_ge(wrote, 1)
                gather(e, fixed[:, :], runs[:, :], tabs["fix_row"][:, 0:1]).then_inc(fix_got, 16)
                e.wait_ge(fix_sum, 1)
                e.indirect_dma_start(out=runs[:, :],
                                     out_offset=bass.IndirectOffsetOnAxis(ap=tabs["fix_row"][:, 0:1], axis=0),
                                     in_=fixed[:, :], in_offset=None).then_inc(fix_put, 16)
                e.wait_ge(fix_put, 16)

            @block.vector
            def _(e):
                e.memset(run[R - 1][:, G - 1, :], 0.0).then_inc(flagged, 1)

                def copies(g, b):
                    if not first(g):
                        wait_free(e, got, g, b)
                    e.tensor_copy(index[b][:, :], cols(tabs["other"], g)).then_inc(indexed, 1)

                def body(g, b):
                    copy_ahead(s, g, b, copies)
                    if prepare and isinstance(g, int) and g in (1, 3):
                        prepare[2][g // 2](e)
                    e.tensor_copy(flag[b][:, :], cols(tabs["same"], g)).then_inc(flagged, 1)
                    e.wait_ge(flagged, g + 2)
                    if not first(g):
                        e.wait_ge(put[b], (g - b) * (16 // R))
                    if beside:
                        beside.hot_group(e, g, b)
                    for t in range(G):
                        wait_rows(e, got, g, b, t)
                        before = run[b][:, t - 1, :] if t else run[(b - 1) % R][:, G - 1, :]
                        if not (isinstance(g, int) and g == 0 and t == 0):
                            e.wait_ge(summed, g * G + t)
                        e.scalar_tensor_tensor(out=run[b][:, t, :], in0=before, scalar=flag[b][:, t:t + 1],
                                               in1=rows[b][:, t, :], op0=ALU.mult, op1=ALU.add
                                               ).then_inc(summed, 1)
                        if beside:
                            beside.hot_tile(e, g, b, t)

                run_groups(e, s, body)
                e.wait_ge(fix_got, 16)
                e.wait_ge(carried, 1)
                e.tensor_tensor(out=fixed[:, :], in0=carry_ps[:, 0:D], in1=fixed[:, :], op=ALU.add
                                ).then_inc(fix_sum, 1)
                if beside:
                    beside.prefix(e)

            @block.sync
            def _(e):
                if prepare:
                    prepare[0](e)

                def body(g, b):
                    e.wait_ge(summed, (g + 1) * G)
                    e.dma_start(tile_rows(view, g), run[b][:, :, :]).then_inc(put[b], 16)

                run_groups(e, s, body)
                for b in range(R):
                    e.wait_ge(put[b], 16 * uses(s, b))
                e.sem_inc(wrote, 1)

            @block.tensor
            def _(e):
                if beside:
                    def body(g, b):
                        if prepare and isinstance(g, int) and g in (1, 3):
                            prepare[1][g // 2](e)
                        beside.count_group(e, g, b)

                    run_groups(e, s, body)
                e.wait_ge(summed, T)
                e.matmul(carry_ps[:, 0:D], tabs["fix"][:, :], run[(NG - 1) % R][:, G - 1, :], start=True,
                         stop=True).then_inc(carried, 1)
                if beside:
                    beside.totals(e)


def hop_phase(nc, c, name, table, index_of, tabs, weight, bias, out, runs=None, next_index=None, passed=None):
    s = c.s
    T, NG = s.T, s.NG
    first_hop = runs is not None
    RINGS = 4
    PRODUCT, LEAD = 2, 4
    W = WIDE if first_hop else D

    def rows_of(m):
        return m[0:s.NP, :].rearrange("(p t) d -> p t d", t=T)

    with ExitStack() as ctx:
        def sb(n, shape, dt):
            return ctx.enter_context(nc.sbuf_tensor(f"{name}_{n}", shape, dt))

        sem = semaphores(nc, ctx, f"{name}")

        def ring(n, shape, dt, k=R):
            return [sb(f"{n}{b}", shape, dt) for b in range(k)]

        index, flag, factor = ring("index", [P, G], I32), ring("flag", [P, G], F32), ring("factor", [P, G], F32)
        rows, run, made = ring("rows", [P, G, W], F32), ring("run", [P, G, D], F32), ring("made", [P, G, WIDE], F32)
        first_made = None if first_hop else ring("first_made", [P, G, WIDE], F32)
        hT = ring("hT", [P, KC, P], F32, RINGS)
        mend = runs if first_hop else out
        MW = D if first_hop else WIDE
        fixed = sb("fixed", [P, MW], F32)
        bare = None if first_hop else sb("bare", [P, WIDE], F32)
        hT_ps = [ctx.enter_context(nc.psum_tensor(f"{name}_hT_ps{b}", [P, 4, P], F32)) for b in range(RINGS)]
        out_ps = [ctx.enter_context(nc.psum_tensor(f"{name}_out_ps{b}", [P, 512], F32)) for b in range(2)]
        carry_ps = ctx.enter_context(nc.psum_tensor(f"{name}_carry", [P, 512], F32))
        indexed, flagged, weight_set, weighed, summed, turned, copied, multiplied, kept, wrote = (
            sem("indexed"), sem("flagged"), sem("weight_set"), sem("weighed"), sem("summed"), sem("turned"),
            sem("copied"), sem("multiplied"), sem("kept"), sem("wrote"))
        got = got_semaphores(sem)
        loaded = [sem(f"loaded{b}") for b in range(R)]
        put_run = [sem(f"put_run{b}") for b in range(R)]
        put = [sem(f"put{b}") for b in range(R)]
        bared, bias_put = sem("bared"), sem("bias_put")
        fix_got, fix_sum, fix_put, carried = sem("fix_got"), sem("fix_sum"), sem("fix_put"), sem("carried")

        with nc.Block() as block:
            @block.gpsimd
            def _(e):
                def body(g, b):
                    if not first(g):
                        e.wait_ge(summed, (g - R + 1) * G)
                    e.wait_ge(indexed, g + 1)
                    e.nop(nofuse=True)
                    for t in range(G):
                        gather(e, rows[b][:, t, :], table[:, :], index[b][:, t:t + 1]).then_inc(got[b][t // Q], 16)

                run_groups(e, s, body)
                e.wait_ge(wrote, 1)
                gather(e, fixed[:, :], mend[:, :], tabs["fix_row"][:, 0:1]).then_inc(fix_got, 16)
                e.wait_ge(fix_sum, 1)
                e.indirect_dma_start(out=mend[:, :],
                                     out_offset=bass.IndirectOffsetOnAxis(ap=tabs["fix_row"][:, 0:1], axis=0),
                                     in_=fixed[:, :], in_offset=None).then_inc(fix_put, 16)
                e.wait_ge(fix_put, 16)

            @block.sync
            def _(e):
                def store(g, b):
                    e.wait_ge(kept, (g + 1) * G)
                    e.dma_start(tile_rows(rows_of(out), g), made[b][:, :, :]).then_inc(put[b], 16)

                def body(g, b):
                    if not first_hop:
                        if not first(g):
                            e.wait_ge(kept, (g - R + 1) * G)
                        e.dma_start(first_made[b][:, :, :], tile_rows(rows_of(passed), g)).then_inc(loaded[b], 16)
                    late = back(g, b, 0, 3 * G)
                    if late is not None:
                        lg, lb = late[:2]
                        if first_hop:
                            e.wait_ge(summed, (lg + 1) * G)
                            e.dma_start(tile_rows(rows_of(runs), lg), run[lb][:, :, :]).then_inc(put_run[lb], 16)
                        store(lg, lb)

                if not first_hop:
                    e.dma_start(out[s.NP:s.NP + 1, :], bias[0:1, :]).then_inc(bias_put, 16)
                run_groups(e, s, body)
                if not first_hop:
                    e.wait_ge(bias_put, 16)
                for k in (3, 2, 1):
                    lg, lb = NG - k, (NG - k) % R
                    if first_hop:
                        e.wait_ge(summed, (lg + 1) * G)
                        e.dma_start(tile_rows(rows_of(runs), lg), run[lb][:, :, :]).then_inc(put_run[lb], 16)
                    store(lg, lb)
                for b in range(R):
                    e.wait_ge(put[b], 16 * uses(s, b))
                    if first_hop:
                        e.wait_ge(put_run[b], 16 * uses(s, b))
                e.sem_inc(wrote, 1)

            @block.tensor
            def _(e):
                def product(g, b, t):
                    n, o = g * G + t, t % 2
                    e.wait_ge(copied, n + 1)
                    if not (first(g) and n < 2):
                        e.wait_ge(kept, n - 1)
                    for k in range(KC):
                        last = e.matmul(out_ps[o][:, 0:WIDE], hT[t % RINGS][:, k, :], weight[:, k, :],
                                        start=(k == 0), stop=(k == KC - 1))
                    last.then_inc(multiplied, 1)

                def body(g, b):
                    for t in range(G):
                        n, o = g * G + t, t % RINGS
                        e.wait_ge(summed, n + 1)
                        if not (first(g) and n < RINGS):
                            e.wait_ge(copied, n + 1 - RINGS)
                        for k in range(KC):
                            last = e.transpose(hT_ps[o][:, k, :], run[b][:, t, k * P:(k + 1) * P], c.ident[:, :])
                        last.then_inc(turned, 1)
                        late = back(g, b, t, PRODUCT)
                        if late is not None:
                            product(*late)

                run_groups(e, s, body)
                behind(s, PRODUCT, product)
                if not first_hop:
                    e.wait_ge(bared, 1)
                e.matmul(carry_ps[:, 0:MW], tabs["fix"][:, :],
                         run[(NG - 1) % R][:, G - 1, :] if first_hop else bare[:, :], start=True,
                         stop=True).then_inc(carried, 1)

            @block.scalar
            def _(e):
                def copy_turned(g, b, t):
                    n, o = g * G + t, t % RINGS
                    e.wait_ge(turned, n + 1)
                    if not (first(g) and n < RINGS):
                        e.wait_ge(multiplied, n + 1 - RINGS)
                    e.activation(hT[o][:, :, :], hT_ps[o][:, 0:KC, :], ACT.Copy).then_inc(copied, 1)

                def body(g, b):
                    e.activation(factor[b][:, :], cols(tabs["weight"], g), ACT.Copy).then_inc(weight_set, 1)
                    e.wait_ge(weight_set, g + 1)
                    for t in range(G):
                        wait_rows(e, got, g, b, t)
                        e.activation(rows[b][:, t, 0:D], rows[b][:, t, 0:D], ACT.Copy,
                                     scale=factor[b][:, t:t + 1]).then_inc(weighed, 1)
                        late = back(g, b, t, 2)
                        if late is not None:
                            copy_turned(*late)

                run_groups(e, s, body)
                behind(s, 2, copy_turned)

            @block.vector
            def _(e):
                e.memset(run[R - 1][:, G - 1, :], 0.0).then_inc(flagged, 1)

                def copies(g, b):
                    if not first(g):
                        wait_free(e, got, g, b)
                    e.tensor_copy(index[b][:, :], cols(index_of, g)).then_inc(indexed, 1)

                def keep(g, b, t):
                    n, o = g * G + t, t % 2
                    if t == 0 and not first(g):
                        e.wait_ge(put[b], (g - b) * (16 // R))
                    if t == 0 and not first_hop:
                        e.wait_ge(loaded[b], (g - b + R) * (16 // R))
                    e.wait_ge(multiplied, n + 1)
                    ps, dst = out_ps[o][:, 0:WIDE], made[b][:, t, :]
                    if first_hop:
                        e.tensor_tensor(out=dst, in0=ps, in1=bias[:, :], op=ALU.add).then_inc(kept, 1)
                    else:
                        e.tensor_tensor(out=dst, in0=ps, in1=first_made[b][:, t, :], op=ALU.add).then_inc(kept, 1)

                def body(g, b):
                    copy_ahead(s, g, b, copies)
                    e.tensor_copy(flag[b][:, :], cols(tabs["same"], g)).then_inc(flagged, 1)
                    e.wait_ge(flagged, g + 2)
                    if not first(g):
                        if first_hop:
                            e.wait_ge(put_run[b], (g - b) * (16 // R))
                        e.wait_ge(turned, (g - R + 1) * G)
                    for t in range(G):
                        if first_hop and t == G - 1:
                            wait_group(e, got, g, b)
                            e.tensor_copy(cols(next_index, g), rows[b][:, :, D])
                        e.wait_ge(weighed, g * G + (t + 1))
                        before = run[b][:, t - 1, :] if t else run[(b - 1) % R][:, G - 1, :]
                        if not (isinstance(g, int) and g == 0 and t == 0):
                            e.wait_ge(summed, g * G + t)
                        e.scalar_tensor_tensor(out=run[b][:, t, :], in0=before, scalar=flag[b][:, t:t + 1],
                                               in1=rows[b][:, t, 0:D], op0=ALU.mult, op1=ALU.add
                                               ).then_inc(summed, 1)
                        late = back(g, b, t, LEAD)
                        if late is not None:
                            keep(*late)

                run_groups(e, s, body)
                behind(s, LEAD, keep)
                if not first_hop:
                    e.wait_ge(kept, T)
                    e.tensor_tensor(out=bare[:, :], in0=made[(NG - 1) % R][:, G - 1, :], in1=bias[:, :],
                                    op=ALU.subtract).then_inc(bared, 1)
                e.wait_ge(fix_got, 16)
                e.wait_ge(carried, 1)
                e.tensor_tensor(out=fixed[:, :], in0=carry_ps[:, 0:MW], in1=fixed[:, :], op=ALU.add
                                ).then_inc(fix_sum, 1)


def back(g, b, t, lag):
    q = (t - lag) // G
    if isinstance(g, int) and g + q < 0:
        return None
    return (g + q if q else g), (b + q) % R, (t - lag) % G


def behind(s, lag, step):
    for t in range(lag):
        step(*back(s.NG, s.NG % R, t, lag))


def variance(e, chained, stats, small):
    mean2, diff, var = small[:, 0, :], small[:, 1, :], small[:, 2, :]
    e.tensor_tensor(out=mean2, in0=stats[:, :, 1], in1=stats[:, :, 4], op=ALU.add)
    e.tensor_tensor(out=diff, in0=stats[:, :, 1], in1=stats[:, :, 4], op=ALU.subtract)
    chained(e.tensor_tensor(out=var, in0=stats[:, :, 2], in1=stats[:, :, 5], op=ALU.add))
    chained(e.tensor_tensor(out=diff, in0=diff, in1=diff, op=ALU.mult))
    chained(e.scalar_tensor_tensor(out=var, in0=diff, scalar=D / 4.0, in1=var, op0=ALU.mult, op1=ALU.add))
    return e.tensor_scalar(var, var, 1.0 / D, EPS, ALU.mult, ALU.add)


def norm_factors(e, chained, small, scale, shift, dinv):
    chained(e.reciprocal(out=scale[:, :], in_=small[:, 3, :]))
    if dinv is not None:
        chained(e.tensor_tensor(out=scale[:, :], in0=scale[:, :], in1=dinv, op=ALU.mult))
    return e.scalar_tensor_tensor(out=shift[:, :], in0=small[:, 0, :], scalar=-0.5, in1=scale[:, :],
                                  op0=ALU.mult, op1=ALU.mult)


def node_phase(nc, c, name, kind, runs, end, x_in, out, weight, bias=None, y_in=None, ragged=0,
               tables=None, next_end=None, head_sums=None, scores=None):
    s = c.s
    T, NG = s.T, s.NG
    hop = kind == "hop"
    AW = XW = WIDE if hop else D
    OW = WIDE if kind in ("hop", "gcn2") else D
    PW = WIDE if hop else D
    summed_in = kind in ("gin", "gcn1", "gcn2")
    normed_out = kind in ("gin", "gcn2", "hop")
    RINGS = 4
    PRODUCT, KEEP, LEAD, NORM = 2, 3, 4, G + 7

    with ExitStack() as ctx:
        def sb(n, shape, dt):
            return ctx.enter_context(nc.sbuf_tensor(f"{name}_{n}", shape, dt))

        sem = semaphores(nc, ctx, f"{name}")

        def ring(n, shape, dt, k=R):
            return [sb(f"{n}{b}", shape, dt) for b in range(k)]

        index = ring("index", [P, G], I32)
        A, X, O = ring("A", [P, G, AW], F32), ring("X", [P, G, XW], F32), ring("O", [P, G, OW], F32)
        head = ring("head", [P, 3, G, H], F32) if hop else None
        Y = ring("Y", [P, G, D], F32) if kind == "gcn2" else None
        h = ring("h", [P, D], F32, 4) if summed_in else None
        hT = ring("hT", [P, KC, P], F32, RINGS)
        half = ring("half", [P, D], F32, 2) if kind == "gcn2" else None
        stats = ring("stats", [P, G, 6], F32)
        small = ring("small", [P, 4, G], F32)
        scale, shift = ring("scale", [P, G], F32), ring("shift", [P, G], F32)
        factor = ring("factor", [P, 2, G], F32)
        hT_ps = [ctx.enter_context(nc.psum_tensor(f"{name}_hT_ps{b}", [P, 4, P], F32)) for b in range(RINGS)]
        out_ps = [ctx.enter_context(nc.psum_tensor(f"{name}_out_ps{b}", [P, 512], F32)) for b in range(RINGS)]
        indexed, factored, added, turned, copied, multiplied, summed = (
            sem("indexed"), sem("factored"), sem("added"), sem("turned"), sem("copied"), sem("multiplied"), sem("summed"))
        halved, measured, chain, root_asked, root_done, factors, normed = (
            sem("halved"), sem("measured"), sem("chain"), sem("root_asked"), sem("root_done"),
            sem("factors"), sem("normed"))
        got = got_semaphores(sem)
        loaded = [sem(f"loaded{b}") for b in range(R)]
        put = [sem(f"put{b}") for b in range(R)]
        scored, put_scores = sem("scored"), [sem(f"put_scores{b}") for b in range(R)]
        loads = (48 if ragged else 16) + (16 if Y else 0)

        def in_rows(view, g, full, dst, e, sm):
            if not ragged:
                e.dma_start(dst, tile_rows(view, g)).then_inc(sm, 16)
                return
            top = view[0:(P - 1) * T, :].rearrange("(p t) d -> p t d", t=T)
            rest = view[(P - 1) * T:s.N, :].rearrange("(p t) d -> p t d", p=1)
            e.dma_start(dst[0:112], tile_rows(top, g, 0, 112)).then_inc(sm, 16)
            e.dma_start(dst[112:127], tile_rows(top, g, 112, 127)).then_inc(sm, 16)
            e.dma_start(dst[127:128], tile_rows(rest, g, 0, 1) if full else tile_rows(top, g, 126, 127)
                        ).then_inc(sm, 16)

        with nc.Block() as block:
            @block.gpsimd
            def _(e):
                def body(g, b):
                    if not first(g):
                        e.wait_ge(added if summed_in else summed, (g - R + 1) * G)
                    e.wait_ge(indexed, g + 1)
                    e.nop(nofuse=True)
                    for t in range(G):
                        gather(e, A[b][:, t, :], runs[:, :], index[b][:, t:t + 1]).then_inc(got[b][t // Q], 16)

                run_groups(e, s, body)

            @block.sync
            def _(e):
                def load(g, b, full):
                    if not first(g):
                        if kind == "gcn1":
                            e.wait_ge(added, (g - R + 1) * G)
                        elif hop:
                            e.wait_ge(turned, (g - R + 1) * G)
                        else:
                            e.wait_ge(summed, (g - R + 1) * G)
                    in_rows(x_in, g, full, X[b][:, :, :], e, loaded[b])
                    if Y:
                        e.dma_start(Y[b][:, :, :], tile_rows(y_in, g)).then_inc(loaded[b], 16)

                def store(g, b):
                    if hop:
                        e.wait_ge(scored, g + 1)
                        e.dma_start(tile_rows(scores, g), head[b][:, 2, :, :]).then_inc(put_scores[b], 16)
                    e.wait_ge(normed, (g + 1) * G)
                    e.dma_start(tile_rows(out, g), O[b][:, :, 0:D] if hop else O[b][:, :, :]
                                ).then_inc(put[b], 16)

                def body(g, b, full=True):
                    load(g, b, full)
                    late = back(g, b, 0, 3 * G)
                    if late is not None:
                        store(late[0], late[1])

                run_groups(e, s, body, ragged)
                for k in (3, 2, 1):
                    store(NG - k, (NG - k) % R)
                for b in range(R):
                    e.wait_ge(put[b], 16 * uses(s, b))
                    if hop:
                        e.wait_ge(put_scores[b], 16 * uses(s, b))

            @block.tensor
            def _(e):
                def turn(g, b, t):
                    n = g * G + t
                    o = t % RINGS
                    if summed_in:
                        e.wait_ge(added, n + 1)
                    elif t == 0:
                        e.wait_ge(loaded[b], (g - b + R) * (loads // R))
                    if not (first(g) and n < RINGS):
                        e.wait_ge(copied, n + 1 - RINGS)
                    src = h[t % 4][:, :] if summed_in else X[b][:, t, :]
                    for k in range(KC):
                        last = e.transpose(hT_ps[o][:, k, :], src[:, k * P:(k + 1) * P], c.ident[:, :])
                    last.then_inc(turned, 1)

                def product(g, b, t):
                    n = g * G + t
                    o = t % RINGS
                    e.wait_ge(copied, n + 1)
                    if not (first(g) and n < RINGS):
                        e.wait_ge({"gcn1": normed, "gcn2": halved}.get(kind, summed), n + 1 - RINGS)
                    dst = out_ps[o][:, 0:PW]
                    if bias is not None:
                        e.matmul(dst, c.ones[:, :], bias[:, :], start=True, stop=False)
                    for k in range(KC):
                        last = e.matmul(dst, hT[o][:, k, :], weight[:, k, :],
                                        start=(k == 0 and bias is None), stop=(k == KC - 1))
                    last.then_inc(multiplied, 1)

                def body(g, b):
                    for t in range(G):
                        turn(g, b, t)
                        late = back(g, b, t, PRODUCT)
                        if late is not None:
                            product(*late)

                run_groups(e, s, body)
                behind(s, PRODUCT, product)

            @block.scalar
            def _(e):
                def norm(g, b, t):
                    if t == 0:
                        e.wait_ge(factors, g + 1)
                    e.activation(O[b][:, t, 0:D], O[b][:, t, 0:D], ACT.Identity, scale=scale[b][:, t:t + 1],
                                 bias=shift[b][:, t:t + 1]).then_inc(normed, 1)

                def roots(g, b):
                    e.wait_ge(root_asked, g + 1)
                    e.activation(small[b][:, 3, :], small[b][:, 2, :], ACT.Sqrt).then_inc(root_done, 1)

                def halve(g, b, t):
                    n = g * G + t
                    e.wait_ge(multiplied, n + 1)
                    e.wait_ge(factored, g + 1)
                    if not (first(g) and n < 2):
                        e.wait_ge(summed, n - 1)
                    e.activation(half[t % 2][:, :], out_ps[t % RINGS][:, 0:D], ACT.Copy,
                                 scale=factor[b][:, 0, t:t + 1]).then_inc(halved, 1)

                def rectify(g, b, t):
                    n = g * G + t
                    if t == 0 and not first(g):
                        e.wait_ge(put[b], (g - b) * (16 // R))
                    e.wait_ge(multiplied, n + 1)
                    e.wait_ge(factored, g + 1)
                    e.activation(O[b][:, t, :], out_ps[t % RINGS][:, 0:D], ACT.Relu,
                                 scale=factor[b][:, 0, t:t + 1]).then_inc(normed, 1)

                def body(g, b):
                    for t in range(G):
                        n = g * G + t
                        o = t % RINGS
                        e.wait_ge(turned, n + 1)
                        if not (first(g) and n < RINGS):
                            e.wait_ge(multiplied, n + 1 - RINGS)
                        e.activation(hT[o][:, :, :], hT_ps[o][:, 0:KC, :], ACT.Copy).then_inc(copied, 1)
                        late = back(g, b, t, KEEP)
                        if late is not None and kind == "gcn1":
                            rectify(*late)
                        if late is not None and kind == "gcn2":
                            halve(*late)
                        if normed_out:
                            late = back(g, b, t, NORM)
                            if late is not None:
                                norm(*late)
                            if t == LEAD + 1 and back(g, b, 0, G) is not None:
                                roots(*back(g, b, 0, G)[:2])

                run_groups(e, s, body)
                if kind in ("gcn1", "gcn2"):
                    behind(s, KEEP, rectify if kind == "gcn1" else halve)
                if normed_out:
                    for t in range(NORM):
                        if t == LEAD + 1:
                            roots(NG - 1, (NG - 1) % R)
                        norm(*back(NG, NG % R, t, NORM))

            @block.vector
            def _(e):
                def copies(g, b):
                    if not first(g):
                        wait_free(e, got, g, b)
                    e.tensor_copy(index[b][:, :], cols(end, g)).then_inc(indexed, 1)

                def copy_factors(g, b):
                    if kind == "gcn1" and not first(g):
                        e.wait_ge(normed, (g - R + 1) * G)
                    name = {"gin": "dinv", "gcn1": "dinv2", "gcn2": "dinv"}[kind]
                    if kind == "gcn2":
                        e.tensor_copy(factor[b][:, 1, :], cols(tables["root"], g))
                    e.tensor_copy(factor[b][:, 0, :], cols(tables[name], g)).then_inc(factored, 1)

                def add(g, b, t):
                    n = g * G + t
                    wait_rows(e, got, g, b, t)
                    if t == 0:
                        e.wait_ge(loaded[b], (g - b + R) * (loads // R))
                    if not (first(g) and n < 4):
                        e.wait_ge(turned, n - 3)
                    e.tensor_tensor(out=h[t % 4][:, :], in0=A[b][:, t, :], in1=X[b][:, t, :], op=ALU.add
                                    ).then_inc(added, 1)

                def residual(g, b, t):
                    n = g * G + t
                    if t == 0 and not first(g):
                        e.wait_ge(put[b], (g - b) * (16 // R))
                    if hop:
                        wait_rows(e, got, g, b, t)
                    if t == 0 and next_end is not None:
                        e.tensor_copy(O[b][:, :, D:OW], cols(next_end, g).unsqueeze(2).broadcast_to([P, G, H]))
                    e.wait_ge(multiplied, n + 1)
                    ps = out_ps[t % RINGS][:, 0:PW]
                    if kind == "gcn2":
                        e.wait_ge(halved, n + 1)
                        e.scalar_tensor_tensor(out=O[b][:, t, 0:D], in0=Y[b][:, t, :],
                                               scalar=factor[b][:, 1, t:t + 1], in1=half[t % 2][:, :],
                                               op0=ALU.mult, op1=ALU.add).then_inc(summed, 1)
                    else:
                        e.tensor_tensor(out=O[b][:, t, :], in0=ps, in1=(A if hop else X)[b][:, t, :],
                                        op=ALU.add).then_inc(summed, 1)

                def measure(g, b, t):
                    n = g * G + t
                    e.wait_ge(summed, n + 1)
                    e.bn_stats(out=stats[b][:, t, :], in_=O[b][:, t, 0:D]).then_inc(measured, 1)

                per = 4 if kind == "gcn2" else 5

                def chained_from(g, k):
                    def chained(ins):
                        k[0] += 1
                        ins.then_inc(chain, 1)
                        e.wait_ge(chain, g * per + k[0])
                    return chained

                def ask(g, b):
                    e.wait_ge(measured, (g + 1) * G)
                    variance(e, chained_from(g, [0]), stats[b], small[b]).then_inc(root_asked, 1)

                def finish(g, b):
                    e.wait_ge(root_done, g + 1)
                    norm_factors(e, chained_from(g, [3]), small[b], scale[b], shift[b],
                                 factor[b][:, 0, :] if kind == "gin" else None).then_inc(factors, 1)
                    if hop:
                        e.wait_ge(factors, g + 1)
                        if not first(g):
                            e.wait_ge(put_scores[b], (g - b) * (16 // R))
                        raw, low, high = O[b][:, :, D:WIDE], head[b][:, 0, :, :], head[b][:, 1, :, :]
                        e.tensor_tensor(out=low, in0=raw, in1=scale[b][:, :].unsqueeze(2).broadcast_to([P, G, H]),
                                        op=ALU.mult)
                        chained_from(g, [4])(
                            e.tensor_tensor(out=high, in0=head_sums[:, :].unsqueeze(1).broadcast_to([P, G, H]),
                                            in1=shift[b][:, :].unsqueeze(2).broadcast_to([P, G, H]), op=ALU.mult))
                        e.tensor_tensor(out=head[b][:, 2, :, :], in0=low, in1=high, op=ALU.add).then_inc(scored, 1)

                def body(g, b):
                    copy_ahead(s, g, b, copies)
                    if summed_in:
                        copy_factors(g, b)
                    for t in range(G):
                        if summed_in:
                            add(g, b, t)
                        if kind != "gcn1":
                            late = back(g, b, t, LEAD)
                            if late is not None:
                                residual(*late)
                        if normed_out:
                            late = back(g, b, t, LEAD + 1)
                            if late is not None:
                                measure(*late)
                            if back(g, b, 0, G) is not None:
                                if t == LEAD + 1:
                                    ask(*back(g, b, 0, G)[:2])
                                if t == LEAD + 2:
                                    finish(*back(g, b, 0, G)[:2])

                run_groups(e, s, body)
                if kind != "gcn1":
                    for t in range(LEAD + 1):
                        if t < LEAD:
                            residual(*back(NG, NG % R, t, LEAD))
                        if normed_out:
                            measure(*back(NG, NG % R, t, LEAD + 1))
                if normed_out:
                    ask(NG - 1, (NG - 1) % R)
                    finish(NG - 1, (NG - 1) % R)


def degrees(nc, c, tabs):
    with ExitStack() as ctx:
        rooted = semaphores(nc, ctx, "degrees")("rooted")
        block = ctx.enter_context(nc.Block())

        @block.scalar
        def _(e):
            e.activation(tabs["root"][:, :], tabs["degree"][:, :], ACT.Sqrt).then_inc(rooted, 1)

        @block.vector
        def _(e):
            e.reciprocal(out=tabs["dinv2"][:, :], in_=tabs["degree"][:, :])
            e.wait_ge(rooted, 1)
            e.reciprocal(out=tabs["dinv"][:, :], in_=tabs["root"][:, :])


def prepare_weights(nc, c, a, w, ctx):
    def sb(n, shape, dt):
        return ctx.enter_context(nc.sbuf_tensor(f"prep_{n}", shape, dt))

    sem = semaphores(nc, ctx, "prep")

    HC = a["W1"].shape[1] // P
    w1 = sb("w1", [P, KC, HC * P], F32)
    w2 = sb("w2", [P, HC, D], F32)
    w1T = sb("w1T", [P, HC, D], F32)
    b1, b = sb("b1", [P, HC], F32), sb("b", [P, KC], F32)
    rows = [sb(f"row{j}", [1, WIDE], F32) for j in range(4)]
    hopT = [sb(f"hopT{j}", [P, KC, D], F32) for j in range(3)]
    heads = sb("heads", [P, 2, D], F32)
    mixed = sb("mixed", [P, 2, KC, D], F32)
    turn_ps = [ctx.enter_context(nc.psum_tensor(f"prep_turn_ps{j}", [P, 512], F32)) for j in range(KC)]
    w_ps = [ctx.enter_context(nc.psum_tensor(f"prep_w_ps{j}", [P, 512], F32)) for j in range(KC)]
    b_ps = ctx.enter_context(nc.psum_tensor("prep_b_ps", [P, 512], F32))
    hopT_ps = [m[:, :].rearrange("p (j n) -> p j n", j=KC) for m in turn_ps]
    head_ps = b_ps[:, D:D + 8 * H].rearrange("p (j h) -> p j h", h=H)
    loaded, turned, copied, multiplied, link = (sem("loaded"), sem("turned"), sem("copied"),
                                                sem("multiplied"), sem("link"))
    bias_split, spread = sem("bias_split"), sem("spread")
    bias_hop = sb("bias_hop", [P, WIDE], BF16)
    hop_summed, hop_turned, hop_copied, heads_made = (
        sem("hop_summed"), sem("hop_turned"), sem("hop_copied"), sem("heads_made"))
    hops = [w["hop_x"], w["hop_1"], w["hop_2"]]
    LOADS = 14

    def chunks(m):
        return m.rearrange("(k p) n -> p k n", p=P)

    def load(e):
        for dst, src in ((w1, a["W1"]), (w2, a["W2"]), (w["gcn1"], a["G1"]), (w["gcn2"], a["G2"]),
                         (w["hop_x"], a["H"][0:D, :]), (w["hop_1"], a["H"][D:2 * D, :]),
                         (w["hop_2"], a["H"][2 * D:3 * D, :]), (w["gat"], a["A"])):
            e.dma_start(dst[:, :, 0:src.shape[1]], chunks(src)).then_inc(loaded, 16)
        with nc.allow_non_contiguous_dma(reason="biases of 512 and 256 elements as columns"):
            e.dma_start(b1[:, :], a["b1"].rearrange("(k p) -> p k", p=P)).then_inc(loaded, 16)
            e.dma_start(b[:, :], a["b"].rearrange("(k p) -> p k", p=P)).then_inc(loaded, 16)
        e.dma_start(rows[0][:, 0:D], a["b2"].rearrange("(o d) -> o d", o=1)).then_inc(loaded, 16)
        e.dma_start(rows[1][:, 0:D], a["b"].rearrange("(o d) -> o d", o=1)).then_inc(loaded, 16)
        for j, m in enumerate((a["al"], a["ar"])):
            e.dma_start(heads[:, j, :], m.rearrange("h d -> (h d)").rearrange("(o n) -> o n", o=1)
                        .broadcast_to([P, D])).then_inc(loaded, 16)

    def products(e):
        e.wait_ge(loaded, 16 * LOADS)
        for k in range(KC):
            for j in range(HC):
                last = e.transpose(turn_ps[k][:, j * P:(j + 1) * P], w1[:, k, j * P:(j + 1) * P],
                                   c.ident[:, :])
        last.then_inc(turned, 1)
        e.wait_ge(copied, 1)
        for k in range(KC):
            for j in range(HC):
                e.matmul(w_ps[k][:, 0:D], w1T[:, j, k * P:(k + 1) * P], w2[:, j, :],
                         start=(j == 0), stop=(j == HC - 1))
        for j in range(HC):
            last = e.matmul(b_ps[0:1, 0:D], b1[:, j:j + 1], w2[:, j, :], start=(j == 0),
                            stop=(j == HC - 1))
        last.then_inc(multiplied, 1)

    def more_products(e):
        e.wait_ge(hop_summed, 1)
        for m in range(3):
            if m == 2:
                e.wait_ge(hop_copied, 1)
            for k in range(KC):
                for j in range(KC):
                    last = e.transpose(hopT_ps[m % 2][:, j, k * P:(k + 1) * P],
                                       hops[m][:, k, j * P:(j + 1) * P], c.ident[:, :])
            last.then_inc(hop_turned, 1)
        e.wait_ge(hop_copied, 3)
        for j in range(3 * KC + 2):
            for k in range(KC):
                if j < 3 * KC:
                    lhsT, to = hopT[j // KC][:, k, (j % KC) * P:(j % KC + 1) * P], head_ps[:, j, :]
                elif j == 3 * KC:
                    lhsT, to = b[:, k:k + 1], head_ps[0:1, j, :]
                else:
                    lhsT, to = c.onesT[:, 0:P], head_ps[:, j, :]
                last = e.matmul(to, lhsT, w["left"][:, k, :], start=(k == 0), stop=(k == KC - 1))
        last.then_inc(heads_made, 1)
        e.wait_ge(bias_split, 1)
        e.matmul(w_ps[0][:, 0:WIDE], c.ones[:, :], bias_hop[:, :], start=True, stop=True).then_inc(spread, 1)

    n = [0]

    def then(e, ins):
        n[0] += 1
        ins.then_inc(link, 1)
        e.wait_ge(link, n[0])

    def combine(e):
        e.memset(w["bias_gin"][:, :], 0.0)
        then(e, e.memset(bias_hop[:, :], 0.0))
        e.wait_ge(turned, 1)
        for k in range(KC):
            last = e.tensor_copy(w1T[:, :, k * P:(k + 1) * P],
                                 turn_ps[k][:, :].rearrange("p (j m) -> p j m", j=HC))
        last.then_inc(copied, 1)
        for k in range(KC):
            e.tensor_tensor(out=w["hop_x"][:, k, k * P:(k + 1) * P], in0=w["hop_x"][:, k, k * P:(k + 1) * P],
                            in1=c.ident[:, :], op=ALU.add)
        for j, dst in ((0, w["left"][:, :, :]), (1, w["gat"][:, :, D:WIDE])):
            for k in range(KC):
                then(e, e.tensor_tensor(out=mixed[:, j, k, :], in0=w["gat"][:, k, 0:D], in1=heads[:, j, :],
                                     op=ALU.mult))
                then(e, e.tensor_reduce(out=dst[:, k, :],
                                     in_=mixed[:, j, k, :].rearrange("p (h d) -> p h d", h=H),
                                     axis=AX.X, op=ALU.add))
        e.sem_inc(hop_summed, 1)

    def combine_more(e):
        for m in range(3):
            e.wait_ge(hop_turned, m + 1)
            e.tensor_copy(hopT[m][:, :, :], hopT_ps[m % 2][:, :, :]).then_inc(hop_copied, 1)
        e.wait_ge(heads_made, 1)
        for m in range(3):
            e.tensor_copy(hops[m][:, :, D:WIDE], head_ps[:, m * KC:(m + 1) * KC, :])
        e.tensor_copy(w["head_sums"][:, :], head_ps[:, 3 * KC + 1, :])
        e.memset(rows[0][:, D:WIDE], 0.0)
        then(e, e.tensor_copy(rows[1][:, D:WIDE], head_ps[0:1, 3 * KC, :]))
        e.wait_ge(multiplied, 1)
        for k in range(KC):
            e.tensor_copy(w["gin"][:, k, :], w_ps[k][:, 0:D])
        then(e, e.tensor_tensor(out=rows[0][:, 0:D], in0=b_ps[0:1, 0:D], in1=rows[0][:, 0:D], op=ALU.add))
        for row, dst in ((rows[0], w["bias_gin"]), (rows[1], bias_hop)):
            left = row
            for part, rest in ((0, rows[2]), (32, rows[3]), (64, None)):
                n_cols = dst.shape[1]
                then(e, e.tensor_copy(dst[part:part + 1, :], left[:, 0:n_cols]))
                if rest is not None:
                    then(e, e.tensor_tensor(out=rest[:, 0:n_cols], in0=left[:, 0:n_cols],
                                         in1=dst[part:part + 1, :], op=ALU.subtract))
                    left = rest
        e.sem_inc(bias_split, 1)
        e.wait_ge(spread, 1)
        e.tensor_copy(w["bias_row"][:, :], w_ps[0][:, 0:WIDE])

    return load, (products, more_products), (combine, combine_more)


def gat_phase(nc, c, x_rows, x_view, scores, left_end, right_end, weight, out, spill):
    s = c.s
    T, NG = s.T, s.NG
    DH = D // H
    with ExitStack() as ctx:
        def sb(n, shape, dt):
            return ctx.enter_context(nc.sbuf_tensor(f"gat_{n}", shape, dt))

        sem = semaphores(nc, ctx, "gat")

        def ring(n, shape, dt, k=R):
            return [sb(f"{n}{b}", shape, dt) for b in range(k)]

        index = ring("index", [P, 2, G], I32)
        A, X, O = ring("A", [P, G, D], F32), ring("X", [P, G, D], F32), ring("O", [P, G, D], F32)
        L = ring("L", [P, G, H], F32)
        XT = ring("XT", [P, G, WIDE], F32, 2)
        hT = ring("hT", [P, KC, P], F32, 2)
        score = ring("score", [P, 3, G, H], F32, 2)
        top = ring("top", [P, 3, G], F32, 2)
        prod = sb("prod", [P, G, D], F32)
        mix = sb("mix", [P, G, DH], F32)
        stats = ring("stats", [P, G, 6], F32)
        small = ring("small", [P, 4, G], F32)
        scale, shift = ring("scale", [P, G], F32), ring("shift", [P, G], F32)
        hT_ps = [ctx.enter_context(nc.psum_tensor(f"gat_hT_ps{b}", [P, 4, P], F32)) for b in range(2)]
        out_ps = [ctx.enter_context(nc.psum_tensor(f"gat_out_ps{b}", [P, 512], F32)) for b in range(2)]
        indexed, turned, copied, multiplied, kept = (sem("indexed"), sem("turned"), sem("copied"),
                                                     sem("multiplied"), sem("kept"))
        chain, exp_asked, exp_done, added, measured, root_asked, root_done, factors, normed = (
            sem("chain"), sem("exp_asked"), sem("exp_done"), sem("added"), sem("measured"),
            sem("root_asked"), sem("root_done"), sem("factors"), sem("normed"))
        got = got_semaphores(sem)
        loaded = [sem(f"loaded{b}") for b in range(R)]
        put = [sem(f"put{b}") for b in range(R)]
        NORM = 2 * G + 4
        out_top = out[0:(P - 1) * T, :].rearrange("(p t) d -> p t d", t=T)
        out_rest = out[(P - 1) * T:s.N, :].rearrange("(p t) d -> p t d", p=1)
        spill_view = spill[:, :].rearrange("(p t) d -> p t d", p=1)

        with nc.Block() as block:
            @block.gpsimd
            def _(e):
                def body(g, b):
                    if not first(g):
                        e.wait_ge(turned, (g - R + 1) * G)
                        e.wait_ge(exp_asked, g - R + 1)
                    e.wait_ge(indexed, g + 1)
                    e.nop(nofuse=True)
                    for t in range(G):
                        gather(e, A[b][:, t, :], x_rows[:, :], index[b][:, 0, t:t + 1]).then_inc(got[b][t // Q], 16)
                        gather(e, L[b][:, t, :], scores[:, :], index[b][:, 1, t:t + 1]).then_inc(got[b][t // Q], 16)

                run_groups(e, s, body)

            @block.sync
            def _(e):
                def store(g, b, full):
                    e.wait_ge(normed, (g + 1) * G)
                    e.dma_start(tile_rows(out_top, g, 0, 112), O[b][0:112]).then_inc(put[b], 16)
                    e.dma_start(tile_rows(out_top, g, 112, 127), O[b][112:127]).then_inc(put[b], 16)
                    e.dma_start(tile_rows(out_rest if full else spill_view, g, 0, 1), O[b][127:128]
                                ).then_inc(put[b], 16)

                def body(g, b, full):
                    if not first(g):
                        e.wait_ge(added, g - R + 1)
                    e.dma_start(X[b][:, :, :], tile_rows(x_view, g)).then_inc(loaded[b], 16)
                    late = back(g, b, 0, 4 * G)
                    if late is not None:
                        store(late[0], late[1], late[0] < s.full if isinstance(late[0], int) else full)

                run_groups(e, s, body, 2)
                for k in (4, 3, 2, 1):
                    store(NG - k, (NG - k) % R, False)
                for b in range(R):
                    e.wait_ge(put[b], 48 * uses(s, b))

            @block.tensor
            def _(e):
                def product(g, b, t):
                    n = g * G + t
                    e.wait_ge(copied, n + 1)
                    if not (first(g) and n < 2):
                        e.wait_ge(kept, n - 1)
                    for k in range(KC):
                        last = e.matmul(out_ps[t % 2][:, 0:WIDE], hT[t % 2][:, k, :], weight[:, k, :],
                                        start=(k == 0), stop=(k == KC - 1))
                    last.then_inc(multiplied, 1)

                def body(g, b):
                    for t in range(G):
                        n = g * G + t
                        wait_rows(e, got, g, b, t, 2)
                        if not (first(g) and n < 2):
                            e.wait_ge(copied, n - 1)
                        for k in range(KC):
                            last = e.transpose(hT_ps[t % 2][:, k, :], A[b][:, t, k * P:(k + 1) * P],
                                               c.ident[:, :])
                        last.then_inc(turned, 1)
                        late = back(g, b, t, 1)
                        if late is not None:
                            product(*late)

                run_groups(e, s, body)
                behind(s, 1, product)

            @block.scalar
            def _(e):
                def keep(g, b, t):
                    n = g * G + t
                    if t == 0 and not (isinstance(g, int) and g < 2):
                        e.wait_ge(added, g - 1)
                    e.wait_ge(multiplied, n + 1)
                    e.activation(XT[b % 2][:, t, :], out_ps[t % 2][:, 0:WIDE], ACT.Copy).then_inc(kept, 1)

                def roots(g, b):
                    e.wait_ge(root_asked, g + 1)
                    e.activation(small[b][:, 3, :], small[b][:, 2, :], ACT.Sqrt).then_inc(root_done, 1)

                def exponents(g, b):
                    e.wait_ge(exp_asked, g + 1)
                    e.activation(score[b % 2][:, 2, :, :], score[b % 2][:, 1, :, :], ACT.Exp
                                 ).then_inc(exp_done, 1)

                def norm(g, b, t):
                    if t == 0:
                        e.wait_ge(factors, g + 1)
                    e.activation(O[b][:, t, :], O[b][:, t, :], ACT.Identity, scale=scale[b][:, t:t + 1],
                                 bias=shift[b][:, t:t + 1]).then_inc(normed, 1)

                def body(g, b):
                    for t in range(G):
                        n = g * G + t
                        e.wait_ge(turned, n + 1)
                        if not (first(g) and n < 2):
                            e.wait_ge(multiplied, n - 1)
                        e.activation(hT[t % 2][:, :, :], hT_ps[t % 2][:, 0:KC, :], ACT.Copy).then_inc(copied, 1)
                        late = back(g, b, t, 2)
                        if late is not None:
                            keep(*late)
                        if t == 2 and back(g, b, 0, 2 * G) is not None:
                            roots(*back(g, b, 0, 2 * G)[:2])
                        if t == 3 and back(g, b, 0, G) is not None:
                            exponents(*back(g, b, 0, G)[:2])
                        late = back(g, b, t, NORM)
                        if late is not None:
                            norm(*late)

                run_groups(e, s, body)
                behind(s, 2, keep)
                for t in range(2):
                    norm(*back(NG, NG % R, t, NORM))
                roots(NG - 2, (NG - 2) % R)
                exponents(NG - 1, (NG - 1) % R)
                for t in range(2, NORM):
                    if t == G + 4:
                        roots(NG - 1, (NG - 1) % R)
                    norm(*back(NG, NG % R, t, NORM))

            @block.vector
            def _(e):
                PER = 12

                def chained_from(g, k):
                    def chained(ins):
                        k[0] += 1
                        ins.then_inc(chain, 1)
                        e.wait_ge(chain, g * PER + k[0])
                    return chained

                def copies(g, b):
                    if not first(g):
                        wait_free(e, got, g, b, 2)
                    e.tensor_copy(index[b][:, 0, :], cols(right_end, g))
                    e.tensor_copy(index[b][:, 1, :], cols(left_end, g)).then_inc(indexed, 1)

                def finish(g, b):
                    e.wait_ge(root_done, g + 1)
                    norm_factors(e, chained_from(g, [PER - 1]), small[b], scale[b], shift[b], None
                                 ).then_inc(factors, 1)

                def attend(g, b):
                    chained = chained_from(g, [0])
                    raw, low, high = (score[b % 2][:, j, :, :] for j in range(3))
                    best, total, inverse = (top[b % 2][:, j, :] for j in range(3))
                    e.wait_ge(kept, (g + 1) * G)
                    wait_group(e, got, g, b, 2)
                    chained(e.tensor_tensor(out=raw, in0=XT[b % 2][:, :, D:WIDE], in1=L[b][:, :, :], op=ALU.add))
                    chained(e.scalar_tensor_tensor(out=raw, in0=raw, scalar=0.01, in1=raw, op0=ALU.mult,
                                                   op1=ALU.max))
                    chained(e.tensor_reduce(out=best, in_=raw, axis=AX.X, op=ALU.max))
                    e.tensor_tensor(out=low, in0=raw, in1=best.unsqueeze(2).broadcast_to([P, G, H]),
                                    op=ALU.subtract).then_inc(exp_asked, 1)
                    e.wait_ge(exp_done, g + 1)
                    chained(e.tensor_reduce(out=total, in_=high, axis=AX.X, op=ALU.add))
                    chained(e.reciprocal(out=inverse, in_=total))
                    chained(e.tensor_tensor(out=low, in0=high, in1=inverse.unsqueeze(2).broadcast_to([P, G, H]),
                                            op=ALU.mult))
                    for t in range(G):
                        ins = e.tensor_tensor(out=prod[:, t, :].rearrange("p (h d) -> p h d", h=H),
                                              in0=XT[b % 2][:, t, 0:D].rearrange("p (h d) -> p h d", h=H),
                                              in1=low[:, t, :].unsqueeze(2).broadcast_to([P, H, DH]), op=ALU.mult)
                    chained(ins)
                    chained(e.tensor_reduce(out=mix[:, :, :], in_=prod[:, :, :].rearrange("p g (h d) -> p g d h", h=H),
                                            axis=AX.X, op=ALU.add))
                    e.wait_ge(loaded[b], (g - b + R) * (16 // R))
                    if not first(g):
                        e.wait_ge(put[b], (g - b) * (48 // R))
                    e.tensor_tensor(out=O[b][:, :, :].rearrange("p g (h d) -> p g h d", h=H),
                                    in0=X[b][:, :, :].rearrange("p g (h d) -> p g h d", h=H),
                                    in1=mix[:, :, :].unsqueeze(2).broadcast_to([P, G, H, DH]), op=ALU.add
                                    ).then_inc(added, 1)
                    e.wait_ge(added, g + 1)
                    for t in range(G):
                        e.bn_stats(out=stats[b][:, t, :], in_=O[b][:, t, :]).then_inc(measured, 1)
                    e.wait_ge(measured, (g + 1) * G)
                    variance(e, chained_from(g, [8]), stats[b], small[b]).then_inc(root_asked, 1)

                def body(g, b):
                    copy_ahead(s, g, b, copies)
                    if back(g, b, 0, 2 * G) is not None:
                        finish(*back(g, b, 0, 2 * G)[:2])
                    if back(g, b, 0, G) is not None:
                        attend(*back(g, b, 0, G)[:2])

                run_groups(e, s, body)
                finish(NG - 2, (NG - 2) % R)
                attend(NG - 1, (NG - 1) % R)
                finish(NG - 1, (NG - 1) % R)


def gnn_stack(nc, a, out):
    s = Shape(a["x"].shape[0])
    T = s.T

    def dram(name, shape):
        return nc.dram_tensor(name, shape, F32).ap()

    with ExitStack() as ctx:
        c = Core(nc, s, ctx)
        runs = dram("runs", (s.NP + 1, D))
        sorted_src, sorted_dst = dram("sorted_src", (s.NP, 4)), dram("sorted_dst", (s.NP, 4))
        z1, z2, x3 = (dram(n, (s.NP, D)) for n in ("z1", "z2", "x3"))
        x2, hop1, hops = dram("x2", (s.NP, WIDE)), dram("hop1", (s.NP, WIDE)), dram("hops", (s.NP + 1, WIDE))
        scores = dram("scores", (s.NP, H))
        spill = dram("spill", (T, D))

        def tiled(rows):
            return rows[0:s.NP, :].rearrange("(p t) d -> p t d", t=T)

        def table(name, dt, shape=None):
            return c.sb(name, shape or [P, T], dt)

        def index_table(name):
            tables.append(table(name, I32, [P, T + G]))
            return tables[-1]

        tables = []
        unsorted = table("unsorted", I32, [P, 1])
        by_src = {"unsorted": unsorted, "end": index_table("src_end"), "other": index_table("src_other"),
                  "weight": table("src_weight", F32), "same": table("src_same", F32),
                  "fix_row": table("src_fix_row", I32, [P, 1]), "fix": table("src_fix", F32, [P, P])}
        by_dst = {"unsorted": unsorted, "end": index_table("dst_end"), "other": index_table("dst_other"),
                  "same": table("dst_same", F32), "degree": table("degree", F32),
                  "root": table("root", F32), "dinv": table("dinv", F32), "dinv2": table("dinv2", F32),
                  "fix_row": table("dst_fix_row", I32, [P, 1]), "fix": table("dst_fix", F32, [P, P])}
        edge_src, edge_dst = index_table("edge_src"), index_table("edge_dst")
        hop_index = index_table("hop_index")
        w = {n: c.sb(f"w_{n}", [P, KC, D], F32) for n in ("gin", "gcn1", "gcn2")}
        w.update({n: c.sb(f"w_{n}", [P, KC, WIDE], F32) for n in ("hop_x", "hop_1", "hop_2", "gat")})
        w["left"], w["head_sums"] = c.sb("w_left", [P, KC, H], F32), c.sb("head_sums", [P, H], F32)
        w["bias_gin"], w["bias_row"] = c.sb("bias_gin", [P, D], BF16), c.sb("bias_row", [P, WIDE], F32)

        constants(nc, c, runs, tables)
        with ExitStack() as held:
            sort = EdgeSort(nc, c, "src", by_src, sorted_src, held)
            sort.split(a["src"], a["dst"], a["edge_weight"], edge_src, edge_dst)
            sort.histogram()
            sort.place()
        sorted_tables(nc, c, "src", sorted_src, by_src)
        with ExitStack() as held:
            sort = EdgeSort(nc, c, "dst", by_dst, sorted_dst, held)
            sort.split(a["dst"], a["src"])
            with ExitStack() as prep:
                edge_phase(nc, c, "gin_e", a["x"], by_src, runs, beside=sort,
                           prepare=prepare_weights(nc, c, a, w, prep))
            sort.place()
        sorted_tables(nc, c, "dst", sorted_dst, by_dst)
        degrees(nc, c, by_dst)
        node_phase(nc, c, "gin_n", "gin", runs, by_src["end"], a["x"], tiled(z1), w["gin"],
                   bias=w["bias_gin"], ragged=1, tables=by_dst)
        edge_phase(nc, c, "gcn1_e", z1, by_dst, runs)
        node_phase(nc, c, "gcn1_n", "gcn1", runs, by_dst["end"], tiled(z1), tiled(z2), w["gcn1"],
                   tables=by_dst)
        edge_phase(nc, c, "gcn2_e", z2, by_dst, runs)
        node_phase(nc, c, "gcn2_n", "gcn2", runs, by_dst["end"], tiled(z2), tiled(x2), w["gcn2"],
                   y_in=tiled(z1), tables=by_dst, next_end=by_src["end"])
        hop_phase(nc, c, "hop1_e", x2, by_src["other"], by_src, w["hop_1"], w["bias_row"], hop1, runs=runs, next_index=hop_index)
        hop_phase(nc, c, "hop2_e", runs, hop_index, by_src, w["hop_2"], w["bias_row"], hops, passed=hop1)
        node_phase(nc, c, "hop_n", "hop", hops, by_src["end"], tiled(x2), tiled(x3), w["hop_x"],
                   head_sums=w["head_sums"], scores=tiled(scores))
        gat_phase(nc, c, x3, tiled(x3), scores, edge_src, edge_dst, w["gat"], out, spill)


INPUTS = {"x": "x", "src": "src", "dst": "dst", "edge_weight": "edge_weight", "W1": "L0_gnn_W1",
          "b1": "L0_gnn_b1", "W2": "L0_gnn_W2", "b2": "L0_gnn_b2", "G1": "L1_gnn_W1", "G2": "L1_gnn_W2",
          "H": "L2_gnn_W", "b": "L2_gnn_b", "A": "L3_gnn_weight", "al": "L3_gnn_attn_l",
          "ar": "L3_gnn_attn_r"}


def kernel(**inputs):
    import concourse.bacc as bacc
    from concourse.bass_utils import run_bass_kernel_spmd

    nc = bacc.Bacc("TRN2", target_bir_lowering=False, num_devices=1)
    arrays, aps = {}, {}
    for short, name in INPUTS.items():
        v = np.ascontiguousarray(inputs[name])
        arrays[f"in_{name}"] = v
        aps[short] = nc.dram_tensor(f"in_{name}", v.shape, mybir.dt.from_np(v.dtype), kind="ExternalInput").ap()
    out = nc.dram_tensor("out_x", inputs["x"].shape, F32, kind="ExternalOutput").ap()
    gnn_stack(nc, aps, out)
    r = run_bass_kernel_spmd(nc, [arrays], core_ids=[0])
    return r.results[0]["out_x"]
```
